# Optimizing a Trainium2 kernel written in Bass

```python
import numpy as np
import jax
import jax.numpy as jnp

def _softmax(x, axis=-1):
    return jax.nn.softmax(x, axis=axis)

def _gelu(x):
    return jax.nn.gelu(x, approximate=True)

def _silu(x):
    return jax.nn.silu(x)

def _sigmoid(x):
    return jax.nn.sigmoid(x)

def _layernorm(x, axis=-1, eps=1e-05):
    m = jnp.mean(x, axis=axis, keepdims=True)
    v = jnp.var(x, axis=axis, keepdims=True)
    return (x - m) / jnp.sqrt(v + eps)

def _scatter_add(tgt, idx, src, axis=0):
    return tgt.at[idx].add(src)

def _segment_sum(src, seg, n):
    return jax.ops.segment_sum(src, seg, n)
kernel_name = 'mk_cond_seq_d4_seqx_r4_891386'

def setup_inputs(seed: int=0):
    np.random.seed(seed)
    _w = jnp.asarray

    def _rec_inputs():
        import jax
        import jax.numpy as jnp
        _rk = jax.random.key(seed)
        x = 7.22e-05 + 1 * jax.random.normal(jax.random.fold_in(_rk, 1), (4, 512, 256), jnp.float32)
        _lenS = 512 - jax.random.randint(jax.random.fold_in(_rk, 7), (4,), 0, max(1, 512 // 4) + 1, jnp.int32)
        _lenS2 = 512 - jax.random.randint(jax.random.fold_in(_rk, 8), (4,), 0, max(1, 512 // 4) + 1, jnp.int32)
        cond_1024 = 0.00782532 + 1.00527 * jax.random.normal(jax.random.fold_in(_rk, 11), (4, 256), jnp.float32)
        return (x, cond_1024)
    x, cond_1024 = _rec_inputs()

    def _L0_cond_setup():
        import jax, jax.numpy as jnp
        import numpy as np
        H = 256
        NH = 16
        DH = H // NH
        MLP = 4 * H
        EPS = 1e-05

        def _ln(x):
            m = jnp.mean(x, axis=-1, keepdims=True)
            v = jnp.mean((x - m) ** 2, axis=-1, keepdims=True)
            return (x - m) * jax.lax.rsqrt(v + EPS)

        def _modulate(x, shift, scale):
            return x * (1.0 + scale[:, None, :]) + shift[:, None, :]
        key = jax.random.key(seed)
        ks = jax.random.split(key, 12)
        s = 1.0 / np.sqrt(H)
        inp = {'x': jax.random.normal(ks[0], (8, 256, H), jnp.float32), 'c': jax.random.normal(ks[1], (8, H), jnp.float32), 'Wc': jax.random.normal(ks[2], (H, 6 * H), jnp.float32) * s, 'bc': jnp.zeros((6 * H,), jnp.float32), 'Wq': jax.random.normal(ks[3], (H, H), jnp.float32) * s, 'bq': jnp.zeros((H,), jnp.float32), 'Wk': jax.random.normal(ks[4], (H, H), jnp.float32) * s, 'bk': jnp.zeros((H,), jnp.float32), 'Wv': jax.random.normal(ks[5], (H, H), jnp.float32) * s, 'bv': jnp.zeros((H,), jnp.float32), 'Wo': jax.random.normal(ks[6], (H, H), jnp.float32) * s, 'bo': jnp.zeros((H,), jnp.float32), 'W1': jax.random.normal(ks[7], (H, MLP), jnp.float32) * s, 'b1': jnp.zeros((MLP,), jnp.float32), 'W2': jax.random.normal(ks[8], (MLP, H), jnp.float32) * (1.0 / np.sqrt(MLP)), 'b2': jnp.zeros((H,), jnp.float32)}
        return inp
    _L0_cond_all = _L0_cond_setup()
    _L0_cond_in = {k: v for k, v in _L0_cond_all.items() if k in ('Wc', 'bc', 'Wq', 'bq', 'Wk', 'bk', 'Wv', 'bv', 'Wo', 'bo', 'W1', 'b1', 'W2', 'b2')}
    del _L0_cond_all

    def _L1_cond_setup():
        import jax, jax.numpy as jnp
        import numpy as np
        B, L, D, P = (8, 512, 256, 64)

        def _ln(x):
            m = x.mean(-1, keepdims=True)
            v = x.var(-1, keepdims=True)
            return (x - m) * jax.lax.rsqrt(v + 1e-05)

        def _s5(u, Lam_re, Lam_im, B_re, B_im, C_re, C_im, D_diag, log_step):
            Lam = Lam_re + 1j * Lam_im
            dt = jnp.exp(log_step)
            Lam_bar = jnp.exp(Lam * dt)
            Bc = B_re + 1j * B_im
            B_bar = ((Lam_bar - 1.0) / Lam)[:, None] * Bc
            Bu = jnp.einsum('bld,pd->blp', u.astype(B_bar.dtype), B_bar)
            A = jnp.broadcast_to(Lam_bar, Bu.shape)

            def binop(e1, e2):
                a1, b1 = e1
                a2, b2 = e2
                return (a1 * a2, a2 * b1 + b2)
            _, xs = jax.lax.associative_scan(binop, (A, Bu), axis=1)
            Cc = C_re + 1j * C_im
            return 2.0 * jnp.einsum('blp,dp->bld', xs, Cc).real + D_diag * u
        key = jax.random.key(seed)
        ks = jax.random.split(key, 16)
        inp = {'y': jax.random.normal(ks[0], (B, L, D), jnp.float32), 't': jax.random.normal(ks[1], (B, D), jnp.float32), 'Wm': jax.random.normal(ks[2], (D, 6 * D), jnp.float32) * 0.02, 'bm': jax.random.normal(ks[3], (6 * D,), jnp.float32) * 0.02, 'Lam_re': -0.5 * jnp.ones((P,), jnp.float32), 'Lam_im': jnp.pi * jnp.arange(P, dtype=jnp.float32), 'B_re': jax.random.normal(ks[4], (P, D), jnp.float32) / np.sqrt(D), 'B_im': jax.random.normal(ks[5], (P, D), jnp.float32) / np.sqrt(D), 'C_re': jax.random.normal(ks[6], (D, P), jnp.float32) / np.sqrt(P), 'C_im': jax.random.normal(ks[7], (D, P), jnp.float32) / np.sqrt(P), 'D_diag': jax.random.normal(ks[8], (D,), jnp.float32), 'log_step': jax.random.uniform(ks[9], (P,), jnp.float32, np.log(0.001), np.log(0.1)), 'Wc': jax.random.normal(ks[10], (D, 2 * D), jnp.float32) * 0.02, 'bc': jax.random.normal(ks[11], (2 * D,), jnp.float32) * 0.02, 'W1': jax.random.normal(ks[12], (D, 4 * D), jnp.float32) / np.sqrt(D), 'b1': jnp.zeros((4 * D,), jnp.float32), 'W2': jax.random.normal(ks[13], (4 * D, D), jnp.float32) / np.sqrt(4 * D) * 0.1, 'b2': jnp.zeros((D,), jnp.float32)}
        return inp
    _L1_cond_all = _L1_cond_setup()
    _L1_cond_in = {k: v for k, v in _L1_cond_all.items() if k in ('Wm', 'bm', 'Lam_re', 'Lam_im', 'B_re', 'B_im', 'C_re', 'C_im', 'D_diag', 'log_step', 'Wc', 'bc', 'W1', 'b1', 'W2', 'b2')}
    del _L1_cond_all

    def _L2_cond_setup():
        import jax, jax.numpy as jnp
        import numpy as np
        DIM = 256
        HEADS = 16
        HEAD_DIM = DIM // HEADS
        MLP = 4 * DIM
        EPS = 1e-05

        def layer_norm(x, g, b):
            mu = jnp.mean(x, axis=-1, keepdims=True)
            var = jnp.var(x, axis=-1, keepdims=True)
            return (x - mu) * jax.lax.rsqrt(var + EPS) * g + b

        def rope_cos_sin(n, d):
            inv_freq = 1.0 / 10000.0 ** (jnp.arange(0, d, 2, dtype=jnp.float32) / d)
            t = jnp.arange(n, dtype=jnp.float32)
            freqs = jnp.outer(t, inv_freq)
            emb = jnp.concatenate([freqs, freqs], -1)
            return (jnp.cos(emb), jnp.sin(emb))

        def rotate_half(x):
            x1, x2 = (x[..., ::2], x[..., 1::2])
            return jnp.concatenate([-x2, x1], axis=-1)
        key = jax.random.key(seed)
        ks = jax.random.split(key, 16)
        B, N = (2, 512)
        s = lambda fan_in: 1.0 / np.sqrt(fan_in)
        inp = {'x': jax.random.normal(ks[0], (B, N, DIM), jnp.float32), 't_emb': jax.random.normal(ks[1], (B, DIM), jnp.float32), 'norm1_g': jnp.ones((DIM,), jnp.float32), 'norm1_b': jnp.zeros((DIM,), jnp.float32), 'Wq': jax.random.normal(ks[2], (DIM, DIM), jnp.float32) * s(DIM), 'Wk': jax.random.normal(ks[3], (DIM, DIM), jnp.float32) * s(DIM), 'Wv': jax.random.normal(ks[4], (DIM, DIM), jnp.float32) * s(DIM), 'Wo': jax.random.normal(ks[5], (DIM, DIM), jnp.float32) * s(DIM), 'norm2_g': jnp.ones((DIM,), jnp.float32), 'norm2_b': jnp.zeros((DIM,), jnp.float32), 'W1': jax.random.normal(ks[6], (DIM, MLP), jnp.float32) * s(DIM), 'W2': jax.random.normal(ks[7], (MLP, DIM), jnp.float32) * s(MLP), 'ada_W': jax.random.normal(ks[8], (DIM, 6 * DIM), jnp.float32) * s(DIM), 'ada_b': jnp.zeros((6 * DIM,), jnp.float32)}
        return inp
    _L2_cond_all = _L2_cond_setup()
    _L2_cond_in = {k: v for k, v in _L2_cond_all.items() if k in ('norm1_g', 'norm1_b', 'Wq', 'Wk', 'Wv', 'Wo', 'norm2_g', 'norm2_b', 'W1', 'W2', 'ada_W', 'ada_b')}
    del _L2_cond_all

    def _L3_cond_setup():
        import jax, jax.numpy as jnp
        import numpy as np
        FEAT = 256
        ADA = 256
        INTER = 256
        RANK = 8
        EPS = 1e-05

        def _layernorm(a, g, b):
            mu = jnp.mean(a, axis=-1, keepdims=True)
            var = jnp.mean(jnp.square(a - mu), axis=-1, keepdims=True)
            return (a - mu) * jax.lax.rsqrt(var + EPS) * g + b
        key = jax.random.key(seed)
        ks = jax.random.split(key, 6)
        B, T = (16, 256)
        x = jax.random.normal(ks[0], (B, T, FEAT), dtype=jnp.float32)
        ada_emb = jax.random.normal(ks[1], (B, ADA), dtype=jnp.float32)
        W1 = jax.random.normal(ks[2], (ADA, INTER), dtype=jnp.float32) / np.sqrt(ADA)
        b1 = jnp.zeros((INTER,), dtype=jnp.float32)
        W2 = jax.random.normal(ks[3], (INTER, FEAT * RANK * 4), dtype=jnp.float32) * (0.1 / np.sqrt(INTER))
        b2 = jnp.zeros((FEAT * RANK * 4,), dtype=jnp.float32)
        ln_g = jnp.ones((ADA,), dtype=jnp.float32)
        ln_b = jnp.zeros((ADA,), dtype=jnp.float32)
        return {'x': x, 'ada_emb': ada_emb, 'ln_g': ln_g, 'ln_b': ln_b, 'W1': W1, 'b1': b1, 'W2': W2, 'b2': b2}
    _L3_cond_all = _L3_cond_setup()
    _L3_cond_in = {k: v for k, v in _L3_cond_all.items() if k in ('ln_g', 'ln_b', 'W1', 'b1', 'W2', 'b2')}
    del _L3_cond_all
    return {'x': x, 'cond_1024': cond_1024, 'L0_cond_Wc': _L0_cond_in['Wc'], 'L0_cond_bc': _L0_cond_in['bc'], 'L0_cond_Wq': _L0_cond_in['Wq'], 'L0_cond_bq': _L0_cond_in['bq'], 'L0_cond_Wk': _L0_cond_in['Wk'], 'L0_cond_bk': _L0_cond_in['bk'], 'L0_cond_Wv': _L0_cond_in['Wv'], 'L0_cond_bv': _L0_cond_in['bv'], 'L0_cond_Wo': _L0_cond_in['Wo'], 'L0_cond_bo': _L0_cond_in['bo'], 'L0_cond_W1': _L0_cond_in['W1'], 'L0_cond_b1': _L0_cond_in['b1'], 'L0_cond_W2': _L0_cond_in['W2'], 'L0_cond_b2': _L0_cond_in['b2'], 'L1_cond_Wm': _L1_cond_in['Wm'], 'L1_cond_bm': _L1_cond_in['bm'], 'L1_cond_Lam_re': _L1_cond_in['Lam_re'], 'L1_cond_Lam_im': _L1_cond_in['Lam_im'], 'L1_cond_B_re': _L1_cond_in['B_re'], 'L1_cond_B_im': _L1_cond_in['B_im'], 'L1_cond_C_re': _L1_cond_in['C_re'], 'L1_cond_C_im': _L1_cond_in['C_im'], 'L1_cond_D_diag': _L1_cond_in['D_diag'], 'L1_cond_log_step': _L1_cond_in['log_step'], 'L1_cond_Wc': _L1_cond_in['Wc'], 'L1_cond_bc': _L1_cond_in['bc'], 'L1_cond_W1': _L1_cond_in['W1'], 'L1_cond_b1': _L1_cond_in['b1'], 'L1_cond_W2': _L1_cond_in['W2'], 'L1_cond_b2': _L1_cond_in['b2'], 'L2_cond_norm1_g': _L2_cond_in['norm1_g'], 'L2_cond_norm1_b': _L2_cond_in['norm1_b'], 'L2_cond_Wq': _L2_cond_in['Wq'], 'L2_cond_Wk': _L2_cond_in['Wk'], 'L2_cond_Wv': _L2_cond_in['Wv'], 'L2_cond_Wo': _L2_cond_in['Wo'], 'L2_cond_norm2_g': _L2_cond_in['norm2_g'], 'L2_cond_norm2_b': _L2_cond_in['norm2_b'], 'L2_cond_W1': _L2_cond_in['W1'], 'L2_cond_W2': _L2_cond_in['W2'], 'L2_cond_ada_W': _L2_cond_in['ada_W'], 'L2_cond_ada_b': _L2_cond_in['ada_b'], 'L3_cond_ln_g': _L3_cond_in['ln_g'], 'L3_cond_ln_b': _L3_cond_in['ln_b'], 'L3_cond_W1': _L3_cond_in['W1'], 'L3_cond_b1': _L3_cond_in['b1'], 'L3_cond_W2': _L3_cond_in['W2'], 'L3_cond_b2': _L3_cond_in['b2']}

def reference(x, cond_1024, L0_cond_Wc, L0_cond_bc, L0_cond_Wq, L0_cond_bq, L0_cond_Wk, L0_cond_bk, L0_cond_Wv, L0_cond_bv, L0_cond_Wo, L0_cond_bo, L0_cond_W1, L0_cond_b1, L0_cond_W2, L0_cond_b2, L1_cond_Wm, L1_cond_bm, L1_cond_Lam_re, L1_cond_Lam_im, L1_cond_B_re, L1_cond_B_im, L1_cond_C_re, L1_cond_C_im, L1_cond_D_diag, L1_cond_log_step, L1_cond_Wc, L1_cond_bc, L1_cond_W1, L1_cond_b1, L1_cond_W2, L1_cond_b2, L2_cond_norm1_g, L2_cond_norm1_b, L2_cond_Wq, L2_cond_Wk, L2_cond_Wv, L2_cond_Wo, L2_cond_norm2_g, L2_cond_norm2_b, L2_cond_W1, L2_cond_W2, L2_cond_ada_W, L2_cond_ada_b, L3_cond_ln_g, L3_cond_ln_b, L3_cond_W1, L3_cond_b1, L3_cond_W2, L3_cond_b2):
    import jax
    import jax.numpy as jnp

    def _L0_cond_ref(x, c, Wc, bc, Wq, bq, Wk, bk, Wv, bv, Wo, bo, W1, b1, W2, b2):
        import jax, jax.numpy as jnp
        import numpy as np
        H = 256
        NH = 16
        DH = H // NH
        MLP = 4 * H
        EPS = 1e-05

        def _ln(x):
            m = jnp.mean(x, axis=-1, keepdims=True)
            v = jnp.mean((x - m) ** 2, axis=-1, keepdims=True)
            return (x - m) * jax.lax.rsqrt(v + EPS)

        def _modulate(x, shift, scale):
            return x * (1.0 + scale[:, None, :]) + shift[:, None, :]
        B, S, _ = x.shape
        c6 = jax.nn.silu(c) @ Wc + bc
        sh_msa, sc_msa, g_msa, sh_mlp, sc_mlp, g_mlp = jnp.split(c6, 6, axis=-1)
        xm = _modulate(_ln(x), sh_msa, sc_msa)
        q = (xm @ Wq + bq).reshape(B, S, NH, DH)
        k = (xm @ Wk + bk).reshape(B, S, NH, DH)
        v = (xm @ Wv + bv).reshape(B, S, NH, DH)
        q = q / DH
        w = jnp.einsum('bqhc,bkhc->bhqk', q, k)
        w = jax.nn.softmax(w, axis=-1)
        y = jnp.einsum('bhqk,bkhc->bqhc', w, v).reshape(B, S, H)
        x = x + g_msa[:, None, :] * (y @ Wo + bo)
        xm2 = _modulate(_ln(x), sh_mlp, sc_mlp)
        h = jax.nn.gelu(xm2 @ W1 + b1, approximate=False)
        x = x + g_mlp[:, None, :] * (h @ W2 + b2)
        return x

    def _L1_cond_ref(y, t, Wm, bm, Lam_re, Lam_im, B_re, B_im, C_re, C_im, D_diag, log_step, Wc, bc, W1, b1, W2, b2):
        import jax, jax.numpy as jnp
        import numpy as np
        B, L, D, P = (8, 512, 256, 64)

        def _ln(x):
            m = x.mean(-1, keepdims=True)
            v = x.var(-1, keepdims=True)
            return (x - m) * jax.lax.rsqrt(v + 1e-05)

        def _s5(u, Lam_re, Lam_im, B_re, B_im, C_re, C_im, D_diag, log_step):
            Lam = Lam_re + 1j * Lam_im
            dt = jnp.exp(log_step)
            Lam_bar = jnp.exp(Lam * dt)
            Bc = B_re + 1j * B_im
            B_bar = ((Lam_bar - 1.0) / Lam)[:, None] * Bc
            Bu = jnp.einsum('bld,pd->blp', u.astype(B_bar.dtype), B_bar)
            A = jnp.broadcast_to(Lam_bar, Bu.shape)

            def binop(e1, e2):
                a1, b1 = e1
                a2, b2 = e2
                return (a1 * a2, a2 * b1 + b2)
            _, xs = jax.lax.associative_scan(binop, (A, Bu), axis=1)
            Cc = C_re + 1j * C_im
            return 2.0 * jnp.einsum('blp,dp->bld', xs, Cc).real + D_diag * u
        mod = t @ Wm + bm
        shift_a, scale_a, gate_a, shift_ff, scale_ff, gate_ff = jnp.split(mod, 6, axis=-1)
        y_mod = _ln(y) * (1 + scale_a[:, None]) + shift_a[:, None]
        a_y = _s5(y_mod, Lam_re, Lam_im, B_re, B_im, C_re, C_im, D_diag, log_step)
        y = y + gate_a[:, None] * a_y
        cond = t @ Wc + bc
        scale_c, shift_c = jnp.split(cond, 2, axis=-1)
        y_norm = _ln(y) * (1 + scale_c[:, None]) + shift_c[:, None]
        y_mod = y_norm * (1 + scale_ff[:, None]) + shift_ff[:, None]
        h = jax.nn.gelu(y_mod @ W1 + b1)
        ff_y = h @ W2 + b2
        return y + gate_ff[:, None] * ff_y

    def _L2_cond_ref(x, t_emb, norm1_g, norm1_b, Wq, Wk, Wv, Wo, norm2_g, norm2_b, W1, W2, ada_W, ada_b):
        import jax, jax.numpy as jnp
        import numpy as np
        DIM = 256
        HEADS = 16
        HEAD_DIM = DIM // HEADS
        MLP = 4 * DIM
        EPS = 1e-05

        def layer_norm(x, g, b):
            mu = jnp.mean(x, axis=-1, keepdims=True)
            var = jnp.var(x, axis=-1, keepdims=True)
            return (x - mu) * jax.lax.rsqrt(var + EPS) * g + b

        def rope_cos_sin(n, d):
            inv_freq = 1.0 / 10000.0 ** (jnp.arange(0, d, 2, dtype=jnp.float32) / d)
            t = jnp.arange(n, dtype=jnp.float32)
            freqs = jnp.outer(t, inv_freq)
            emb = jnp.concatenate([freqs, freqs], -1)
            return (jnp.cos(emb), jnp.sin(emb))

        def rotate_half(x):
            x1, x2 = (x[..., ::2], x[..., 1::2])
            return jnp.concatenate([-x2, x1], axis=-1)
        B, N, C = x.shape
        H, D = (HEADS, HEAD_DIM)
        scale = D ** (-0.5)
        mod = jax.nn.silu(t_emb) @ ada_W + ada_b
        shift_msa, scale_msa, gate_msa, shift_mlp, scale_mlp, gate_mlp = jnp.split(mod, 6, axis=-1)
        xn = layer_norm(x, norm1_g, norm1_b) * (1 + scale_msa[:, None, :]) + shift_msa[:, None, :]
        q = (xn @ Wq).reshape(B, N, H, D).transpose(0, 2, 1, 3)
        k = (xn @ Wk).reshape(B, N, H, D).transpose(0, 2, 1, 3)
        v = (xn @ Wv).reshape(B, N, H, D).transpose(0, 2, 1, 3)
        cos, sin = rope_cos_sin(N, D)
        q = q * cos + rotate_half(q) * sin
        k = k * cos + rotate_half(k) * sin
        attn = jnp.einsum('bhnd,bhmd->bhnm', q, k) * scale
        attn = jax.nn.softmax(attn, axis=-1)
        out = jnp.einsum('bhnm,bhmd->bhnd', attn, v)
        out = out.transpose(0, 2, 1, 3).reshape(B, N, C) @ Wo
        x = x + gate_msa[:, None, :] * out
        xn = layer_norm(x, norm2_g, norm2_b) * (1 + scale_mlp[:, None, :]) + shift_mlp[:, None, :]
        mlp = jax.nn.gelu(xn @ W1, approximate=False) @ W2
        x = x + gate_mlp[:, None, :] * mlp
        return x

    def _L3_cond_ref(x, ada_emb, ln_g, ln_b, W1, b1, W2, b2):
        import jax, jax.numpy as jnp
        import numpy as np
        FEAT = 256
        ADA = 256
        INTER = 256
        RANK = 8
        EPS = 1e-05

        def _layernorm(a, g, b):
            mu = jnp.mean(a, axis=-1, keepdims=True)
            var = jnp.mean(jnp.square(a - mu), axis=-1, keepdims=True)
            return (a - mu) * jax.lax.rsqrt(var + EPS) * g + b
        B, T, D = x.shape
        h = jax.nn.gelu(_layernorm(ada_emb, ln_g, ln_b) @ W1 + b1, approximate=False)
        w = h @ W2 + b2
        a1, bb1, a2, bb2 = jnp.split(w, 4, axis=-1)
        a1 = a1.reshape(B, D, RANK)
        bb1 = bb1.reshape(B, D, RANK)
        a2 = a2.reshape(B, D, RANK)
        bb2 = bb2.reshape(B, D, RANK)
        y = jnp.einsum('btd,bdr->btr', x, a1)
        y = jnp.einsum('btr,bdr->btd', y, bb1)
        y = jax.nn.gelu(y, approximate=False)
        y = jnp.einsum('btd,bdr->btr', y, a2)
        y = jnp.einsum('btr,bdr->btd', y, bb2)
        return y + x
    x = _L0_cond_ref(x, cond_1024, L0_cond_Wc, L0_cond_bc, L0_cond_Wq, L0_cond_bq, L0_cond_Wk, L0_cond_bk, L0_cond_Wv, L0_cond_bv, L0_cond_Wo, L0_cond_bo, L0_cond_W1, L0_cond_b1, L0_cond_W2, L0_cond_b2)
    x = _L1_cond_ref(x, cond_1024, L1_cond_Wm, L1_cond_bm, L1_cond_Lam_re, L1_cond_Lam_im, L1_cond_B_re, L1_cond_B_im, L1_cond_C_re, L1_cond_C_im, L1_cond_D_diag, L1_cond_log_step, L1_cond_Wc, L1_cond_bc, L1_cond_W1, L1_cond_b1, L1_cond_W2, L1_cond_b2)
    x = _L2_cond_ref(x, cond_1024, L2_cond_norm1_g, L2_cond_norm1_b, L2_cond_Wq, L2_cond_Wk, L2_cond_Wv, L2_cond_Wo, L2_cond_norm2_g, L2_cond_norm2_b, L2_cond_W1, L2_cond_W2, L2_cond_ada_W, L2_cond_ada_b)
    x = _L3_cond_ref(x, cond_1024, L3_cond_ln_g, L3_cond_ln_b, L3_cond_W1, L3_cond_b1, L3_cond_W2, L3_cond_b2)
    return x

_drawn_inputs = setup_inputs


def setup_inputs(seed=0):
    import zlib

    import numpy as np

    out = dict(_drawn_inputs(seed))
    spreads = {'L0_cond_bc': (0.0, 0.1),
     'L0_cond_bq': (0.0, 2.0),
     'L0_cond_bk': (0.0, 2.0),
     'L0_cond_bv': (0.0, 0.1),
     'L0_cond_bo': (0.0, 0.1),
     'L0_cond_b1': (0.0, 0.1),
     'L0_cond_b2': (0.0, 0.1),
     'L1_cond_Lam_re': (-0.5, 0.6),
     'L1_cond_b1': (0.0, 0.8),
     'L1_cond_b2': (0.0, 0.277),
     'L2_cond_norm1_g': (1.0, 0.2),
     'L2_cond_norm1_b': (0.0, 0.1),
     'L2_cond_norm2_g': (1.0, 0.2),
     'L2_cond_norm2_b': (0.0, 0.277),
     'L2_cond_ada_b': (0.0, 0.1),
     'L3_cond_ln_g': (1.0, 0.2),
     'L3_cond_ln_b': (0.0, 0.272),
     'L3_cond_b1': (0.0, 0.1),
     'L3_cond_b2': (0.0, 0.1)}
    factors = {'L1_cond_bm': 3.087,
     'L1_cond_Wc': 6.947,
     'L1_cond_bc': 8.0,
     'L1_cond_W1': 3.308,
     'L1_cond_W2': 2.909}
    for name, (base, spread) in spreads.items():
        noise = np.random.default_rng([zlib.crc32(name.encode()), seed]).standard_normal(out[name].shape)
        drawn = base * np.exp(spread * noise) if base else spread * noise
        out[name] = jnp.asarray(drawn.astype(out[name].dtype))
    for name, factor in factors.items():
        out[name] = (out[name] * factor).astype(out[name].dtype)
    return out
```

```python
from contextlib import ExitStack

import concourse.bass as bass
from concourse import mybir

F32 = mybir.dt.float32
BF16 = mybir.dt.bfloat16
I32 = mybir.dt.int32
ACT = mybir.ActivationFunctionType
ALU = mybir.AluOpType
AX = mybir.AxisListType

P = 128
B, T, D = 4, 512, 256
TT = T // P
DH = D // P
NH, HD = 16, 16
F = 1024
FM = F // P
SSM = 64
RANK = 8
EPS = 1e-5
LOG2E = 1.4426950408889634
LN2_HI, LN2_LO = 0.693145751953125, 1.4286068203094172e-06
TWO_PI_A, TWO_PI_B, TWO_PI_C = 6.28125, 0.0019350051879882812, 3.019916050561733e-07
ROUND = 12582912.0

ROWS = {}
for _name, _n in (("cond", 8), ("L0_bq", 2), ("L0_bk", 2), ("L0_b1", 8), ("L1_b1", 8), ("n1g", 2), ("n1b", 2),
                  ("n2g", 2), ("n2b", 2), ("lng", 2), ("lnb", 2), ("L3_b1", 2), ("Dd", 2)):
    ROWS[_name] = (sum(n for _, n in ROWS.values()), _n)
NROWS = sum(n for _, n in ROWS.values())

SHIFT, SCALE, GATE, SHIFT2, SCALE2, GATE2 = range(6)

NG = 16
NSTEP = NG * 16
LOOK = 28
FILLS = 12 * 16
MISC_KINDS = ("V", "T", "Q", "K", "RQ", "RK", "M", "PJ")


def attention_schedule(rope):
    s = {}

    def put(n, *task):
        s.setdefault(n, []).append(task)

    for b in range(B):
        o = 64 * (b - 1)
        first = b == 0
        put(-50 if first else o - 20, "LNS", b, 0)
        put(-49 if first else o - 10, "LNN", b, 0)
        put(-48 if first else o + 4, "T", b, 0)
        put(-47 if first else o + 6, "T", b, 1)
        for half in range(2):
            at = (-46 + 8 * half) if first else o + 8 + 12 * half
            put(at, "Q", b, half)
            put(at + 2, "K", b, half)
            if rope:
                put(at + 1 if first else at + 4, "RQ", b, half)
                put(at + 3 if first else at + 6, "RK", b, half)
            put(at + 4 if first else at + 10, "SPLIT", b, half)
            put(at + 5 if first else at + 14, "SAVE", b, half)
        for g in range(4):
            put((-40 + 8 * (g // 2)) if first else o + (26, 35, 50, 66)[g], "FILL", b, g)
        put(64 * b + 2, "V", b, 0)
        put(64 * b + 3, "V", b, 1)
        put(64 * b + 80, "PJ", b, 0)
        put(64 * b + 82, "PJ", b, 1)
    for G in range(NG):
        put(16 * G - 10, "M", G, 0)
        put(16 * G - 9, "MROW", G, 0)
        put(16 * G + 18, "O", G, 0)
        put(16 * G + 19, "OSAVE", G, 0)
        put(16 * G + 23, "OLOAD", G, 0)
        if G % 2:
            put(16 * G + 27, "NORM", G // 2, 0)
    return s


def build(nc, A, out):
    misc = {}
    scheds = [attention_schedule(False), attention_schedule(True)]
    for a, sched in enumerate(scheds):
        for n in sorted(sched):
            for task in sched[n]:
                if task[0] in MISC_KINDS:
                    misc[(a,) + task] = sum(1 for k in misc if k[0] == a)

    with ExitStack() as ctx:
        def sb(name, shape, dt=F32):
            return ctx.enter_context(nc.sbuf_tensor(name, shape, dt))

        def sem(name):
            return ctx.enter_context(nc.semaphore(name))

        def scratch(name, shape, dt=F32):
            return nc.dram_tensor(name, shape, dt, kind="Internal").ap()

        PS = ctx.enter_context(nc.psum_tensor("PS", [P, 8, 512], F32))

        x = sb("x", [P, B * TT, D])
        WA = sb("WA", [P, 4, DH, D])
        W1 = sb("W1", [P, DH, F])
        W2 = sb("W2", [P, FM, D])
        gates = sb("gates", [P, 2, 2, B, D])
        gate_bias = sb("gate_bias", [P, D])
        bias_bc = sb("bias_bc", [P, 4, D])
        ident = sb("ident", [P, P])
        rot = sb("rot", [P, P])
        rope = sb("rope", [P, 2, T])
        rows = sb("rows", [NROWS, P])
        col = sb("col", [P, NROWS])
        bq16 = sb("bq16", [P, 2])
        cs = sb("cs", [P, 2, 32])
        cc = sb("cc", [P, 2, 32])
        csig = sb("csig", [P, 8])
        mrow_f = sb("mrow_f", [96, 512])
        mbias = sb("mbias", [96, 512])
        mcol = sb("mcol", [P, 2, 4, 96])
        mod = sb("mod", [P, 6, 2, 2, B])
        st6 = sb("st6", [P, TT, 6])
        mv = sb("mv", [P, TT, 2])
        ve = sb("ve", [P, TT])
        rs = sb("rs", [P, 3, TT])
        mhalf = sb("mhalf", [P, TT])
        xnorm = sb("xnorm", [P, TT, D])
        XN = sb("XN", [P, DH, T])
        tsc = sb("tsc", [P, 4, D])
        PH = sb("PH", [P, 2, 4, T])
        H = PH[:, :, :, :].rearrange("p a b t -> p (a b) t")
        UW = 21504
        U = sb("U", [P, UW])

        at = [0]

        def take(words, dt=F32):
            ap = U[:, at[0]:at[0] + words]
            at[0] += words
            assert at[0] <= UW, at[0]
            return ap if dt == F32 else ap.bitcast(dt)

        QP = [take(1024, BF16).rearrange("p (j t) -> p j t", j=4) for _ in range(4)]
        KP = [take(1024, BF16).rearrange("p (j t) -> p j t", j=4) for _ in range(4)]
        Vt = take(TT * NH * 32).rearrange("p (k h c) -> p k h c", k=TT, h=NH)
        parts = [take(768, BF16).rearrange("p (c t) -> p c t", c=3) for _ in range(4)]
        q32 = [take(T) for _ in range(4)]
        resid = take(T)
        Osb = [take(T) for _ in range(2)]
        Onum = [take(T) for _ in range(2)]
        Oden = [take(T) for _ in range(2)]
        yT = take(2 * T).rearrange("p (h t) -> p h t", h=2)
        mx = take(32).rearrange("p (a c) -> p a c", a=2)
        mneg = [take(128, BF16).rearrange("p (i c) -> p i c", i=2) for _ in range(2)]
        rt = [take(T) for _ in range(2)]

        at[0] = 0
        ring = [take(2048).rearrange("p (k n) -> p k n", k=2) for _ in range(4)]
        Wm1 = take(3072).rearrange("p (k n) -> p k n", k=2)
        Wm2 = take(3072).rearrange("p (k n) -> p k n", k=2)
        Wc1 = take(1024).rearrange("p (k n) -> p k n", k=2)
        WL3 = take(512).rearrange("p (k n) -> p k n", k=2)
        CC, SS, RR = take(T), take(T), take(T)
        BT = take(512).rearrange("p (a k n) -> p a k n", a=2, k=2)
        CT = take(512).rearrange("p (a n) -> p a n", a=2)
        diagD = take(256).rearrange("p (k n) -> p k n", k=2)
        s5B = take(512).rearrange("p (a n) -> p a n", a=2)
        s5C = take(512).rearrange("p (a k n) -> p a k n", a=2, k=2)
        s5W = take(512).rearrange("p (a n) -> p a n", a=2)
        s5t = take(T)
        Wm0 = PH[:, :, :, :].rearrange("p a b t -> p (a b t)")[:, 0:3072].rearrange("p (k n) -> p k n", k=2)
        at[0] = 0
        bu = [take(T) for _ in range(2)]
        ysc = [[take(T) for _ in range(2)] for _ in range(2)]
        yst = [take(T) for _ in range(2)]
        XS = [take(2 * T).rearrange("p (h t) -> p h t", h=2) for _ in range(2)]
        at[0] = 0
        xT = [take(2 * T).rearrange("p (h t) -> p h t", h=2) for _ in range(B)]
        gT = [take(2 * T).rearrange("p (h t) -> p h t", h=2) for _ in range(B)]
        z1 = [take(T) for _ in range(B)]
        z2 = [take(T) for _ in range(B)]
        btr = take(2 * B * D).rearrange("p (a b d) -> p a b d", a=2, b=B)

        sv = sb("sv", [P, 64])
        lam = sb("lam", [P, 4])
        lam_i = sb("lam_i", [P, 1], I32)
        c4 = sb("c4", [B, D])
        c4s = sb("c4s", [B, 8])
        lnc = sb("lnc", [P, 2, 32])
        h3 = sb("h3", [P, 2, 32])
        wrow = tsc
        b2row = xnorm

        raw_a1 = sb("raw_a1", [P, 4, B, 2, RANK])

        d_gate = scratch("d_gate", (3, 2, B, D))
        d_parts = scratch("d_parts", (2, 16, P, 3, T), BF16)
        d_o = scratch("d_o", (2, NG, P, T))
        d_low = scratch("d_low", (4, B, 2 * D * RANK // 2))

        ld_rows, ld_const, ld_rope, ld_s5 = sem("ld_rows"), sem("ld_const"), sem("ld_rope"), sem("ld_s5")
        ld_x = [sem(f"ld_x{b}") for b in range(B)]
        ld_wm0, ld_mb = sem("ld_wm0"), sem("ld_mb")
        ld_wa, ld_bias = sem("ld_wa"), sem("ld_bias")
        ld_mlp = [sem(f"ld_mlp{i}") for i in range(3)]
        ld_mid = sem("ld_mid")
        ld_ring = [sem("ld_ring0"), sem("ld_ring1")]
        ld_b2 = [sem("ld_b2_0"), sem("ld_b2_1")]
        ld_low = sem("ld_low")
        ld_gate = [sem(f"ld_gate{i}") for i in range(3)]
        gate_saved = sem("gate_saved")
        low_saved = sem("low_saved")
        out_done = sem("out_done")
        dve_c, act_c, pool_c, pe_c = sem("dve_c"), sem("act_c"), sem("pool_c"), sem("pe_c")
        cols_ready, silu_e, silu_ready = sem("cols_ready"), sem("silu_e"), sem("silu_ready")
        mod_ps, mod_row, mod_tr, mod_ready = sem("mod_ps"), sem("mod_row"), sem("mod_tr"), sem("mod_ready")
        row_tr = sem("row_tr")
        s5_tr, s5_ready, s5_pre = sem("s5_tr"), sem("s5_ready"), sem("s5_pre")
        l3_tr, l3_h, l3_hg, l3_w, l3_wr, l3_bt, l3_ready = (sem(n) for n in (
            "l3_tr", "l3_h", "l3_hg", "l3_w", "l3_wr", "l3_bt", "l3_ready"))
        consts_set = sem("consts_set")
        ln_stats, ln_rstd, ln_done = sem("ln_stats"), sem("ln_rstd"), sem("ln_done")

        class Chain:

            def __init__(self, eng, s):
                self.eng, self.s, self.n = eng, s, 0

            def __call__(self, ins):
                self.n += 1
                ins.then_inc(self.s, 1)
                self.eng.wait_ge(self.s, self.n)

        def column(name, i):
            return col[:, ROWS[name][0] + i:ROWS[name][0] + i + 1]

        def batch(b):
            return x[:, TT * b:TT * (b + 1), :]

        def bank(i, n=512):
            return PS[:, i, 0:n]

        def norm_stats(v, link, k, b, waits):
            for s, n in waits:
                v.wait_ge(s, n)
            for t in range(TT):
                ins = v.bn_stats(st6[:, t, :], x[:, TT * b + t, :])
            link(ins)
            for t in range(TT):
                ins = v.bn_aggr(mv[:, t, :], st6[:, t, :])
            link(ins)
            v.tensor_scalar(ve[:, :], mv[:, :, 1], EPS, None, ALU.add).then_inc(ln_stats, 1)

        def norm_rstd(pool, link, k):
            pool.wait_ge(ln_stats, k + 1)
            link(pool.tensor_tensor(rs[:, 0, :], ve[:, :], mhalf[:, :], ALU.pow))
            link(pool.tensor_tensor(rs[:, 1, :], rs[:, 0, :], rs[:, 0, :], ALU.mult))
            link(pool.tensor_tensor(rs[:, 1, :], rs[:, 1, :], ve[:, :], ALU.mult))
            link(pool.tensor_scalar(rs[:, 1, :], rs[:, 1, :], -0.5, 1.5, ALU.mult, ALU.add))
            pool.tensor_tensor(rs[:, 2, :], rs[:, 0, :], rs[:, 1, :], ALU.mult).then_inc(ln_rstd, 1)

        def norm_apply(v, k, b, waits):
            v.wait_ge(ln_rstd, k + 1)
            for s, n in waits:
                v.wait_ge(s, n)
            for t in range(TT):
                ins = v.tensor_scalar(xnorm[:, t, :], x[:, TT * b + t, :], mv[:, t, 0:1], rs[:, 2, t:t + 1],
                                      ALU.subtract, ALU.mult)
            ins.then_inc(ln_done, 1)

        def turn(pe, dst, half, src=None):
            for t in range(TT):
                s_ = xnorm[:, t, half * P:(half + 1) * P] if src is None else src(t)
                ins = pe.transpose(dst[:, t * P:(t + 1) * P], s_, ident[:, :])
            return ins

        def section(i, s_, half):
            return mcol[:, i % 2, 2 * (s_ % 2) + half, 32 * (s_ // 2):32 * (s_ // 2) + B]


        def mod_rows(pe, i, W, C, nchunk, waits):
            for s, n in waits:
                pe.wait_ge(s, n)
            for k in range(DH):
                for c in range(nchunk):
                    ins = pe.matmul(PS[32 * c:32 * c + 32, 0, :], C[:, k, :], W[:, k, 512 * c:512 * (c + 1)],
                                    start=(k == 0), stop=(k == 1))
            ins.then_inc(mod_ps, 1)
            pe.wait_ge(mod_row, i + 1)
            for f in range(4):
                ins = pe.transpose(PS[:, 1, f * 96:f * 96 + 32 * nchunk], mrow_f[0:32 * nchunk, f * P:(f + 1) * P],
                                   ident[0:32 * nchunk, 0:32 * nchunk])
            ins.then_inc(mod_tr, 1)

        MOD_L = (0, 1, None, 2)
        MBIAS = (3, 6, 7, 10)

        def mod_evac(v, i, nchunk, save_waits):
            v.wait_ge(mod_ps, i + 1)
            v.wait_ge(ld_mb, 16 * MBIAS[i])
            for s, n in save_waits:
                v.wait_ge(s, n)
            v.tensor_tensor(mrow_f[0:32 * nchunk, :], PS[0:32 * nchunk, 0, :], mbias[0:32 * nchunk, :],
                            ALU.add).then_inc(mod_row, 1)
            v.wait_ge(mod_tr, i + 1)
            for f in range(4):
                ins = v.tensor_copy(mcol[:, i % 2, f, 0:32 * nchunk], PS[:, 1, f * 96:f * 96 + 32 * nchunk])
            ins.then_inc(mod_ready, 1)

        def load_mbias(sp, src, nchunk):
            for c in range(nchunk):
                sp.dma_start(mbias[32 * c:32 * c + 32, :],
                             src[512 * c:512 * (c + 1)].partition_broadcast(32)).then_inc(ld_mb, 16)

        def save_gates(sp, i):
            l = MOD_L[i]
            sp.wait_ge(mod_row, i + 1)
            sp.dma_start(d_gate[l, 0], mrow_f[32:32 + B, 0:D]).then_inc(gate_saved, 16)
            sp.dma_start(d_gate[l, 1], mrow_f[64:64 + B, D:2 * D]).then_inc(gate_saved, 16)

        def load_gates(sp, l):
            sp.wait_ge(gate_saved, 32 * (l + 1))
            src = d_gate[l].rearrange("a b d -> (a b d)")
            sp.dma_start(gates[:, l % 2].rearrange("p a b d -> p (a b d)"),
                         src.partition_broadcast(P)).then_inc(ld_gate[l], 16)

        def view(w):
            return w.rearrange("(k p) n -> p k n", p=P)

        class Attention:

            def __init__(self, a, before):
                self.a, self.before, self.sched = a, before, scheds[a]
                n = f"a{a}_"
                self.st_full, self.st_read = sem(n + "st_full"), sem(n + "st_read")
                self.sm_full, self.sm_free = sem(n + "sm_full"), sem(n + "sm_free")
                self.pv_done, self.o_free = sem(n + "pv_done"), sem(n + "o_free")
                self.m_full, self.m_free = sem(n + "misc_full"), sem(n + "misc_free")
                self.split = sem(n + "split")
                self.saved = [sem(n + f"saved{i}") for i in range(2)]
                self.filled = [sem(n + f"filled{g}") for g in range(4)]
                self.mset = [sem(n + f"mset{g}") for g in range(4)]
                self.osaved = [sem(n + f"osaved{i}") for i in range(2)]
                self.oloaded = [sem(n + f"oloaded{i}") for i in range(2)]
                self.rec, self.y = sem(n + "rec"), sem(n + "y")
                self.pj, self.xd, self.ropet = sem(n + "pj"), sem(n + "x_done"), sem(n + "ropet")
                self.init = sem(n + "init")
                self.norm0 = 0 if a == 0 else 16

            def idx(self, *task):
                return misc[(self.a,) + task]

            def steps(self):
                return range(min(self.sched), max(max(self.sched), NSTEP + 1) + 1)

            def pe(self, pe):
                for s, n in self.before:
                    pe.wait_ge(s, n)
                pe.wait_ge(ld_wa, 64 * (self.a + 1))
                if self.a:
                    pe.wait_ge(ld_rope, 48)
                pe.wait_ge(self.init, 1)

                def misc_done(ins):
                    ins.then_inc(self.m_full, 1)

                def task(kind, b, i):
                    if kind not in MISC_KINDS:
                        return
                    k = self.idx(kind, b, i)
                    if k:
                        pe.wait_ge(self.m_free, k)
                    if kind == "T":
                        pe.wait_ge(ln_done, self.norm0 + b + 1)
                        misc_done(turn(pe, bank(7), i))
                    elif kind in ("Q", "K"):
                        pe.wait_ge(self.m_free, self.idx("T", b, 1) + 1)
                        w = WA[:, "QK".index(kind)]
                        for k_ in range(DH):
                            ins = pe.matmul(bank(7), w[:, k_, i * P:(i + 1) * P], XN[:, k_, :],
                                            start=(k_ == 0), stop=(k_ == 1))
                        misc_done(ins)
                    elif kind in ("RQ", "RK"):
                        pe.wait_ge(self.m_free, self.idx(kind[1], b, i) + 1)
                        misc_done(pe.matmul(bank(7), rot[:, :], q32[2 * i + (kind == "RK")], start=True, stop=True))
                    elif kind == "V":
                        for t in range(2):
                            for k_ in range(DH):
                                ins = pe.matmul(PS[:, 7, 256 * t:256 * (t + 1)],
                                                XN[:, k_, (2 * i + t) * P:(2 * i + t + 1) * P], WA[:, 2, k_, :],
                                                start=(k_ == 0), stop=(k_ == 1))
                        misc_done(ins)
                    elif kind == "M":
                        pe.wait_ge(self.sm_free, 8 * (b + 1))
                        misc_done(pe.transpose(PS[0:16, 7, 0:P], mx[:, b % 2, :], ident[:, :]))
                    elif kind == "PJ":
                        pe.wait_ge(self.y, 2 * b + 2)
                        for t in range(2):
                            for k_ in range(DH):
                                ins = pe.matmul(PS[:, 7, 256 * t:256 * (t + 1)],
                                                yT[:, k_, (2 * i + t) * P:(2 * i + t + 1) * P], WA[:, 3, k_, :],
                                                start=(k_ == 0), stop=(k_ == 1))
                        misc_done(ins)

                for n in self.steps():
                    for kind, b, i in self.sched.get(n, []):
                        task(kind, b, i)
                    if 0 <= n < NSTEP:
                        b, g, kt, j = n // 64, n // 16 % 4, n // 4 % 4, n % 4
                        if n % 16 == 0:
                            pe.wait_ge(self.mset[g], 32 * (b + 1))
                        if n >= 2:
                            pe.wait_ge(self.st_read, n - 1)
                        pe.matmul(bank(n % 2), KP[g][0:98, j, kt * P:(kt + 1) * P], QP[g][0:98, j, :],
                                  start=True, stop=True).then_inc(self.st_full, 1)
                    w = n + LOOK
                    if 0 <= w < NSTEP:
                        b, g, j, qt = w // 64, w // 16 % 4, w // 4 % 4, w % 4
                        if w % 16 == 0:
                            pe.wait_ge(self.filled[g], FILLS * (b + 1))
                        if w % 2 == 0 and w >= 4:
                            pe.wait_ge(self.sm_free, w // 2 - 1)
                        ins = pe.matmul(bank(2 + w % 4), QP[g][0:96, j, qt * P:(qt + 1) * P], KP[g][0:96, j, :],
                                        start=True, stop=True)
                        if w % 2:
                            ins.then_inc(self.sm_full, 1)
                    if n % 4 == 1 and 0 <= (n - 5) // 4 < NG * 4:
                        m = (n - 5) // 4
                        b, g, kt = m // 16, m // 4 % 4, m % 4
                        pe.wait_ge(self.st_read, 4 * m + 4)
                        if kt == 0:
                            pe.wait_ge(self.m_free, self.idx("V", b, 1) + 1)
                            if m:
                                pe.wait_ge(self.o_free, m // 4)
                        for j in range(4):
                            ins = pe.matmul(PS[32 * j:32 * j + 32, 6, :], Vt[:, kt, 4 * g + j, :], PH[:, m % 2, j, :],
                                            start=(kt == 0), stop=(kt == 3))
                        ins.then_inc(self.pv_done, 1)

            def act(self, act):
                def task(kind, b, i):
                    if kind == "T":
                        act.wait_ge(self.m_full, self.idx(kind, b, i) + 1)
                        if b:
                            act.wait_ge(self.m_full, self.idx("V", b - 1, 1) + 1)
                        m = 0 if self.a == 0 else 4
                        nc.scalar.activation(XN[:, i, :], bank(7), ACT.Identity, bias=mod[:, m, 0, i, b:b + 1],
                                             scale=mod[:, m, 1, i, b:b + 1]).then_inc(self.m_free, 1)
                    elif kind in ("Q", "K"):
                        act.wait_ge(self.m_full, self.idx(kind, b, i) + 1)
                        if b:
                            act.wait_ge(self.split, 2 * b + i - 1)
                        o = q32[2 * i + (kind == "K")]
                        if self.a == 0:
                            bias = bq16[:, i:i + 1] if kind == "Q" else column("L0_bk", i)
                            ins = nc.scalar.activation(o, bank(7), ACT.Identity, bias=bias,
                                                       scale=1.0 / HD if kind == "Q" else 1.0)
                        else:
                            ins = nc.scalar.activation(o, bank(7), ACT.Copy, scale=HD ** -0.5 if kind == "Q" else 1.0)
                        ins.then_inc(self.m_free, 1)
                    elif kind == "V" and self.a == 1:
                        act.wait_ge(self.m_full, self.idx(kind, b, i) + 1)
                        if b:
                            act.wait_ge(self.pv_done, 16 * b)
                        nc.scalar.activation(Vt[:, 2 * i:2 * i + 2, :, 0:HD],
                                             bank(7).rearrange("p (t h c) -> p t h c", t=2, h=NH),
                                             ACT.Copy).then_inc(self.m_free, 1)
                    elif kind == "O":
                        act.wait_ge(self.pv_done, 4 * b + 4)
                        if b >= 2:
                            act.wait_ge(self.osaved[b % 2], 16 * (b // 2))
                        nc.scalar.activation(Osb[b % 2], bank(6), ACT.Copy).then_inc(self.o_free, 1)

                for n in self.steps():
                    for kind, b, i in self.sched.get(n, []):
                        task(kind, b, i)
                    if 0 <= n < NSTEP:
                        m, j = n // 4, n % 4
                        act.wait_ge(self.st_full, n + 1)
                        if j == 0 and m >= 2:
                            act.wait_ge(self.pv_done, m - 1)
                        nc.scalar.activation(PH[:, m % 2, j, :], bank(n % 2), ACT.Exp).then_inc(self.st_read, 1)

            def dve(self, v, link):
                for s, n in self.before:
                    v.wait_ge(s, n)
                for g in range(4):
                    v.memset(KP[g][96:98, :, :], 1.0)
                v.memset(Vt[:, :, :, HD:2 * HD], 1.0).then_inc(self.init, 1)

                def task(kind, b, i):
                    if kind == "LNS":
                        norm_stats(v, link, self.norm0 + b, b, [(ld_x[b], 16) if self.a == 0 else (mlp1.xd, b + 1)])
                    elif kind == "LNN":
                        norm_apply(v, self.norm0 + b, b, [(self.m_full, self.idx("T", b - 1, 1) + 1)] if b else [])
                    elif kind == "V" and self.a == 0:
                        v.wait_ge(self.m_full, self.idx(kind, b, i) + 1)
                        if b:
                            v.wait_ge(self.pv_done, 16 * b)
                        else:
                            v.wait_ge(ld_bias, 64)
                        for t in range(2):
                            ins = v.tensor_tensor(Vt[:, 2 * i + t, :, 0:HD],
                                                  PS[:, 7, 256 * t:256 * (t + 1)].rearrange("p (h c) -> p h c", h=NH),
                                                  bias_bc[:, 0, :].rearrange("p (h c) -> p h c", h=NH), ALU.add)
                        ins.then_inc(self.m_free, 1)
                    elif kind in ("RQ", "RK"):
                        v.wait_ge(self.m_full, self.idx(kind, b, i) + 1)
                        p = 2 * b + i
                        k = 2 * p + (kind == "RK")
                        if k >= 2:
                            v.wait_ge(self.split, (k - 2) // 2 + 1)
                        v.tensor_tensor(rt[k % 2], bank(7), rope[:, 1, :], ALU.mult).then_inc(self.m_free, 1)
                    elif kind == "M":
                        v.wait_ge(self.m_full, self.idx(kind, b, i) + 1)
                        if b >= 2:
                            v.wait_ge(self.mset[(b - 2) % 4], 32 * ((b - 2) // 4 + 1))
                        d = mneg[b % 2]
                        link(v.tensor_scalar(d[0:16, 0, :], PS[0:16, 7, 0:P], -1.0, None, ALU.mult))
                        ins = v.scalar_tensor_tensor(out=d[0:16, 1, :], in0=PS[0:16, 7, 0:P], scalar=-1.0,
                                                     in1=d[0:16, 0, :], op0=ALU.mult, op1=ALU.subtract)
                        ins.then_inc(self.m_free, 1)
                    elif kind == "NORM":
                        v.wait_ge(self.oloaded[b % 2], 64 * (b // 2 + 1))
                        v.reciprocal(Oden[b % 2], Oden[b % 2]).then_inc(self.rec, 1)
                    elif kind == "PJ":
                        v.wait_ge(self.m_full, self.idx(kind, b, i) + 1)
                        if b == 0 and i == 0:
                            v.wait_ge(ld_gate[2 * self.a], 16)
                        if b:
                            v.wait_ge(self.xd, 2 * b + i - 1)
                        v.tensor_tensor(tsc[:, 2 * i:2 * i + 2, :],
                                        bank(7).rearrange("p (t c) -> p t c", t=2),
                                        gates[:, 0, 0, b:b + 1, :].to_broadcast([P, 2, D]),
                                        ALU.mult).then_inc(self.m_free, 1)

                for n in self.steps():
                    for kind, b, i in self.sched.get(n, []):
                        task(kind, b, i)
                    w = n + LOOK
                    if 0 <= w < NSTEP and w % 2:
                        u = w // 2
                        G, c = w // 16, (w - 1) % 16
                        v.wait_ge(self.sm_full, u + 1)
                        if u % 8 == 0 and G >= 2:
                            v.wait_ge(self.m_full, self.idx("M", G - 2, 0) + 1)
                        v.tensor_reduce(mx[:, G % 2, c:c + 2], PS[:, 2 + (w - 1) % 4:4 + (w - 1) % 4, :],
                                        AX.X, ALU.max).then_inc(self.sm_free, 1)

            def pool(self, pool, link):
                def task(kind, b, i):
                    if kind == "LNS":
                        norm_rstd(pool, link, self.norm0 + b)
                    elif kind == "SPLIT":
                        p = 2 * b + i
                        if b:
                            pool.wait_ge(self.saved[i], 32 * b)
                        last = "RK" if self.a else "K"
                        pool.wait_ge(self.m_free, self.idx(last, b, i) + 1)
                        for k in range(2):
                            src, d = q32[2 * i + k], parts[2 * i + k]
                            if self.a:
                                link(pool.tensor_tensor(src, src, rope[:, 0, :], ALU.mult))
                                link(pool.tensor_tensor(src, src, rt[k], ALU.add))
                            link(pool.tensor_copy(d[:, 0, :], src))
                            link(pool.tensor_tensor(resid, src, d[:, 0, :], ALU.subtract))
                            link(pool.tensor_copy(d[:, 1, :], resid))
                            ins = pool.tensor_tensor(d[:, 2, :], resid, d[:, 1, :], ALU.subtract)
                            if k == 0:
                                link(ins)
                        ins.then_inc(self.split, 1)
                    elif kind == "NORM":
                        pool.wait_ge(self.rec, b + 1)
                        if b >= 2:
                            pool.wait_ge(self.m_full, self.idx("PJ", b // 2 - 1, 1) + 1)
                        pool.tensor_tensor(yT[:, b % 2, :], Onum[b % 2], Oden[b % 2], ALU.mult).then_inc(self.y, 1)
                    elif kind == "PJ":
                        if self.a == 0 and i == 0:
                            pool.wait_ge(ld_gate[0], 16)
                            pool.wait_ge(ln_done, self.norm0 + b + 1)
                            link(pool.tensor_tensor(gate_bias[:, :], gates[:, 0, 0, b, :], bias_bc[:, 1, :], ALU.mult))
                            for t in range(TT):
                                ins = pool.tensor_tensor(x[:, TT * b + t, :], x[:, TT * b + t, :], gate_bias[:, :], ALU.add)
                            link(ins)
                        pool.wait_ge(self.m_free, self.idx(kind, b, i) + 1)
                        xs = x[:, TT * b + 2 * i:TT * b + 2 * i + 2, :]
                        pool.tensor_tensor(xs, xs, tsc[:, 2 * i:2 * i + 2, :], ALU.add).then_inc(self.xd, 1)

                for n in self.steps():
                    for kind, b, i in self.sched.get(n, []):
                        task(kind, b, i)

            def sync(self, sp):
                def task(kind, b, i):
                    if kind == "SAVE":
                        sp.wait_ge(self.split, 2 * b + i + 1)
                        for k in range(2):
                            sp.dma_start(d_parts[self.a, 4 * b + 2 * i + k], parts[2 * i + k]).then_inc(self.saved[i], 16)
                    elif kind == "FILL":
                        g = i
                        sp.wait_ge(self.saved[g // 2], 32 * (b + 1))
                        if b:
                            sp.wait_ge(self.st_full, 64 * (b - 1) + 16 * (g + 1))
                        q = d_parts[self.a, 4 * b + 2 * (g // 2)]
                        k = d_parts[self.a, 4 * b + 2 * (g // 2) + 1]
                        for dst, src, plan in ((QP[g], q, ("000", "11", "2")), (KP[g], k, ("012", "01", "0"))):
                            slot = 0
                            for pieces in plan:
                                for c in pieces:
                                    s_ = src[64 * (g % 2):64 * (g % 2) + 64, int(c), :].rearrange(
                                        "(j d) t -> d j t", j=4)
                                    sp.dma_start(dst[16 * slot:16 * slot + 16, :, :], s_).then_inc(self.filled[g], 16)
                                    slot += 1
                    elif kind == "MROW":
                        g = b % 4
                        sp.wait_ge(self.m_free, self.idx("M", b, 0) + 1)
                        for r in range(2):
                            sp.dma_start(QP[g][96 + r:97 + r, :, :].rearrange("p j (q c) -> p (j q) c", c=P),
                                         mneg[b % 2][0:16, r, :]).then_inc(self.mset[g], 16)
                    elif kind == "OSAVE":
                        sp.wait_ge(self.o_free, b + 1)
                        sp.dma_start(d_o[self.a, b], Osb[b % 2]).then_inc(self.osaved[b % 2], 16)
                    elif kind == "OLOAD":
                        sp.wait_ge(self.osaved[b % 2], 16 * (b // 2 + 1))
                        hp = b // 2
                        if hp >= 2:
                            sp.wait_ge(self.y, hp - 1)
                        src = d_o[self.a, b].rearrange("(j r) t -> j r t", j=4)
                        r0 = 64 * (b % 2)
                        for dst, lo in ((Onum, 0), (Oden, HD)):
                            sp.dma_start(dst[hp % 2][r0:r0 + 64, :], src[:, lo:lo + HD, :]).then_inc(
                                self.oloaded[hp % 2], 16)

                for n in self.steps():
                    for kind, b, i in self.sched.get(n, []):
                        task(kind, b, i)


        class MLP:

            def __init__(self, l, before, xready, norm0, b1, func, bias_row, extra=None):
                self.l, self.before, self.xready, self.norm0 = l, before, xready, norm0
                self.b1, self.func, self.bias_row, self.extra = b1, func, bias_row, extra
                n = f"m{l}_"
                self.t_full, self.t_out = sem(n + "t_full"), sem(n + "t_out")
                self.w1, self.h_full, self.h_free = sem(n + "w1"), sem(n + "h_full"), sem(n + "h_free")
                self.w2, self.acc_free, self.xd = sem(n + "w2"), sem(n + "acc_free"), sem(n + "x_done")

            def pe(self, pe):
                for s_, n in self.before:
                    pe.wait_ge(s_, n)

                def transposes(b):
                    pe.wait_ge(ln_done, self.norm0 + b + 1)
                    if b:
                        pe.wait_ge(self.t_out, 2 * b)
                    for half in range(2):
                        turn(pe, bank(6 + half), half).then_inc(self.t_full, 1)

                transposes(0)
                pe.wait_ge(ld_mlp[self.l], 32)
                for b in range(B):
                    pe.wait_ge(self.t_out, 2 * b + 2)
                    for m in range(FM):
                        q = FM * b + m
                        if q >= 2:
                            pe.wait_ge(self.h_free, q - 1)
                        for k in range(DH):
                            ins = pe.matmul(bank(4 + q % 2), W1[:, k, m * P:(m + 1) * P], XN[:, k, :],
                                            start=(k == 0), stop=(k == 1))
                        ins.then_inc(self.h_full, 1)
                    if b + 1 < B:
                        transposes(b + 1)
                    if b:
                        pe.wait_ge(self.acc_free, b)
                    for m in range(FM):
                        pe.wait_ge(self.h_free, FM * b + m + 1)
                        for t in range(TT):
                            ins = pe.matmul(bank(t, D), H[:, m, t * P:(t + 1) * P], W2[:, m, :],
                                            start=(m == 0), stop=(m == FM - 1))
                    ins.then_inc(self.w2, 1)

            def act(self, act):
                for b in range(B):
                    for m in range(FM):
                        act.wait_ge(self.h_full, FM * b + m + 1)
                        if m == 0 and b:
                            act.wait_ge(self.w2, b)
                        bias = column(self.b1, m) if self.b1 else 0.0
                        nc.scalar.activation(H[:, m, :], bank(4 + (FM * b + m) % 2), self.func,
                                             bias=bias).then_inc(self.h_free, 1)

            def dve(self, v, link):
                def norm(b):
                    s_, n = self.xready
                    norm_stats(v, link, self.norm0 + b, b, [(s_, n * (b + 1))])
                    norm_apply(v, self.norm0 + b, b, [(self.t_full, 2 * b)] if b else [])
                    if b:
                        v.wait_ge(self.h_full, FM * b)
                    for half in range(2):
                        v.wait_ge(self.t_full, 2 * b + half + 1)
                        m = 2 * self.l + 1
                        v.tensor_scalar(XN[:, half, :], bank(6 + half), mod[:, m, 1, half, b:b + 1],
                                        mod[:, m, 0, half, b:b + 1], ALU.mult, ALU.add).then_inc(self.t_out, 1)

                norm(0)
                for b in range(B):
                    if b + 1 < B:
                        norm(b + 1)
                    if self.extra:
                        self.extra(v, link, b)
                    v.wait_ge(self.w2, b + 1)
                    if b:
                        v.wait_ge(self.xd, b)
                    v.tensor_tensor(tsc[:, :, :], PS[:, 0:TT, 0:D],
                                    gates[:, self.l % 2, 1, b:b + 1, :].to_broadcast([P, TT, D]),
                                    ALU.mult).then_inc(self.acc_free, 1)

            def pool(self, pool, link):
                norm_rstd(pool, link, self.norm0)
                for b in range(B):
                    if b + 1 < B:
                        norm_rstd(pool, link, self.norm0 + b + 1)
                    if self.bias_row is not None:
                        link(pool.tensor_tensor(gate_bias[:, :], gates[:, self.l % 2, 1, b, :],
                                                bias_bc[:, self.bias_row, :], ALU.mult))
                        pool.wait_ge(ln_done, self.norm0 + b + 1)
                        for t in range(TT):
                            ins = pool.tensor_tensor(x[:, TT * b + t, :], x[:, TT * b + t, :], gate_bias[:, :], ALU.add)
                        link(ins)
                    pool.wait_ge(self.acc_free, b + 1)
                    pool.tensor_tensor(batch(b), batch(b), tsc[:, :, :], ALU.add).then_inc(self.xd, 1)

        class S5:
            def __init__(self, before, xready, norm0):
                self.before, self.xready, self.norm0 = before, xready, norm0
                self.t_full, self.t_out = sem("s_t_full"), sem("s_t_out")
                self.bu_full, self.bu_free = sem("s_bu_full"), sem("s_bu_free")
                self.scan, self.yprod = sem("s_scan"), sem("s_yprod")
                self.c_full, self.acc_free, self.xd = sem("s_c_full"), sem("s_acc_free"), sem("s_x_done")

            def pe(self, pe):
                for s_, n in self.before:
                    pe.wait_ge(s_, n)

                def inputs(b):
                    pe.wait_ge(ln_done, self.norm0 + b + 1)
                    if b:
                        pe.wait_ge(self.t_out, 2 * b)
                    for half in range(2):
                        turn(pe, bank(6 + half), half).then_inc(self.t_full, 1)
                    pe.wait_ge(self.t_out, 2 * b + 2)
                    if b:
                        pe.wait_ge(self.bu_free, b)
                    for a in range(2):
                        for k in range(DH):
                            ins = pe.matmul(bank(4 + a), BT[:, a, k, :], XS[b % 2][:, k, :],
                                            start=(k == 0), stop=(k == 1))
                    ins.then_inc(self.bu_full, 1)

                def outputs(b):
                    pe.wait_ge(self.yprod, b + 1)
                    if b:
                        pe.wait_ge(self.acc_free, b)
                    for t in range(TT):
                        c = slice(t * P, (t + 1) * P)
                        for k in range(DH):
                            pe.matmul(PS[:, t, k * P:(k + 1) * P], XS[b % 2][:, k, c], diagD[:, k, :],
                                      start=(k == 0), stop=False, skip_group_check=True)
                        for a in range(2):
                            ins = pe.matmul(bank(t, D), ysc[b % 2][a][:, c], CT[:, a, :],
                                            start=False, stop=(a == 1), skip_group_check=True)
                    ins.then_inc(self.c_full, 1)

                for b in range(B):
                    inputs(b)
                    if b:
                        outputs(b - 1)
                outputs(B - 1)

            def dve(self, v, link):
                def norm(b):
                    s_, n = self.xready
                    norm_stats(v, link, self.norm0 + b, b, [(s_, n * (b + 1))])
                    norm_apply(v, self.norm0 + b, b, [(self.t_full, 2 * b)] if b else [])
                    if b >= 2:
                        v.wait_ge(self.c_full, b - 1)
                    for half in range(2):
                        v.wait_ge(self.t_full, 2 * b + half + 1)
                        v.tensor_scalar(XS[b % 2][:, half, :], bank(6 + half), mod[:, 2, 1, half, b:b + 1],
                                        mod[:, 2, 0, half, b:b + 1], ALU.mult, ALU.add).then_inc(self.t_out, 1)

                def result(b):
                    v.wait_ge(self.c_full, b + 1)
                    if b == 0:
                        v.wait_ge(ld_gate[1], 16)
                        v.wait_ge(low_saved, 128)
                    else:
                        v.wait_ge(self.xd, b)
                    v.tensor_tensor(tsc[:, :, :], PS[:, 0:TT, 0:D],
                                    gates[:, 1, 0, b:b + 1, :].to_broadcast([P, TT, D]),
                                    ALU.mult).then_inc(self.acc_free, 1)

                norm(0)
                for b in range(B):
                    if b + 1 < B:
                        norm(b + 1)
                    v.wait_ge(self.bu_full, b + 1)
                    if b:
                        v.wait_ge(self.scan, b)
                    v.tensor_tensor(bu[0], bank(4), CC, ALU.mult)
                    ins = v.tensor_tensor(bu[1], bank(5), SS, ALU.mult)
                    ins.then_inc(self.bu_free, 1)
                    v.wait_ge(self.bu_free, b + 1)
                    link(v.tensor_tensor(bu[0], bu[0], bu[1], ALU.add))
                    if b >= 2:
                        v.wait_ge(self.yprod, b - 1)
                    v.tensor_tensor_scan(yst[b % 2], RR, bu[0], 0.0, ALU.mult, ALU.add).then_inc(self.scan, 1)
                    if b:
                        result(b - 1)
                result(B - 1)

            def pool(self, pool, link):
                norm_rstd(pool, link, self.norm0)

                def add(b):
                    pool.wait_ge(self.acc_free, b + 1)
                    pool.tensor_tensor(batch(b), batch(b), tsc[:, :, :], ALU.add).then_inc(self.xd, 1)

                for b in range(B):
                    if b + 1 < B:
                        norm_rstd(pool, link, self.norm0 + b + 1)
                    pool.wait_ge(self.scan, b + 1)
                    if b >= 2:
                        pool.wait_ge(self.c_full, b - 1)
                    pool.tensor_tensor(ysc[b % 2][0], yst[b % 2], CC, ALU.mult)
                    pool.tensor_tensor(ysc[b % 2][1], yst[b % 2], SS, ALU.mult).then_inc(self.yprod, 1)
                    if b:
                        add(b - 1)
                add(B - 1)

        def c_(i):
            return sv[:, i:i + 1]

        (DT, KN, RD, EA, TH, VV, SN, CM, TMP, RAD, CO, NR, NI, FR, FI, SFI, NSFR, DEN, ANG_C, ANG_S, T2, M2SG,
         TWO_N) = range(23)

        def s5_scalars(v, link):
            v.wait_ge(ld_s5, 16 * 19)
            re, im, ls, sg = (lam[:, i:i + 1] for i in range(4))

            def ts(o, a, s1, s2, op0, op1=ALU.bypass):
                link(v.tensor_scalar(c_(o), a, s1, s2, op0, op1) if s2 is not None else
                     v.tensor_scalar(c_(o), a, s1, None, op0))

            def stt(o, a, s_, b_, op0, op1):
                link(v.scalar_tensor_tensor(out=c_(o), in0=a, scalar=s_, in1=b_, op0=op0, op1=op1))

            ts(KN, ls, LOG2E, None, ALU.mult)
            ts(KN, c_(KN), ROUND, None, ALU.add)
            ts(KN, c_(KN), -ROUND, None, ALU.add)
            stt(RD, c_(KN), -LN2_HI, ls, ALU.mult, ALU.add)
            stt(RD, c_(KN), -LN2_LO, c_(RD), ALU.mult, ALU.add)
            ts(DT, c_(RD), 1.0 / 5040, 1.0 / 720, ALU.mult, ALU.add)
            for q in (1.0 / 120, 1.0 / 24, 1.0 / 6, 0.5, 1.0, 1.0):
                ts(DT, c_(DT), c_(RD), q, ALU.mult, ALU.add)
            link(v.tensor_scalar(lam_i[:, :], c_(KN), 127.0, 8388608.0, ALU.add, ALU.mult))
            stt(DT, c_(DT), 1.0, lam_i[:, :].bitcast(F32), ALU.mult, ALU.mult)
            ts(TMP, re, c_(DT), 1.0 / 64, ALU.mult, ALU.mult)
            ts(EA, c_(TMP), 1.0 / 40320, 1.0 / 5040, ALU.mult, ALU.add)
            for q in (1.0 / 720, 1.0 / 120, 1.0 / 24, 1.0 / 6, 0.5, 1.0):
                ts(EA, c_(EA), c_(TMP), q, ALU.mult, ALU.add)
            ts(EA, c_(EA), c_(TMP), None, ALU.mult)
            for _ in range(6):
                stt(EA, c_(EA), 2.0, c_(EA), ALU.add, ALU.mult)
            ts(RAD, c_(EA), 1.0, None, ALU.add)
            ts(TH, im, c_(DT), None, ALU.mult)
            ts(KN, c_(TH), 0.15915494309189535, None, ALU.mult)
            ts(KN, c_(KN), ROUND, None, ALU.add)
            ts(KN, c_(KN), -ROUND, None, ALU.add)
            for q in (TWO_PI_A, TWO_PI_B, TWO_PI_C):
                stt(TH, c_(KN), -q, c_(TH), ALU.mult, ALU.add)
            ts(TH, c_(TH), 0.125, None, ALU.mult)
            ts(VV, c_(TH), c_(TH), None, ALU.mult)
            ts(SN, c_(VV), 1.0 / 362880, -1.0 / 5040, ALU.mult, ALU.add)
            for q in (1.0 / 120, -1.0 / 6, 1.0):
                ts(SN, c_(SN), c_(VV), q, ALU.mult, ALU.add)
            ts(SN, c_(SN), c_(TH), None, ALU.mult)
            ts(CM, c_(VV), 1.0 / 40320, -1.0 / 720, ALU.mult, ALU.add)
            for q in (1.0 / 24, -0.5):
                ts(CM, c_(CM), c_(VV), q, ALU.mult, ALU.add)
            ts(CM, c_(CM), c_(VV), None, ALU.mult)
            for _ in range(3):
                ts(TMP, c_(CM), 1.0, 2.0, ALU.add, ALU.mult)
                ts(T2, c_(SN), c_(TMP), None, ALU.mult)
                ts(CM, c_(SN), c_(SN), -2.0, ALU.mult, ALU.mult)
                ts(SN, c_(T2), 1.0, None, ALU.mult)
            ts(CO, c_(CM), 1.0, None, ALU.add)
            stt(NR, c_(EA), c_(CO), c_(CM), ALU.mult, ALU.add)
            ts(NI, c_(RAD), c_(SN), None, ALU.mult)
            ts(DEN, re, re, None, ALU.mult)
            stt(DEN, im, im, c_(DEN), ALU.mult, ALU.add)
            link(v.reciprocal(c_(DEN), c_(DEN)))
            ts(FR, c_(NI), im, None, ALU.mult)
            stt(FR, c_(NR), re, c_(FR), ALU.mult, ALU.add)
            ts(FR, c_(FR), c_(DEN), None, ALU.mult)
            ts(FI, c_(NR), im, None, ALU.mult)
            stt(FI, c_(NI), re, c_(FI), ALU.mult, ALU.subtract)
            ts(FI, c_(FI), c_(DEN), None, ALU.mult)
            ts(SFI, c_(FI), sg, None, ALU.mult)
            ts(NSFR, c_(FR), sg, -1.0, ALU.mult, ALU.mult)
            ts(M2SG, sg, -2.0, None, ALU.mult)

        def s5_tables(v, link):
            link(v.memset(CC[:, 0:1], 1.0))
            link(v.memset(SS[:, 0:1], 0.0))
            link(v.memset(RR, 1.0))
            link(v.tensor_scalar(RR, RR, c_(RAD), None, ALU.mult))
            link(v.tensor_copy(c_(ANG_C), c_(CO)))
            link(v.tensor_copy(c_(ANG_S), c_(SN)))
            n = 1
            while n < T:
                link(v.tensor_scalar(s5t[:, 0:n], SS[:, 0:n], c_(ANG_S), -1.0, ALU.mult, ALU.mult))
                link(v.scalar_tensor_tensor(out=CC[:, n:2 * n], in0=CC[:, 0:n], scalar=c_(ANG_C), in1=s5t[:, 0:n],
                                            op0=ALU.mult, op1=ALU.add))
                link(v.tensor_scalar(s5t[:, 0:n], SS[:, 0:n], c_(ANG_C), None, ALU.mult))
                link(v.scalar_tensor_tensor(out=SS[:, n:2 * n], in0=CC[:, 0:n], scalar=c_(ANG_S), in1=s5t[:, 0:n],
                                            op0=ALU.mult, op1=ALU.add))
                link(v.tensor_scalar(c_(TMP), c_(ANG_S), c_(ANG_S), -1.0, ALU.mult, ALU.mult))
                link(v.tensor_scalar(c_(T2), c_(ANG_S), c_(ANG_C), 2.0, ALU.mult, ALU.mult))
                link(v.scalar_tensor_tensor(out=c_(ANG_C), in0=c_(ANG_C), scalar=c_(ANG_C), in1=c_(TMP),
                                            op0=ALU.mult, op1=ALU.add))
                link(v.tensor_copy(c_(ANG_S), c_(T2)))
                n *= 2
            for a, (p_, q_) in enumerate(((FR, SFI), (FI, NSFR))):
                link(v.tensor_scalar(s5t[:, 0:D], s5B[:, 1, :], c_(q_), None, ALU.mult))
                link(v.scalar_tensor_tensor(out=s5W[:, a, :], in0=s5B[:, 0, :], scalar=c_(p_), in1=s5t[:, 0:D],
                                            op0=ALU.mult, op1=ALU.add))
            for k in range(DH):
                ins = v.tensor_scalar(diagD[:, k, :], ident[:, :], column("Dd", k), None, ALU.mult)
            ins.then_inc(s5_pre, 1)

        def setup_pe(pe):
            pe.wait_ge(ld_rows, 16 * 13)
            pe.wait_ge(ld_const, 32)
            pe.transpose(PS[:, 2, 0:NROWS], rows[:, :], ident[0:NROWS, 0:NROWS]).then_inc(row_tr, 1)
            mod_rows(pe, 0, Wm0, cs, 3, [(silu_ready, 1), (ld_wm0, 16)])

        def setup_act(act):
            act.wait_ge(cols_ready, 1)
            nc.scalar.activation(csig[:, :], col[:, 0:8], ACT.Exp, scale=-1.0).then_inc(silu_e, 1)

        def setup_dve(v, link):
            v.memset(cs[:, :, :], 0.0)
            v.memset(cc[:, :, :], 0.0)
            v.memset(lnc[:, :, :], 0.0)
            link(v.memset(h3[:, :, :], 0.0))
            v.memset(mhalf[:, :], -0.5).then_inc(consts_set, 1)
            v.wait_ge(row_tr, 1)
            v.tensor_copy(col[:, :], PS[:, 2, 0:NROWS]).then_inc(cols_ready, 1)
            v.wait_ge(silu_e, 1)
            link(v.tensor_scalar(csig[:, :], csig[:, :], 1.0, None, ALU.add))
            link(v.reciprocal(csig[:, :], csig[:, :]))
            cond = col[:, 0:8].rearrange("p (b k) -> p k b", k=2)
            v.tensor_tensor(cs[:, :, 0:B], cond, csig[:, :].rearrange("p (b k) -> p k b", k=2), ALU.mult)
            v.tensor_copy(cc[:, :, 0:B], cond).then_inc(silu_ready, 1)
            link(v.tensor_scalar(bq16[:, :], col[:, ROWS["L0_bq"][0]:ROWS["L0_bq"][0] + 2], 1.0 / HD, None, ALU.mult))

        def mod_simple(v, link, i, m, s_shift, s_scale, g=None, b_=None):
            for half in range(2):
                sh, sc = mod[:, m, 0, half, :], mod[:, m, 1, half, :]
                link(v.tensor_scalar(sc, section(i, s_scale, half), 1.0, None, ALU.add))
                if g is None:
                    link(v.tensor_copy(sh, section(i, s_shift, half)))
                else:
                    link(v.scalar_tensor_tensor(out=sh, in0=sc, scalar=column(b_, half),
                                                in1=section(i, s_shift, half), op0=ALU.mult, op1=ALU.add))
                    link(v.tensor_scalar(sc, sc, column(g, half), None, ALU.mult))

        def mid_pe(pe, before):
            for s_, n in before:
                pe.wait_ge(s_, n)
            mod_rows(pe, 1, Wm1, cc, 3, [(ld_mid, 16 * 4)])
            mod_rows(pe, 2, Wc1, cc, 1, [(mod_ready, 2)])
            mod_rows(pe, 3, Wm2, cs, 3, [(mod_ready, 3)])
            pe.wait_ge(s5_pre, 1)
            for a in range(2):
                for k in range(DH):
                    pe.transpose(PS[:, 4, (2 * a + k) * P:(2 * a + k + 1) * P], s5W[:, a, k * P:(k + 1) * P], ident[:, :])
                    ins = pe.transpose(PS[:, 5, (2 * a + k) * P:(2 * a + k + 1) * P], s5C[:, a, k, :], ident[:, :])
            ins.then_inc(s5_tr, 1)
            pe.wait_ge(l3_ready, 1)
            for k in range(DH):
                ins = pe.transpose(PS[:, 6, k * 32:k * 32 + B], c4[:, k * P:(k + 1) * P], ident[0:B, 0:B])
            ins.then_inc(l3_tr, 1)
            pe.wait_ge(l3_ready, 2)
            for m in range(2):
                for k in range(DH):
                    ins = pe.matmul(PS[:, 7, m * 32:m * 32 + B], WL3[:, k, m * P:(m + 1) * P], lnc[:, k, 0:B],
                                    start=(k == 0), stop=(k == 1))
            ins.then_inc(l3_h, 1)
            pe.wait_ge(l3_hg, 2)
            for r in range(2):
                pe.wait_ge(ld_ring[r], 16 * 4)
                if r:
                    pe.wait_ge(l3_wr, 1)
                for c in range(2):
                    for k in range(DH):
                        for j in range(4):
                            ins = pe.matmul(PS[32 * j:32 * j + 32, 2 + c, :], h3[:, k, :],
                                            ring[j][:, k, 512 * c:512 * (c + 1)], start=(k == 0), stop=(k == 1))
                ins.then_inc(l3_w, 1)

        def mid_act(act):
            for m in range(2):
                act.wait_ge(l3_h, 1)
                nc.scalar.activation(h3[:, m, 0:B], PS[:, 7, m * 32:m * 32 + B], ACT.Gelu,
                                     bias=column("L3_b1", m)).then_inc(l3_hg, 1)

        def mid_dve(v, link):
            mod_evac(v, 1, 3, [(gate_saved, 32)])
            v.wait_ge(mod_ready, 2)
            mod_simple(v, link, 1, 2, SHIFT, SCALE)
            mod_evac(v, 2, 1, [(gate_saved, 64)])
            v.wait_ge(mod_ready, 3)
            for half in range(2):
                sh, sc = mod[:, 3, 0, half, :], mod[:, 3, 1, half, :]
                sf = mod[:, 0, 0, half, :]
                link(v.tensor_scalar(sf, section(1, SCALE2, half), 1.0, None, ALU.add))
                link(v.tensor_scalar(sc, section(2, 0, half), 1.0, None, ALU.add))
                link(v.tensor_tensor(sc, sc, sf, ALU.mult))
                link(v.tensor_tensor(sh, section(2, 1, half), sf, ALU.mult))
                link(v.tensor_tensor(sh, sh, section(1, SHIFT2, half), ALU.add))
            mod_evac(v, 3, 3, [])
            v.wait_ge(mod_ready, 4)
            mod_simple(v, link, 3, 4, SHIFT, SCALE, "n1g", "n1b")
            mod_simple(v, link, 3, 5, SHIFT2, SCALE2, "n2g", "n2b")
            v.wait_ge(s5_tr, 1)
            v.tensor_copy(BT, bank(4).rearrange("p (a k n) -> p a k n", a=2, k=2))
            v.tensor_scalar(CT[:, 0, :], PS[:, 5, 0:D], c_(M2SG), None, ALU.mult)
            v.tensor_scalar(CT[:, 1, :], PS[:, 5, D:2 * D], -2.0, None, ALU.mult).then_inc(s5_ready, 1)
            link(v.bn_stats(c4s[:, 0:6], c4[:, :]))
            link(v.bn_aggr(c4s[:, 6:8], c4s[:, 0:6]))
            v.tensor_scalar(c4s[:, 0:1], c4s[:, 7:8], EPS, None, ALU.add).then_inc(l3_bt, 1)
            v.wait_ge(l3_bt, 2)
            v.tensor_scalar(c4[:, :], c4[:, :], c4s[:, 6:7], c4s[:, 1:2], ALU.subtract, ALU.mult).then_inc(l3_ready, 1)
            v.wait_ge(l3_tr, 1)
            for k in range(DH):
                ins = v.tensor_scalar(lnc[:, k, 0:B], PS[:, 6, k * 32:k * 32 + B], column("lng", k), column("lnb", k),
                                      ALU.mult, ALU.add)
            ins.then_inc(l3_ready, 1)
            for r in range(2):
                v.wait_ge(l3_w, r + 1)
                v.wait_ge(ld_b2[r], 16 * 4)
                if r:
                    v.wait_ge(low_saved, 64)
                v.tensor_tensor(tsc[:, :, :].rearrange("p a b -> p (a b)"),
                                PS[:, 2:4, :].rearrange("p a b -> p (a b)"),
                                xnorm[:, :, :].rearrange("p a b -> p (a b)"), ALU.add).then_inc(l3_wr, 1)

        def mid_pool(pool, link):
            pool.wait_ge(l3_bt, 1)
            link(pool.tensor_tensor(c4s[:, 1:2], c4s[:, 0:1], mhalf[0:B, 0:1], ALU.pow))
            link(pool.tensor_tensor(c4s[:, 2:3], c4s[:, 1:2], c4s[:, 1:2], ALU.mult))
            link(pool.tensor_tensor(c4s[:, 2:3], c4s[:, 2:3], c4s[:, 0:1], ALU.mult))
            link(pool.tensor_scalar(c4s[:, 2:3], c4s[:, 2:3], -0.5, 1.5, ALU.mult, ALU.add))
            pool.tensor_tensor(c4s[:, 1:2], c4s[:, 1:2], c4s[:, 2:3], ALU.mult).then_inc(l3_bt, 1)

        f_bt, f_btr, f_t, f_to = sem("f_bt"), sem("f_btr"), sem("f_t"), sem("f_to")
        f_z, f_zo, f_y, f_yo, f_z2, f_z2o, f_o, f_oo = (sem("f_" + n) for n in (
            "z", "zo", "y", "yo", "z2", "z2o", "o", "oo"))

        class Low:

            def __init__(self, before, xready):
                self.before, self.xready = before, xready

            def pe(self, pe):
                for s_, n in self.before:
                    pe.wait_ge(s_, n)
                pe.wait_ge(ld_low, 64)
                for w in range(2):
                    for b in range(B):
                        for h in range(DH):
                            q = (w * B + b) * DH + h
                            ins = pe.transpose(PS[0:RANK, q // 4, (q % 4) * P:(q % 4 + 1) * P],
                                               raw_a1[:, 1 + 2 * w, b, h, :], ident[:, :])
                ins.then_inc(f_bt, 1)
                for b in range(B):
                    pe.wait_ge(self.xready[0], self.xready[1] * (b + 1))
                    if b:
                        pe.wait_ge(f_to, 2 * b)
                    for half in range(2):
                        turn(pe, bank(6 + half), half,
                             lambda t: x[:, TT * b + t, half * P:(half + 1) * P]).then_inc(f_t, 1)
                for b in range(B):
                    pe.wait_ge(f_to, 2 * b + 2)
                    if b >= 2:
                        pe.wait_ge(f_zo, b - 1)
                    for k in range(DH):
                        ins = pe.matmul(PS[0:RANK, 4 + b % 2, :], raw_a1[:, 0, b, k, :], xT[b][:, k, :],
                                        start=(k == 0), stop=(k == 1))
                    ins.then_inc(f_z, 1)
                pe.wait_ge(f_btr, 4)
                for b in range(B):
                    pe.wait_ge(f_zo, b + 1)
                    for h in range(DH):
                        q = 2 * b + h
                        if q >= 4:
                            pe.wait_ge(f_yo, q - 3)
                        pe.matmul(bank(q % 4), btr[0:RANK, 0, b, h * P:(h + 1) * P], z1[b][0:RANK, :],
                                  start=True, stop=True).then_inc(f_y, 1)
                for b in range(B):
                    pe.wait_ge(f_yo, 2 * b + 2)
                    if b < 2:
                        pe.wait_ge(f_zo, 3 + b)
                    else:
                        pe.wait_ge(f_z2o, b - 1)
                    for k in range(DH):
                        ins = pe.matmul(PS[0:RANK, 4 + b % 2, :], raw_a1[:, 2, b, k, :], gT[b][:, k, :],
                                        start=(k == 0), stop=(k == 1))
                    ins.then_inc(f_z2, 1)
                for b in range(B):
                    pe.wait_ge(f_z2o, b + 1)
                    pe.wait_ge(f_yo, 2 * B)
                    if b:
                        pe.wait_ge(f_oo, b)
                    for t in range(TT):
                        ins = pe.matmul(bank(t, D), z2[b][0:RANK, t * P:(t + 1) * P], btr[0:RANK, 1, b, :],
                                        start=True, stop=True)
                    ins.then_inc(f_o, 1)

            def act(self, act):
                for b in range(B):
                    for h in range(DH):
                        q = 2 * b + h
                        act.wait_ge(f_y, q + 1)
                        nc.scalar.activation(gT[b][:, h, :], bank(q % 4), ACT.Gelu).then_inc(f_yo, 1)

            def dve(self, v, link):
                v.wait_ge(f_bt, 1)
                for w in range(2):
                    for c in range(2):
                        v.tensor_copy(btr[0:RANK, w, 2 * c:2 * c + 2, :], PS[0:RANK, 2 * w + c, :].rearrange(
                            "p (b d) -> p b d", b=2)).then_inc(f_btr, 1)
                for b in range(B):
                    for half in range(2):
                        v.wait_ge(f_t, 2 * b + half + 1)
                        v.tensor_copy(xT[b][:, half, :], bank(6 + half)).then_inc(f_to, 1)
                for b in range(B):
                    v.wait_ge(f_z, b + 1)
                    v.tensor_copy(z1[b][0:RANK, :], PS[0:RANK, 4 + b % 2, :]).then_inc(f_zo, 1)
                for b in range(B):
                    v.wait_ge(f_z2, b + 1)
                    v.tensor_copy(z2[b][0:RANK, :], PS[0:RANK, 4 + b % 2, :]).then_inc(f_z2o, 1)
                for b in range(B):
                    v.wait_ge(f_o, b + 1)
                    v.tensor_tensor(batch(b), batch(b), PS[:, 0:TT, 0:D], ALU.add).then_inc(f_oo, 1)

            def sync(self, sp):
                for b in range(B):
                    sp.wait_ge(f_oo, b + 1)
                    sp.dma_start(out[b].rearrange("(t p) d -> p t d", p=P), batch(b)).then_inc(out_done, 16)
                sp.wait_ge(out_done, 16 * B)

        att0 = Attention(0, [(mod_ready, 1)])
        PJ0, M0 = len([k for k in misc if k[0] == 0]), None
        mlp0 = MLP(0, [(att0.m_free, PJ0), (att0.o_free, NG), (att0.sm_free, 8 * NG), (att0.st_read, NSTEP)],
                   (att0.xd, 2), 4, "L0_b1", ACT.Gelu, 2,
                   lambda v, link, b: (s5_scalars, s5_tables)[b](v, link) if b < 2 else None)
        s5 = S5([(s5_ready, 1), (l3_wr, 2), (l3_hg, 2), (l3_ready, 2)], (mlp0.xd, 1), 8)
        mlp1 = MLP(1, [(s5.t_out, 2 * B), (s5.acc_free, B), (s5.bu_free, B)], (s5.xd, 1), 12, "L1_b1",
                   ACT.Gelu_apprx_tanh, 3)
        att1 = Attention(1, [(mlp1.t_out, 2 * B), (mlp1.acc_free, B), (mlp1.h_free, FM * B)])
        PJ1 = len([k for k in misc if k[0] == 1])
        mlp2 = MLP(2, [(att1.m_free, PJ1), (att1.o_free, NG), (att1.sm_free, 8 * NG), (att1.st_read, NSTEP)],
                   (att1.xd, 2), 20, None, ACT.Gelu, None)
        low = Low([(mlp2.t_out, 2 * B), (mlp2.acc_free, B), (mlp2.h_free, FM * B)], (mlp2.xd, 1))

        block = ctx.enter_context(nc.Block())

        @block.tensor
        def _(pe):
            setup_pe(pe)
            att0.pe(pe)
            mlp0.pe(pe)
            mid_pe(pe, [(mlp0.t_out, 2 * B), (mlp0.acc_free, B), (mlp0.h_free, FM * B)])
            s5.pe(pe)
            mlp1.pe(pe)
            att1.pe(pe)
            mlp2.pe(pe)
            low.pe(pe)

        @block.scalar
        def _(act):
            for k, name in enumerate(("L0_cond_Wq", "L0_cond_Wk", "L0_cond_Wv", "L0_cond_Wo")):
                act.dma_start(WA[:, k], view(A[name])).then_inc(ld_wa, 16)
            for k, name in enumerate(("L0_cond_bv", "L0_cond_bo", "L0_cond_b2", "L1_cond_b2")):
                act.dma_start(bias_bc[:, k, :], A[name].partition_broadcast(P)).then_inc(ld_bias, 16)
            setup_act(act)
            act.wait_ge(mod_ready, 1)
            att0.act(act)
            mlp0.act(act)
            mid_act(act)
            mlp1.act(act)
            att1.act(act)
            mlp2.act(act)
            low.act(act)

        @block.vector
        def _(v):
            link = Chain(v, dve_c)
            setup_dve(v, link)
            mod_evac(v, 0, 3, [])
            v.wait_ge(mod_ready, 1)
            mod_simple(v, link, 0, 0, SHIFT, SCALE)
            mod_simple(v, link, 0, 1, SHIFT2, SCALE2)
            att0.dve(v, link)
            mlp0.dve(v, link)
            mid_dve(v, link)
            s5.dve(v, link)
            mlp1.dve(v, link)
            att1.dve(v, link)
            mlp2.dve(v, link)
            low.dve(v, link)

        @block.gpsimd
        def _(pool):
            link = Chain(pool, pool_c)
            pool.wait_ge(consts_set, 1)
            att0.pool(pool, link)
            mlp0.pool(pool, link)
            mid_pool(pool, link)
            s5.pool(pool, link)
            mlp1.pool(pool, link)
            att1.pool(pool, link)
            mlp2.pool(pool, link)

        @block.sync
        def _(sp):
            for name, src in (("cond", "cond_1024"), ("L0_bq", "L0_cond_bq"), ("L0_bk", "L0_cond_bk"),
                              ("L0_b1", "L0_cond_b1"), ("L1_b1", "L1_cond_b1"), ("n1g", "L2_cond_norm1_g"),
                              ("n1b", "L2_cond_norm1_b"), ("n2g", "L2_cond_norm2_g"), ("n2b", "L2_cond_norm2_b"),
                              ("lng", "L3_cond_ln_g"), ("lnb", "L3_cond_ln_b"), ("L3_b1", "L3_cond_b1"),
                              ("Dd", "L1_cond_D_diag")):
                r0, n = ROWS[name]
                src = A[src] if name != "cond" else A[src].rearrange("b d -> (b d)")
                sp.dma_start(rows[r0:r0 + n, :], src.rearrange("(r c) -> r c", c=P)).then_inc(ld_rows, 16)
            sp.dma_start(ident[:, :], A["const_ident"]).then_inc(ld_const, 16)
            sp.dma_start(lam[:, 3:4], A["const_sign"]).then_inc(ld_const, 16)
            sp.dma_start(Wm0, view(A["L0_cond_Wc"])).then_inc(ld_wm0, 16)
            load_mbias(sp, A["L0_cond_bc"], 3)
            for b in range(B):
                sp.dma_start(batch(b), A["x"][b].rearrange("(t p) d -> p t d", p=P)).then_inc(ld_x[b], 16)
            save_gates(sp, 0)
            load_gates(sp, 0)
            sp.dma_start(W1[:, :, :], view(A["L0_cond_W1"])).then_inc(ld_mlp[0], 16)
            sp.dma_start(W2[:, :, :], view(A["L0_cond_W2"])).then_inc(ld_mlp[0], 16)
            sp.dma_start(rot[:, :], A["const_rot"]).then_inc(ld_rope, 16)
            for k in range(2):
                sp.dma_start(rope[:, k, :], A["const_rope"][k]).then_inc(ld_rope, 16)
            sp.dma_start(c4[:, :], A["cond_1024"]).then_inc(ld_s5, 16)
            for k, name in enumerate(("Lam_re", "Lam_im", "log_step")):
                for h in range(2):
                    sp.dma_start(lam[SSM * h:SSM * (h + 1), k:k + 1],
                                 A["L1_cond_" + name].rearrange("(n o) -> n o", o=1)).then_inc(ld_s5, 16)
            att0.sync(sp)
            sp.wait_ge(att0.m_free, PJ0)
            for h in range(2):
                for a in range(2):
                    sp.dma_start(s5B[SSM * h:SSM * (h + 1), a, :],
                                 A["L1_cond_B_im" if h != a else "L1_cond_B_re"]).then_inc(ld_s5, 16)
                    for k in range(DH):
                        sp.dma_start(s5C[:, a, k, SSM * h:SSM * (h + 1)],
                                     A["L1_cond_C_im" if h != a else "L1_cond_C_re"][k * P:(k + 1) * P, :]).then_inc(
                                         ld_s5, 16)
            load_mbias(sp, A["L1_cond_bm"], 3)
            sp.dma_start(Wm1, view(A["L1_cond_Wm"])).then_inc(ld_mid, 16)
            sp.dma_start(Wc1, view(A["L1_cond_Wc"])).then_inc(ld_mid, 16)
            sp.dma_start(Wm2, view(A["L2_cond_ada_W"])).then_inc(ld_mid, 16)
            sp.dma_start(WL3, view(A["L3_cond_W1"])).then_inc(ld_mid, 16)
            w3, b3 = view(A["L3_cond_W2"]), A["L3_cond_b2"]

            def load_ring(r):
                for j in range(4):
                    c = slice(2048 * j + 1024 * r, 2048 * j + 1024 * (r + 1))
                    sp.dma_start(ring[j], w3[:, :, c]).then_inc(ld_ring[r], 16)

            def load_b2(r):
                for j in range(4):
                    c = slice(2048 * j + 1024 * r, 2048 * j + 1024 * (r + 1))
                    sp.dma_start(xnorm[32 * j:32 * j + 32, :, :].rearrange("p a b -> p (a b)"),
                                 b3[c].partition_broadcast(32)).then_inc(ld_b2[r], 16)

            load_ring(0)
            for k, name in enumerate(("L2_cond_Wq", "L2_cond_Wk", "L2_cond_Wv", "L2_cond_Wo")):
                sp.dma_start(WA[:, k], view(A[name])).then_inc(ld_wa, 16)
            sp.wait_ge(mlp0.t_full, 2 * B)
            load_b2(0)
            sp.wait_ge(mlp0.w2, B)
            sp.dma_start(W1[:, :, :], view(A["L1_cond_W1"])).then_inc(ld_mlp[1], 16)
            sp.dma_start(W2[:, :, :], view(A["L1_cond_W2"])).then_inc(ld_mlp[1], 16)
            save_gates(sp, 1)
            sp.wait_ge(mod_row, 2)
            load_mbias(sp, A["L1_cond_bc"], 1)
            load_gates(sp, 1)
            sp.wait_ge(mod_row, 3)
            load_mbias(sp, A["L2_cond_ada_b"], 3)
            save_gates(sp, 3)
            sp.wait_ge(l3_w, 1)
            load_ring(1)
            sp.wait_ge(l3_wr, 1)
            load_b2(1)
            for r in range(2):
                sp.wait_ge(l3_wr, r + 1)
                for j in range(4):
                    sp.dma_start(d_low[j][:, 1024 * r:1024 * (r + 1)],
                                 tsc[32 * j:32 * j + B, :, :].rearrange("p a b -> p (a b)")).then_inc(low_saved, 16)
            sp.wait_ge(low_saved, 128)
            for j in range(4):
                sp.dma_start(raw_a1[:, j], d_low[j].rearrange("b (h d r) -> d b h r", h=DH, r=RANK)).then_inc(ld_low, 16)
            load_gates(sp, 2)
            sp.wait_ge(mlp1.w2, B)
            sp.dma_start(W1[:, :, :], view(A["L2_cond_W1"])).then_inc(ld_mlp[2], 16)
            sp.dma_start(W2[:, :, :], view(A["L2_cond_W2"])).then_inc(ld_mlp[2], 16)
            att1.sync(sp)
            low.sync(sp)


def constants():
    import numpy as np
    rot = np.zeros((P, P), np.float32)
    for h in range(P // HD):
        for j in range(HD // 2):
            rot[h * HD + 2 * j + 1, h * HD + j] = -1.0
            rot[h * HD + 2 * j, h * HD + HD // 2 + j] = 1.0
    inv = np.float32(1.0) / np.float32(10000.0) ** (np.arange(0, HD, 2, dtype=np.float32) / np.float32(HD))
    f = np.outer(np.arange(T, dtype=np.float32), inv).astype(np.float32)
    e = np.concatenate([f, f], -1).T
    rope = np.stack([np.tile(np.cos(e), (P // HD, 1)), np.tile(np.sin(e), (P // HD, 1))]).astype(np.float32)
    sign = np.concatenate([-np.ones((SSM, 1)), np.ones((SSM, 1))]).astype(np.float32)
    return {"const_ident": np.eye(P, dtype=np.float32), "const_rot": rot, "const_rope": rope, "const_sign": sign}


def kernel(**inputs):
    import numpy as _np
    import concourse.bacc as _bacc
    from concourse import mybir as _mybir
    from concourse.bass_utils import run_bass_kernel_spmd as _run

    nc = _bacc.Bacc("TRN2", target_bir_lowering=False, num_devices=1)
    arrays, args = {}, {}
    for name, value in list(inputs.items()) + list(constants().items()):
        a = _np.ascontiguousarray(value)
        arrays[f"in_{name}_dram"] = a
        args[name] = nc.dram_tensor(f"in_{name}_dram", a.shape, _mybir.dt.from_np(a.dtype), kind="ExternalInput").ap()
    out = nc.dram_tensor("out_0_dram", (B, T, D), F32, kind="ExternalOutput").ap()
    build(nc, args, out)
    r = _run(nc, [arrays], core_ids=[0])
    return r.results[0]["out_0_dram"]
```

```python
from contextlib import ExitStack

import concourse.bass as bass
from concourse import mybir

F32 = mybir.dt.float32
BF16 = mybir.dt.bfloat16
I32 = mybir.dt.int32
ACT = mybir.ActivationFunctionType
ALU = mybir.AluOpType
AX = mybir.AxisListType

P = 128
B, T, D = 4, 512, 256
TT = T // P
DH = D // P
NH, HD = 16, 16
F = 1024
FM = F // P
SSM = 64
RANK = 8
EPS = 1e-5
LOG2E = 1.4426950408889634
LN2_HI, LN2_LO = 0.693145751953125, 1.4286068203094172e-06
TWO_PI_A, TWO_PI_B, TWO_PI_C = 6.28125, 0.0019350051879882812, 3.019916050561733e-07
ROUND = 12582912.0

ROWS = {}
for _name, _n in (("cond", 8), ("L0_bq", 2), ("L0_bk", 2), ("L0_b1", 8), ("L1_b1", 8), ("n1g", 2), ("n1b", 2),
                  ("n2g", 2), ("n2b", 2), ("lng", 2), ("lnb", 2), ("L3_b1", 2), ("Dd", 2)):
    ROWS[_name] = (sum(n for _, n in ROWS.values()), _n)
NROWS = sum(n for _, n in ROWS.values())

SHIFT, SCALE, GATE, SHIFT2, SCALE2, GATE2 = range(6)

NG = 16
NSTEP = NG * 16
LOOK = 28
FILLS = 12 * 16
MISC_KINDS = ("V", "T", "Q", "K", "RQ", "RK", "M", "PJ")


def attention_schedule(rope):
    s = {}

    def put(n, *task):
        s.setdefault(n, []).append(task)

    for b in range(B):
        o = 64 * (b - 1)
        first = b == 0
        put(-60 if first else o - 40, "LNS", b, 0)
        put(-59 if first else o - 30, "LNN", b, 0)
        put(-58 if first else o - 16, "T", b, 0)
        put(-57 if first else o - 14, "T", b, 1)
        for half in range(2):
            at = (-56 + 6 * half) if first else o - 12 + 16 * half
            put(at, "Q", b, half)
            put(at + 1 if first else at + 2, "K", b, half)
            if rope:
                put(at + 2 if first else at + 4, "RQ", b, half)
                put(at + 3 if first else at + 6, "RK", b, half)
            put(at + 4 if first else at + 8, "SPLIT", b, half)
            put(at + 5 if first else at + 24, "SAVE", b, half)
        for g in range(4):
            put((-51 + 6 * (g // 2)) if first else o + (17, 35, 50, 66)[g], "FILL", b, g)
        put(64 * b + 2, "V", b, 0)
        put(64 * b + 3, "V", b, 1)
        put(64 * b + 86, "PJ", b, 0)
        put(64 * b + 88, "PJ", b, 1)
    for G in range(NG):
        put(16 * G - 10, "M", G, 0)
        put(16 * G - 9, "MROW", G, 0)
        put(16 * G + 18, "O", G, 0)
        put(16 * G + 19, "OSAVE", G, 0)
        put(16 * G + 23, "OLOAD", G, 0)
        if G % 2:
            put(16 * G + 27, "RCP", G // 2, 0)
            put(16 * G + 28, "RSAVE", G // 2, 0)
            put(16 * G + 31, "RLOAD", G // 2, 0)
            put(16 * G + 35, "NORM", G // 2, 0)
    put(215, "MLS", 0, 0)
    put(225, "MLN", 0, 0)
    return s


LEAD, TAIL = -30, NSTEP + 2


def build(nc, A, out):
    misc = {}
    scheds = [attention_schedule(False), attention_schedule(True)]
    for a, sched in enumerate(scheds):
        for n in sorted(sched):
            for task in sched[n]:
                if task[0] in MISC_KINDS:
                    misc[(a,) + task] = sum(1 for k in misc if k[0] == a)

    with ExitStack() as ctx:
        def sb(name, shape, dt=F32):
            return ctx.enter_context(nc.sbuf_tensor(name, shape, dt))

        def sem(name):
            return ctx.enter_context(nc.semaphore(name))

        def scratch(name, shape, dt=F32):
            return nc.dram_tensor(name, shape, dt, kind="Internal").ap()

        PS = ctx.enter_context(nc.psum_tensor("PS", [P, 8, 512], F32))

        x = sb("x", [P, B * TT, D])
        WA = sb("WA", [P, 4, DH, D])
        W1 = sb("W1", [P, DH, F])
        W2 = sb("W2", [P, FM, D])
        gates = sb("gates", [P, 2, 2, B, D])
        gate_bias = sb("gate_bias", [P, D])
        bias_bc = sb("bias_bc", [P, 4, D])
        ident = sb("ident", [P, P])
        rot = sb("rot", [P, P])
        rope = sb("rope", [P, 2, T])
        rows = sb("rows", [NROWS, P])
        col = sb("col", [P, NROWS])
        bq16 = sb("bq16", [P, 2])
        cs = sb("cs", [P, 2, 32])
        cc = sb("cc", [P, 2, 32])
        csig = sb("csig", [P, 8])
        mrow_f = sb("mrow_f", [96, 512])
        mbias = sb("mbias", [96, 512])
        mcol = sb("mcol", [P, 2, 4, 96])
        mod = sb("mod", [P, 6, 2, 2, B])
        st6 = sb("st6", [P, TT, 6])
        mv = sb("mv", [P, TT, 2])
        ve = sb("ve", [P, TT])
        rs = sb("rs", [P, 3, TT])
        mhalf = sb("mhalf", [P, TT])
        xnorm = sb("xnorm", [P, TT, D])
        XN = sb("XN", [P, 2, DH, T])
        tsc = sb("tsc", [P, 4, D])
        PH = sb("PH", [P, 2, 4, T])
        H = PH[:, :, :, :].rearrange("p a b t -> p (a b) t")
        UW = 21504
        U = sb("U", [P, UW])

        at = [0]

        def take(words, dt=F32):
            ap = U[:, at[0]:at[0] + words]
            at[0] += words
            assert at[0] <= UW, at[0]
            return ap if dt == F32 else ap.bitcast(dt)

        QP = [take(1024, BF16).rearrange("p (j t) -> p j t", j=4) for _ in range(4)]
        KP = [take(1024, BF16).rearrange("p (j t) -> p j t", j=4) for _ in range(4)]
        Vt = take(TT * NH * 32).rearrange("p (k h c) -> p k h c", k=TT, h=NH)
        parts = [take(768, BF16).rearrange("p (c t) -> p c t", c=3) for _ in range(4)]
        q32 = [take(T) for _ in range(4)]
        resid = take(T)
        Osb = [take(T) for _ in range(2)]
        Onum = [take(T) for _ in range(2)]
        Oden = [take(T) for _ in range(2)]
        Osum = [take(32) for _ in range(2)]
        yT = take(2 * T).rearrange("p (h t) -> p h t", h=2)
        mx = take(32).rearrange("p (a c) -> p a c", a=2)
        mneg = [take(128, BF16).rearrange("p (i c) -> p i c", i=2) for _ in range(2)]
        rt = [take(T) for _ in range(2)]

        at[0] = 0
        ring = [take(2048).rearrange("p (k n) -> p k n", k=2) for _ in range(4)]
        Wm1 = take(3072).rearrange("p (k n) -> p k n", k=2)
        Wm2 = take(3072).rearrange("p (k n) -> p k n", k=2)
        Wc1 = take(1024).rearrange("p (k n) -> p k n", k=2)
        WL3 = take(512).rearrange("p (k n) -> p k n", k=2)
        CC, SS, RR = take(T), take(T), take(T)
        BT = take(512).rearrange("p (a k n) -> p a k n", a=2, k=2)
        CT = take(512).rearrange("p (a n) -> p a n", a=2)
        diagD = take(256).rearrange("p (k n) -> p k n", k=2)
        s5B = take(512).rearrange("p (a n) -> p a n", a=2)
        s5C = take(512).rearrange("p (a k n) -> p a k n", a=2, k=2)
        s5W = take(512).rearrange("p (a n) -> p a n", a=2)
        s5t = take(T)
        Wm0 = PH[:, :, :, :].rearrange("p a b t -> p (a b t)")[:, 0:3072].rearrange("p (k n) -> p k n", k=2)
        at[0] = 0
        bu = [take(T) for _ in range(2)]
        ysc = [[take(T) for _ in range(2)] for _ in range(2)]
        yst = [take(T) for _ in range(2)]
        XS = [take(2 * T).rearrange("p (h t) -> p h t", h=2) for _ in range(2)]
        at[0] = 0
        xT = [take(2 * T).rearrange("p (h t) -> p h t", h=2) for _ in range(B)]
        gT = [take(2 * T).rearrange("p (h t) -> p h t", h=2) for _ in range(B)]
        z1 = [take(T) for _ in range(B)]
        z2 = [take(T) for _ in range(B)]
        btr = take(2 * B * D).rearrange("p (a b d) -> p a b d", a=2, b=B)

        sv = sb("sv", [P, 64])
        lam = sb("lam", [P, 4])
        lam_i = sb("lam_i", [P, 1], I32)
        c4 = sb("c4", [B, D])
        c4s = sb("c4s", [B, 8])
        lnc = sb("lnc", [P, 2, 32])
        h3 = sb("h3", [P, 2, 32])
        b2row = [U[:, 8192 + 1024 * r:8192 + 1024 * (r + 1)] for r in range(2)]
        wrow = [U[:, 10240 + 1024 * r:10240 + 1024 * (r + 1)] for r in range(2)]
        modf = sb("modf", [P, 2, 2, B])
        czero, czero2 = sb("czero", [P, 1]), sb("czero2", [P, 1])
        mods_set = sem("mods_set")

        raw_a1 = sb("raw_a1", [P, 4, B, 2, RANK])

        d_gate = scratch("d_gate", (3, 2, B, D))
        d_parts = scratch("d_parts", (2, 16, P, 3, T), BF16)
        d_o = scratch("d_o", (2, NG, P, T))
        d_rec = scratch("d_rec", (2, NG // 2, 8, T))
        d_low = scratch("d_low", (4, B, 2 * D * RANK // 2))

        ld_cond, ld_bc = sem("ld_cond"), sem("ld_bc")
        ld_rows, ld_const, ld_rope, ld_s5 = sem("ld_rows"), sem("ld_const"), sem("ld_rope"), sem("ld_s5")
        ld_x = [sem(f"ld_x{b}") for b in range(B)]
        ld_wm0, ld_mb = sem("ld_wm0"), sem("ld_mb")
        ld_wa, ld_bias = sem("ld_wa"), sem("ld_bias")
        ld_mlp = [sem(f"ld_mlp{i}") for i in range(3)]
        ld_mid = sem("ld_mid")
        ld_ring = [sem("ld_ring0"), sem("ld_ring1")]
        ld_b2 = [sem("ld_b2_0"), sem("ld_b2_1")]
        ld_low = sem("ld_low")
        ld_gate = [sem(f"ld_gate{i}") for i in range(3)]
        gate_saved = sem("gate_saved")
        low_saved = sem("low_saved")
        out_done = sem("out_done")
        dve_c, pool_c = sem("dve_c"), sem("pool_c")
        cols_ready, silu_e, silu_ready = sem("cols_ready"), sem("silu_e"), sem("silu_ready")
        mod_ps, mod_row, mod_tr, mod_ready = sem("mod_ps"), sem("mod_row"), sem("mod_tr"), sem("mod_ready")
        row_tr = sem("row_tr")
        s5_tr, s5_ready, s5_pre = sem("s5_tr"), sem("s5_ready"), sem("s5_pre")
        l3_tr, l3_h, l3_hg, l3_w, l3_wr, l3_bt, l3_ready = (sem(n) for n in (
            "l3_tr", "l3_h", "l3_hg", "l3_w", "l3_wr", "l3_bt", "l3_ready"))
        consts_set = sem("consts_set")
        ln_stats, ln_rstd, ln_done = sem("ln_stats"), sem("ln_rstd"), sem("ln_done")

        class Chain:

            def __init__(self, eng, s):
                self.eng, self.s, self.n = eng, s, 0

            def __call__(self, ins):
                self.n += 1
                ins.then_inc(self.s, 1)
                self.eng.wait_ge(self.s, self.n)

        def column(name, i):
            return col[:, ROWS[name][0] + i:ROWS[name][0] + i + 1]

        def batch(b):
            return x[:, TT * b:TT * (b + 1), :]

        def bank(i, n=512):
            return PS[:, i, 0:n]

        def norm_stats(v, link, k, b, waits):
            for s, n in waits:
                v.wait_ge(s, n)
            for t in range(TT):
                ins = v.bn_stats(st6[:, t, :], x[:, TT * b + t, :])
            link(ins)
            for t in range(TT):
                ins = v.bn_aggr(mv[:, t, :], st6[:, t, :])
            link(ins)
            v.tensor_scalar(ve[:, :], mv[:, :, 1], EPS, None, ALU.add).then_inc(ln_stats, 1)

        def norm_rstd(pool, link, k):
            pool.wait_ge(ln_stats, k + 1)
            link(pool.tensor_tensor(rs[:, 0, :], ve[:, :], mhalf[:, :], ALU.pow))
            link(pool.tensor_tensor(rs[:, 1, :], rs[:, 0, :], rs[:, 0, :], ALU.mult))
            link(pool.tensor_tensor(rs[:, 1, :], rs[:, 1, :], ve[:, :], ALU.mult))
            link(pool.tensor_scalar(rs[:, 1, :], rs[:, 1, :], -0.5, 1.5, ALU.mult, ALU.add))
            pool.tensor_tensor(rs[:, 2, :], rs[:, 0, :], rs[:, 1, :], ALU.mult).then_inc(ln_rstd, 1)

        def norm_apply(v, k, b, waits):
            v.wait_ge(ln_rstd, k + 1)
            for s, n in waits:
                v.wait_ge(s, n)
            for t in range(TT):
                ins = v.tensor_scalar(xnorm[:, t, :], x[:, TT * b + t, :], mv[:, t, 0:1], rs[:, 2, t:t + 1],
                                      ALU.subtract, ALU.mult)
            ins.then_inc(ln_done, 1)

        def turn(pe, dst, half, src=None):
            for t in range(TT):
                s_ = xnorm[:, t, half * P:(half + 1) * P] if src is None else src(t)
                ins = pe.transpose(dst[:, t * P:(t + 1) * P], s_, ident[:, :])
            return ins

        def section(i, s_, half):
            return mcol[:, i % 2, 2 * (s_ % 2) + half, 32 * (s_ // 2):32 * (s_ // 2) + B]


        def mod_rows(pe, i, W, C, nchunk, waits):
            for s, n in waits:
                pe.wait_ge(s, n)
            for k in range(DH):
                for c in range(nchunk):
                    ins = pe.matmul(PS[32 * c:32 * c + 32, 6, :], C[:, k, :], W[:, k, 512 * c:512 * (c + 1)],
                                    start=(k == 0), stop=(k == 1))
            ins.then_inc(mod_ps, 1)

        def mod_turn(pe, i, nchunk):
            pe.wait_ge(mod_row, i + 1)
            for f in range(4):
                ins = pe.transpose(PS[:, 7, f * 96:f * 96 + 32 * nchunk], mrow_f[0:32 * nchunk, f * P:(f + 1) * P],
                                   ident[0:32 * nchunk, 0:32 * nchunk])
            ins.then_inc(mod_tr, 1)

        MOD_L = (0, 1, None, 2)
        MBIAS = (3, 6, 7, 10)

        def mod_evac(v, i, nchunk, save_waits):
            v.wait_ge(mod_ps, i + 1)
            v.wait_ge(ld_mb, 16 * MBIAS[i])
            for s, n in save_waits:
                v.wait_ge(s, n)
            v.tensor_tensor(mrow_f[0:32 * nchunk, :], PS[0:32 * nchunk, 6, :], mbias[0:32 * nchunk, :],
                            ALU.add).then_inc(mod_row, 1)
            v.wait_ge(mod_tr, i + 1)
            for f in range(4):
                ins = v.tensor_copy(mcol[:, i % 2, f, 0:32 * nchunk], PS[:, 7, f * 96:f * 96 + 32 * nchunk])
            ins.then_inc(mod_ready, 1)

        def load_mbias(sp, src, nchunk):
            for c in range(nchunk):
                sp.dma_start(mbias[32 * c:32 * c + 32, :],
                             src[512 * c:512 * (c + 1)].partition_broadcast(32)).then_inc(ld_mb, 16)

        def save_gates(sp, i):
            l = MOD_L[i]
            sp.wait_ge(mod_row, i + 1)
            sp.dma_start(d_gate[l, 0], mrow_f[32:32 + B, 0:D]).then_inc(gate_saved, 16)
            sp.dma_start(d_gate[l, 1], mrow_f[64:64 + B, D:2 * D]).then_inc(gate_saved, 16)

        def load_gates(sp, l):
            sp.wait_ge(gate_saved, 32 * (l + 1))
            src = d_gate[l].rearrange("a b d -> (a b d)")
            sp.dma_start(gates[:, l % 2].rearrange("p a b d -> p (a b d)"),
                         src.partition_broadcast(P)).then_inc(ld_gate[l], 16)

        def view(w):
            return w.rearrange("(k p) n -> p k n", p=P)

        moved = [[sem(f"{n}{i}") for i in range(m)] for n, m in (
            ("parts_saved", 2), ("filled", 4), ("max_set", 4), ("o_saved", 2), ("o_loaded", 2), ("sums_loaded", 2),
            ("recip_saved", 2), ("recip_loaded", 2))]

        class Attention:

            def __init__(self, a, before):
                self.a, self.before, self.sched = a, before, scheds[a]
                n = f"a{a}_"
                self.st_full, self.st_read = sem(n + "st_full"), sem(n + "st_read")
                self.sm_full, self.sm_free = sem(n + "sm_full"), sem(n + "sm_free")
                self.pv_done, self.o_free = sem(n + "pv_done"), sem(n + "o_free")
                self.m_full, self.m_free = sem(n + "misc_full"), sem(n + "misc_free")
                self.split = sem(n + "split")
                (self.saved, self.filled, self.mset, self.osaved, self.oloaded, self.sloaded, self.rsaved,
                 self.rloaded) = moved
                self.b0 = B * a
                self.rec, self.y = sem(n + "rec"), sem(n + "y")
                self.mlp = None
                self.xd = sem(n + "x_done")
                self.init = sem(n + "init")
                self.norm0 = 0 if a == 0 else 16

            def idx(self, *task):
                return misc[(self.a,) + task]

            def steps(self, task):
                for n in range(LEAD, TAIL + 1):
                    for t in self.sched.get(n, []):
                        task(*t)
                    yield n

            def tasks(self, lo, hi):
                return [t for n in sorted(self.sched) if lo <= n < hi for t in self.sched[n]]

            def lead(self):
                return self.tasks(-100, LEAD)

            def tail(self):
                return self.tasks(TAIL + 1, 1000)

            def pe_task(self, pe):
                def misc_done(ins):
                    ins.then_inc(self.m_full, 1)

                def task(kind, b, i):
                    if kind not in MISC_KINDS:
                        return
                    k = self.idx(kind, b, i)
                    if k:
                        pe.wait_ge(self.m_free, k)
                    if kind == "T":
                        pe.wait_ge(ln_done, self.norm0 + b + 1)
                        misc_done(turn(pe, bank(7), i))
                    elif kind in ("Q", "K"):
                        pe.wait_ge(ld_wa, 64 * (self.a + 1))
                        pe.wait_ge(self.m_free, self.idx("T", b, 1) + 1)
                        w = WA[:, "QK".index(kind)]
                        for k_ in range(DH):
                            ins = pe.matmul(bank(7), w[:, k_, i * P:(i + 1) * P], XN[:, b % 2, k_, :],
                                            start=(k_ == 0), stop=(k_ == 1))
                        misc_done(ins)
                    elif kind in ("RQ", "RK"):
                        pe.wait_ge(self.m_free, self.idx(kind[1], b, i) + 1)
                        pe.wait_ge(ld_rope, 48)
                        misc_done(pe.matmul(bank(7), rot[:, :], q32[2 * i + (kind == "RK")], start=True, stop=True))
                    elif kind == "V":
                        for t in range(2):
                            for k_ in range(DH):
                                ins = pe.matmul(PS[:, 7, 256 * t:256 * (t + 1)],
                                                XN[:, b % 2, k_, (2 * i + t) * P:(2 * i + t + 1) * P], WA[:, 2, k_, :],
                                                start=(k_ == 0), stop=(k_ == 1))
                        misc_done(ins)
                    elif kind == "M":
                        pe.wait_ge(self.sm_free, 8 * (b + 1))
                        misc_done(pe.transpose(PS[0:16, 7, 0:P], mx[:, b % 2, :], ident[:, :]))
                    elif kind == "PJ":
                        pe.wait_ge(self.y, 2 * b + 2)
                        for t in range(2):
                            for k_ in range(DH):
                                ins = pe.matmul(PS[:, 7, 256 * t:256 * (t + 1)],
                                                yT[:, k_, (2 * i + t) * P:(2 * i + t + 1) * P], WA[:, 3, k_, :],
                                                start=(k_ == 0), stop=(k_ == 1))
                        misc_done(ins)

                return task

            def pe(self, pe):
                for s, n in self.before:
                    pe.wait_ge(s, n)
                for n in self.steps(self.pe_task(pe)):
                    if n == 0:
                        pe.wait_ge(self.init, 1)
                    if 0 <= n < NSTEP:
                        b, g, kt, j = n // 64, n // 16 % 4, n // 4 % 4, n % 4
                        if n % 16 == 0:
                            pe.wait_ge(self.mset[g], 32 * (self.b0 + b + 1))
                        if n >= 2:
                            pe.wait_ge(self.st_read, n - 1)
                        pe.matmul(bank(n % 2), KP[g][0:98, j, kt * P:(kt + 1) * P], QP[g][0:98, j, :],
                                  start=True, stop=True).then_inc(self.st_full, 1)
                    w = n + LOOK
                    if 0 <= w < NSTEP:
                        b, g, j, qt = w // 64, w // 16 % 4, w // 4 % 4, w % 4
                        if w % 16 == 0:
                            pe.wait_ge(self.filled[g], FILLS * (self.b0 + b + 1))
                        if w % 2 == 0 and w >= 4:
                            pe.wait_ge(self.sm_free, w // 2 - 1)
                        ins = pe.matmul(bank(2 + w % 4), QP[g][0:96, j, qt * P:(qt + 1) * P], KP[g][0:96, j, :],
                                        start=True, stop=True)
                        if w % 2:
                            ins.then_inc(self.sm_full, 1)
                    if n % 4 == 1 and 0 <= (n - 5) // 4 < NG * 4:
                        m = (n - 5) // 4
                        b, g, kt = m // 16, m // 4 % 4, m % 4
                        pe.wait_ge(self.st_read, 4 * m + 4)
                        if kt == 0:
                            pe.wait_ge(self.m_free, self.idx("V", b, 1) + 1)
                            if m:
                                pe.wait_ge(self.o_free, m // 4)
                        for j in range(4):
                            ins = pe.matmul(PS[32 * j:32 * j + 32, 6, :], Vt[:, kt, 4 * g + j, :], PH[:, m % 2, j, :],
                                            start=(kt == 0), stop=(kt == 3))
                        ins.then_inc(self.pv_done, 1)

            def act_task(self, act):
                def task(kind, b, i):
                    if kind == "T":
                        act.wait_ge(self.m_full, self.idx(kind, b, i) + 1)
                        if b >= 2:
                            act.wait_ge(self.m_full, self.idx("V", b - 2, 1) + 1)
                        elif self.a == 0:
                            act.wait_ge(mod_ready, 1)
                        m = 0 if self.a == 0 else 4
                        nc.scalar.activation(XN[:, b % 2, i, :], bank(7), ACT.Identity, bias=mod[:, m, 0, i, b:b + 1],
                                             scale=mod[:, m, 1, i, b:b + 1]).then_inc(self.m_free, 1)
                    elif kind in ("Q", "K"):
                        act.wait_ge(self.m_full, self.idx(kind, b, i) + 1)
                        if b:
                            act.wait_ge(self.split, 2 * b + i - 1)
                        o = q32[2 * i + (kind == "K")]
                        if self.a == 0:
                            bias = bq16[:, i:i + 1] if kind == "Q" else column("L0_bk", i)
                            ins = nc.scalar.activation(o, bank(7), ACT.Identity, bias=bias,
                                                       scale=1.0 / HD if kind == "Q" else 1.0)
                        else:
                            ins = nc.scalar.activation(o, bank(7), ACT.Copy, scale=HD ** -0.5 if kind == "Q" else 1.0)
                        ins.then_inc(self.m_free, 1)
                    elif kind == "V" and self.a == 1:
                        act.wait_ge(self.m_full, self.idx(kind, b, i) + 1)
                        if b:
                            act.wait_ge(self.pv_done, 16 * b)
                        nc.scalar.activation(Vt[:, 2 * i:2 * i + 2, :, 0:HD],
                                             bank(7).rearrange("p (t h c) -> p t h c", t=2, h=NH),
                                             ACT.Copy).then_inc(self.m_free, 1)
                    elif kind == "O":
                        act.wait_ge(self.pv_done, 4 * b + 4)
                        if b >= 2:
                            act.wait_ge(self.osaved[b % 2], 16 * (2 * self.b0 + b // 2))
                        nc.scalar.activation(Osb[b % 2], bank(6), ACT.Copy).then_inc(self.o_free, 1)

                return task

            def act(self, act):
                for n in self.steps(self.act_task(act)):
                    if 0 <= n < NSTEP:
                        m, j = n // 4, n % 4
                        act.wait_ge(self.st_full, n + 1)
                        if j == 0 and m >= 2:
                            act.wait_ge(self.pv_done, m - 1)
                        nc.scalar.activation(PH[:, m % 2, j, :], bank(n % 2), ACT.Exp).then_inc(self.st_read, 1)

            def split_parts(self, eng, link, b, i):
                zero = czero[:, 0:1].to_broadcast([P, T])
                if b:
                    eng.wait_ge(self.saved[i], 32 * (self.b0 + b))
                last = "RK" if self.a else "K"
                eng.wait_ge(self.m_free, self.idx(last, b, i) + 1)
                for k in range(2):
                    src, d = q32[2 * i + k], parts[2 * i + k]
                    if self.a:
                        link(eng.tensor_tensor(src, src, rope[:, 0, :], ALU.mult))
                        eng.tensor_tensor(d[:, 0, :], src, rt[k], ALU.add)
                        link(eng.tensor_tensor(src, src, rt[k], ALU.add))
                    else:
                        link(eng.tensor_tensor(d[:, 0, :], src, zero, ALU.add))
                    link(eng.tensor_tensor(resid, src, d[:, 0, :], ALU.subtract))
                    link(eng.tensor_tensor(d[:, 1, :], resid, zero, ALU.add))
                    ins = eng.tensor_tensor(d[:, 2, :], resid, d[:, 1, :], ALU.subtract)
                    if k == 0:
                        link(ins)
                ins.then_inc(self.split, 1)

            def dve_task(self, v, link):
                def task(kind, b, i):
                    if kind == "LNS":
                        norm_stats(v, link, self.norm0 + b, b, [(ld_x[b], 16) if self.a == 0 else (mlp1.xd, b + 1)])
                    elif kind == "SPLIT" and b == 0:
                        self.split_parts(v, link, b, i)
                    elif kind == "MLS":
                        norm_stats(v, link, self.mlp.norm0, 0, [(self.xd, 2)])
                    elif kind == "MLN":
                        norm_apply(v, self.mlp.norm0, 0, [(self.m_full, self.idx("T", B - 1, 1) + 1)])
                    elif kind == "LNN":
                        norm_apply(v, self.norm0 + b, b, [(self.m_full, self.idx("T", b - 1, 1) + 1)] if b else
                                   [(mlp1.t_full, 2 * B)] if self.a else [])
                    elif kind == "V" and self.a == 0:
                        v.wait_ge(self.m_full, self.idx(kind, b, i) + 1)
                        if b:
                            v.wait_ge(self.pv_done, 16 * b)
                        else:
                            v.wait_ge(ld_bias, 64)
                        for t in range(2):
                            ins = v.tensor_tensor(Vt[:, 2 * i + t, :, 0:HD],
                                                  PS[:, 7, 256 * t:256 * (t + 1)].rearrange("p (h c) -> p h c", h=NH),
                                                  bias_bc[:, 0, :].rearrange("p (h c) -> p h c", h=NH), ALU.add)
                        ins.then_inc(self.m_free, 1)
                    elif kind in ("RQ", "RK"):
                        v.wait_ge(self.m_full, self.idx(kind, b, i) + 1)
                        p = 2 * b + i
                        k = 2 * p + (kind == "RK")
                        if k >= 2:
                            v.wait_ge(self.split, (k - 2) // 2 + 1)
                        v.tensor_tensor(rt[k % 2], bank(7), rope[:, 1, :], ALU.mult).then_inc(self.m_free, 1)
                    elif kind == "M":
                        v.wait_ge(self.m_full, self.idx(kind, b, i) + 1)
                        if b >= 2:
                            v.wait_ge(self.mset[(b - 2) % 4], 32 * (self.b0 + (b - 2) // 4 + 1))
                        d = mneg[b % 2]
                        link(v.tensor_scalar(d[0:16, 0, :], PS[0:16, 7, 0:P], -1.0, None, ALU.mult))
                        ins = v.scalar_tensor_tensor(out=d[0:16, 1, :], in0=PS[0:16, 7, 0:P], scalar=-1.0,
                                                     in1=d[0:16, 0, :], op0=ALU.mult, op1=ALU.subtract)
                        ins.then_inc(self.m_free, 1)
                    elif kind == "RCP":
                        v.wait_ge(self.sloaded[b % 2], 32 * (self.b0 + b // 2 + 1))
                        v.reciprocal(Osum[b % 2], Osum[b % 2]).then_inc(self.rec, 1)
                    elif kind == "PJ":
                        v.wait_ge(self.m_full, self.idx(kind, b, i) + 1)
                        if b == 0 and i == 0:
                            v.wait_ge(ld_gate[2 * self.a], 16)
                        if b:
                            v.wait_ge(self.xd, 2 * b + i - 1)
                        if b == B - 1:
                            v.wait_ge(self.mlp.xd, 1)
                        v.tensor_tensor(tsc[:, 2 * i:2 * i + 2, :],
                                        bank(7).rearrange("p (t c) -> p t c", t=2),
                                        gates[:, 0, 0, b:b + 1, :].to_broadcast([P, 2, D]),
                                        ALU.mult).then_inc(self.m_free, 1)

                return task

            def dve(self, v, link):
                for n in self.steps(self.dve_task(v, link)):
                    w = n + LOOK
                    if 0 <= w < NSTEP and w % 2:
                        u = w // 2
                        G, c = w // 16, (w - 1) % 16
                        v.wait_ge(self.sm_full, u + 1)
                        if u % 8 == 0 and G >= 2:
                            v.wait_ge(self.m_full, self.idx("M", G - 2, 0) + 1)
                        v.tensor_reduce(mx[:, G % 2, c:c + 2], PS[:, 2 + (w - 1) % 4:4 + (w - 1) % 4, :],
                                        AX.X, ALU.max).then_inc(self.sm_free, 1)

            def pool_task(self, pool, link):
                def task(kind, b, i):
                    if kind == "LNS":
                        norm_rstd(pool, link, self.norm0 + b)
                    elif kind == "MLS":
                        norm_rstd(pool, link, self.mlp.norm0)
                    elif kind == "SPLIT" and b:
                        self.split_parts(pool, link, b, i)
                    elif kind == "NORM":
                        pool.wait_ge(self.oloaded[b % 2], 32 * (self.b0 + b // 2 + 1))
                        pool.wait_ge(self.rloaded[b % 2], 16 * (self.b0 + b // 2 + 1))
                        if b >= 2:
                            pool.wait_ge(self.m_full, self.idx("PJ", b // 2 - 1, 1) + 1)
                        pool.tensor_tensor(yT[:, b % 2, :], Onum[b % 2], Oden[b % 2], ALU.mult).then_inc(self.y, 1)
                    elif kind == "PJ":
                        if self.a == 0 and i == 0:
                            pool.wait_ge(ld_gate[0], 16)
                            pool.wait_ge(ln_done, self.norm0 + b + 1)
                            link(pool.tensor_tensor(gate_bias[:, :], gates[:, 0, 0, b, :], bias_bc[:, 1, :], ALU.mult))
                            for t in range(TT):
                                ins = pool.tensor_tensor(x[:, TT * b + t, :], x[:, TT * b + t, :], gate_bias[:, :], ALU.add)
                            link(ins)
                        pool.wait_ge(self.m_free, self.idx(kind, b, i) + 1)
                        xs = x[:, TT * b + 2 * i:TT * b + 2 * i + 2, :]
                        pool.tensor_tensor(xs, xs, tsc[:, 2 * i:2 * i + 2, :], ALU.add).then_inc(self.xd, 1)

                return task

            def pool(self, pool, link):
                if self.a == 0:
                    pool.wait_ge(ln_rstd, len([t for t in self.lead() if t[0] == "LNS"]))
                else:
                    pool.wait_ge(mlp1.xd, B)
                for g in range(4):
                    link(pool.memset(KP[g][96:98, :, :], 1.0))
                pool.memset(Vt[:, :, :, HD:2 * HD], 1.0).then_inc(self.init, 1)
                for n in self.steps(self.pool_task(pool, link)):
                    pass

            def sync_task(self, sp):
                def task(kind, b, i):
                    if kind == "SAVE":
                        sp.wait_ge(self.split, 2 * b + i + 1)
                        for k in range(2):
                            sp.dma_start(d_parts[self.a, 4 * b + 2 * i + k], parts[2 * i + k]).then_inc(self.saved[i], 16)
                    elif kind == "FILL":
                        g = i
                        sp.wait_ge(self.saved[g // 2], 32 * (self.b0 + b + 1))
                        if b:
                            sp.wait_ge(self.st_full, 64 * (b - 1) + 16 * (g + 1))
                        q = d_parts[self.a, 4 * b + 2 * (g // 2)]
                        k = d_parts[self.a, 4 * b + 2 * (g // 2) + 1]
                        for dst, src, plan in ((QP[g], q, ("000", "11", "2")), (KP[g], k, ("012", "01", "0"))):
                            slot = 0
                            for pieces in plan:
                                for c in pieces:
                                    s_ = src[64 * (g % 2):64 * (g % 2) + 64, int(c), :].rearrange(
                                        "(j d) t -> d j t", j=4)
                                    sp.dma_start(dst[16 * slot:16 * slot + 16, :, :], s_).then_inc(self.filled[g], 16)
                                    slot += 1
                    elif kind == "MROW":
                        g = b % 4
                        sp.wait_ge(self.m_free, self.idx("M", b, 0) + 1)
                        for r in range(2):
                            sp.dma_start(QP[g][96 + r:97 + r, :, :].rearrange("p j (q c) -> p (j q) c", c=P),
                                         mneg[b % 2][0:16, r, :]).then_inc(self.mset[g], 16)
                    elif kind == "OSAVE":
                        sp.wait_ge(self.o_free, b + 1)
                        sp.dma_start(d_o[self.a, b], Osb[b % 2]).then_inc(self.osaved[b % 2], 16)
                    elif kind == "OLOAD":
                        sp.wait_ge(self.osaved[b % 2], 16 * (2 * self.b0 + b // 2 + 1))
                        hp = b // 2
                        if hp >= 2:
                            sp.wait_ge(self.y, hp - 1)
                        src = d_o[self.a, b].rearrange("(j r) t -> j r t", j=4)
                        r0 = 64 * (b % 2)
                        sp.dma_start(Onum[hp % 2][r0:r0 + 64, :], src[:, 0:HD, :]).then_inc(self.oloaded[hp % 2], 16)
                        sp.dma_start(Osum[hp % 2][r0:r0 + 64, :], src[:, HD, :].rearrange(
                            "j (a c) -> j a c", c=32)).then_inc(self.sloaded[hp % 2], 16)
                    elif kind == "RSAVE":
                        sp.wait_ge(self.rec, b + 1)
                        sp.dma_start(d_rec[self.a, b].rearrange("j (a c) -> (j a) c", c=32),
                                     Osum[b % 2]).then_inc(self.rsaved[b % 2], 16)
                    elif kind == "RLOAD":
                        sp.wait_ge(self.rsaved[b % 2], 16 * (self.b0 + b // 2 + 1))
                        sp.dma_start(Oden[b % 2], d_rec[self.a, b].unsqueeze(1).to_broadcast([8, HD, T])).then_inc(
                            self.rloaded[b % 2], 16)

                return task


        class MLP:

            def __init__(self, l, before, xready, norm0, b1, func, bias_row, after, t_free):
                self.l, self.before, self.xready, self.norm0 = l, before, xready, norm0
                self.b1, self.func, self.bias_row, self.after, self.t_free = b1, func, bias_row, after, t_free
                n = f"m{l}_"
                self.t_full, self.t_out = sem(n + "t_full"), sem(n + "t_out")
                self.h_full, self.h_free = sem(n + "h_full"), sem(n + "h_free")
                self.w2, self.acc_free, self.xd = sem(n + "w2"), sem(n + "acc_free"), sem(n + "x_done")

            def t_bank(self, b, half):
                return bank((6 if b or self.l == 1 else 2) + half)

            def pe_transposes(self, pe, b):
                pe.wait_ge(ln_done, self.norm0 + b + 1)
                for s_, n in self.t_free(b):
                    pe.wait_ge(s_, n)
                if b:
                    pe.wait_ge(self.t_out, 2 * b)
                for half in range(2):
                    turn(pe, self.t_bank(b, half), half).then_inc(self.t_full, 1)

            def pe(self, pe, fill, lead):
                for s_, n in self.before:
                    pe.wait_ge(s_, n)
                if self.l != 1:
                    self.pe_transposes(pe, 0)
                pe.wait_ge(ld_mlp[self.l], 32)
                for b in range(B):
                    pe.wait_ge(self.t_out, 2 * b + 2)
                    for m in range(FM):
                        q = FM * b + m
                        if q >= 2:
                            pe.wait_ge(self.h_free, q - 1)
                        for k in range(DH):
                            ins = pe.matmul(bank(4 + q % 2), W1[:, k, m * P:(m + 1) * P], XN[:, b % 2, k, :],
                                            start=(k == 0), stop=(k == 1))
                        ins.then_inc(self.h_full, 1)
                        if m == 3 and b:
                            fill(1, b - 1)
                    if b + 1 < B:
                        self.pe_transposes(pe, b + 1)
                    if b:
                        pe.wait_ge(self.acc_free, b)
                    else:
                        pe.wait_ge(self.t_out, 2)
                    for m in range(FM):
                        if b == B - 1:
                            for task in lead[len(lead) * m // FM:len(lead) * (m + 1) // FM]:
                                task()
                        pe.wait_ge(self.h_free, FM * b + m + 1)
                        for t in range(TT):
                            ins = pe.matmul(bank(t, D), H[:, m, t * P:(t + 1) * P], W2[:, m, :],
                                            start=(m == 0), stop=(m == FM - 1))
                    ins.then_inc(self.w2, 1)
                    if b + 1 < B:
                        fill(0, b)

            def act(self, act, fill, lead):
                for b in range(B):
                    for m in range(FM):
                        act.wait_ge(self.h_full, FM * b + m + 1)
                        if m == 0 and b:
                            act.wait_ge(self.w2, b)
                        bias = column(self.b1, m) if self.b1 else 0.0
                        nc.scalar.activation(H[:, m, :], bank(4 + (FM * b + m) % 2), self.func,
                                             bias=bias).then_inc(self.h_free, 1)
                    fill(b)
                for task in lead:
                    task()

            def dve_norm(self, v, link, b):
                s_, n = self.xready
                norm_stats(v, link, self.norm0 + b, b, [(s_, n * (b + 1))])
                norm_apply(v, self.norm0 + b, b, [(self.t_full, 2 * b)] if b else
                           [(s5.t_full, 2 * B)] if self.l == 1 else [])

            def dve_modulate(self, v, b):
                if b >= 2:
                    v.wait_ge(self.h_full, FM * (b - 1))
                m = 2 * self.l + 1
                for half in range(2):
                    v.wait_ge(self.t_full, 2 * b + half + 1)
                    v.tensor_scalar(XN[:, b % 2, half, :], self.t_bank(b, half), mod[:, m, 1, half, b:b + 1],
                                    mod[:, m, 0, half, b:b + 1], ALU.mult, ALU.add).then_inc(self.t_out, 1)

            def dve(self, v, link, side, fill, lead):
                if self.l != 1:
                    self.dve_modulate(v, 0)
                for b in range(B):
                    if b + 1 < B:
                        self.dve_norm(v, link, b + 1)
                        if b == 0 and self.l != 1:
                            for t in self.after.tail():
                                if t[0] == "RCP":
                                    self.after.dve_task(v, link)(*t)
                        self.dve_modulate(v, b + 1)
                        side(b)
                    else:
                        for task in lead:
                            task()
                    v.wait_ge(self.w2, b + 1)
                    if b:
                        v.wait_ge(self.xd, b)
                    if b == 0:
                        v.wait_ge(self.after.xd, B if self.l == 1 else 2 * (B - 1))
                    if b == 1 and self.l != 1:
                        v.wait_ge(self.after.xd, 2 * B)
                    v.tensor_tensor(tsc[:, :, :], PS[:, 0:TT, 0:D],
                                    gates[:, self.l % 2, 1, b:b + 1, :].to_broadcast([P, TT, D]),
                                    ALU.mult).then_inc(self.acc_free, 1)
                    if b == 0 and self.l != 1:
                        for t in self.after.tail():
                            if t[0] == "PJ":
                                self.after.dve_task(v, link)(*t)
                    if b + 1 < B:
                        fill(b)

            def pool(self, pool, link, fill, lead):
                for b in range(B):
                    if b + 1 < B:
                        norm_rstd(pool, link, self.norm0 + b + 1)
                        fill(b)
                    else:
                        for task in lead:
                            task()
                    if b == 0 and self.l != 1:
                        for t in self.after.tail():
                            if t[0] == "NORM":
                                self.after.pool_task(pool, link)(*t)
                    if self.bias_row is not None:
                        link(pool.tensor_tensor(gate_bias[:, :], gates[:, self.l % 2, 1, b, :],
                                                bias_bc[:, self.bias_row, :], ALU.mult))
                        pool.wait_ge(ln_done, self.norm0 + b + 1)
                        for t in range(TT):
                            ins = pool.tensor_tensor(x[:, TT * b + t, :], x[:, TT * b + t, :], gate_bias[:, :], ALU.add)
                        link(ins)
                    pool.wait_ge(self.acc_free, b + 1)
                    pool.tensor_tensor(batch(b), batch(b), tsc[:, :, :], ALU.add).then_inc(self.xd, 1)
                    if b == 0 and self.l != 1:
                        for t in self.after.tail():
                            if t[0] == "PJ":
                                self.after.pool_task(pool, link)(*t)

        class S5:
            def __init__(self, before, xready, norm0):
                self.before, self.xready, self.norm0 = before, xready, norm0
                self.t_full, self.t_out = sem("s_t_full"), sem("s_t_out")
                self.bu_full, self.bu_free = sem("s_bu_full"), sem("s_bu_free")
                self.scan, self.yprod = sem("s_scan"), sem("s_yprod")
                self.c_full, self.acc_free, self.xd = sem("s_c_full"), sem("s_acc_free"), sem("s_x_done")

            def pe(self, pe):
                for s_, n in self.before:
                    pe.wait_ge(s_, n)

                def inputs(b):
                    if b:
                        self.pe_transposes(pe, b)
                    pe.wait_ge(self.t_out, 2 * b + 2)
                    if b:
                        pe.wait_ge(self.bu_free, b)
                    for a in range(2):
                        for k in range(DH):
                            ins = pe.matmul(bank(4 + a), BT[:, a, k, :], XS[b % 2][:, k, :],
                                            start=(k == 0), stop=(k == 1))
                    ins.then_inc(self.bu_full, 1)

                def outputs(b):
                    pe.wait_ge(self.yprod, b + 1)
                    if b:
                        pe.wait_ge(self.acc_free, b)
                    for t in range(TT):
                        c = slice(t * P, (t + 1) * P)
                        for k in range(DH):
                            pe.matmul(PS[:, t, k * P:(k + 1) * P], XS[b % 2][:, k, c], diagD[:, k, :],
                                      start=(k == 0), stop=False, skip_group_check=True)
                        for a in range(2):
                            ins = pe.matmul(bank(t, D), ysc[b % 2][a][:, c], CT[:, a, :],
                                            start=False, stop=(a == 1), skip_group_check=True)
                    ins.then_inc(self.c_full, 1)

                for b in range(B):
                    inputs(b)
                    if b:
                        outputs(b - 1)
                mlp1.pe_transposes(pe, 0)
                outputs(B - 1)

            def pe_transposes(self, pe, b):
                pe.wait_ge(ln_done, self.norm0 + b + 1)
                if b:
                    pe.wait_ge(self.t_out, 2 * b)
                for half in range(2):
                    turn(pe, bank(6 + half), half).then_inc(self.t_full, 1)

            def dve_norm(self, v, link, b):
                    s_, n = self.xready
                    norm_stats(v, link, self.norm0 + b, b, [(s_, n * (b + 1))])
                    norm_apply(v, self.norm0 + b, b, [(self.t_full, 2 * b)] if b else [(mlp0.t_full, 2 * B)])
                    if b >= 2:
                        v.wait_ge(self.c_full, b - 1)
                    for half in range(2):
                        v.wait_ge(self.t_full, 2 * b + half + 1)
                        v.tensor_scalar(XS[b % 2][:, half, :], bank(6 + half), mod[:, 2, 1, half, b:b + 1],
                                        mod[:, 2, 0, half, b:b + 1], ALU.mult, ALU.add).then_inc(self.t_out, 1)

            def dve(self, v, link):
                def result(b):
                    v.wait_ge(self.c_full, b + 1)
                    if b == 0:
                        v.wait_ge(ld_gate[1], 16)
                        v.wait_ge(mlp0.xd, B)
                    else:
                        v.wait_ge(self.xd, b)
                    v.tensor_tensor(tsc[:, :, :], PS[:, 0:TT, 0:D],
                                    gates[:, 1, 0, b:b + 1, :].to_broadcast([P, TT, D]),
                                    ALU.mult).then_inc(self.acc_free, 1)

                for b in range(B):
                    if b + 1 < B:
                        self.dve_norm(v, link, b + 1)
                    v.wait_ge(self.bu_full, b + 1)
                    if b:
                        v.wait_ge(self.scan, b)
                    v.tensor_tensor(bu[0], bank(4), CC, ALU.mult)
                    ins = v.tensor_tensor(bu[1], bank(5), SS, ALU.mult)
                    ins.then_inc(self.bu_free, 1)
                    v.wait_ge(self.bu_free, b + 1)
                    link(v.tensor_tensor(bu[0], bu[0], bu[1], ALU.add))
                    if b >= 2:
                        v.wait_ge(self.yprod, b - 1)
                    v.tensor_tensor_scan(yst[b % 2], RR, bu[0], 0.0, ALU.mult, ALU.add).then_inc(self.scan, 1)
                    if b:
                        result(b - 1)
                mlp1.dve_norm(v, link, 0)
                mlp1.dve_modulate(v, 0)
                result(B - 1)

            def pool(self, pool, link):
                def add(b):
                    pool.wait_ge(self.acc_free, b + 1)
                    pool.tensor_tensor(batch(b), batch(b), tsc[:, :, :], ALU.add).then_inc(self.xd, 1)

                for b in range(B):
                    if b + 1 < B:
                        norm_rstd(pool, link, self.norm0 + b + 1)
                    pool.wait_ge(self.scan, b + 1)
                    if b >= 2:
                        pool.wait_ge(self.c_full, b - 1)
                    pool.tensor_tensor(ysc[b % 2][0], yst[b % 2], CC, ALU.mult)
                    pool.tensor_tensor(ysc[b % 2][1], yst[b % 2], SS, ALU.mult).then_inc(self.yprod, 1)
                    if b:
                        add(b - 1)
                norm_rstd(pool, link, mlp1.norm0)
                add(B - 1)

        def c_(i):
            return sv[:, i:i + 1]

        (DT, KN, RD, EA, TH, VV, SN, CM, TMP, RAD, CO, NR, NI, FR, FI, SFI, NSFR, DEN, ANG_C, ANG_S, T2, M2SG,
         TWO_N) = range(23)

        def s5_decay(v, link):
            v.wait_ge(ld_s5, 16 * 8)
            re, im, ls, sg = (lam[:, i:i + 1] for i in range(4))

            def ts(o, a, s1, s2, op0, op1=ALU.bypass):
                link(v.tensor_scalar(c_(o), a, s1, s2, op0, op1) if s2 is not None else
                     v.tensor_scalar(c_(o), a, s1, None, op0))

            def stt(o, a, s_, b_, op0, op1):
                link(v.scalar_tensor_tensor(out=c_(o), in0=a, scalar=s_, in1=b_, op0=op0, op1=op1))

            ts(KN, ls, LOG2E, None, ALU.mult)
            ts(KN, c_(KN), ROUND, None, ALU.add)
            ts(KN, c_(KN), -ROUND, None, ALU.add)
            stt(RD, c_(KN), -LN2_HI, ls, ALU.mult, ALU.add)
            stt(RD, c_(KN), -LN2_LO, c_(RD), ALU.mult, ALU.add)
            ts(DT, c_(RD), 1.0 / 5040, 1.0 / 720, ALU.mult, ALU.add)
            for q in (1.0 / 120, 1.0 / 24, 1.0 / 6, 0.5, 1.0, 1.0):
                ts(DT, c_(DT), c_(RD), q, ALU.mult, ALU.add)
            link(v.tensor_scalar(lam_i[:, :], c_(KN), 127.0, 8388608.0, ALU.add, ALU.mult))
            stt(DT, c_(DT), 1.0, lam_i[:, :].bitcast(F32), ALU.mult, ALU.mult)
            ts(TMP, re, c_(DT), 1.0 / 64, ALU.mult, ALU.mult)
            ts(EA, c_(TMP), 1.0 / 40320, 1.0 / 5040, ALU.mult, ALU.add)
            for q in (1.0 / 720, 1.0 / 120, 1.0 / 24, 1.0 / 6, 0.5, 1.0):
                ts(EA, c_(EA), c_(TMP), q, ALU.mult, ALU.add)
            ts(EA, c_(EA), c_(TMP), None, ALU.mult)
            for _ in range(6):
                stt(EA, c_(EA), 2.0, c_(EA), ALU.add, ALU.mult)
            ts(RAD, c_(EA), 1.0, None, ALU.add)

        def s5_angles(v, link):
            re, im, ls, sg = (lam[:, i:i + 1] for i in range(4))

            def ts(o, a, s1, s2, op0, op1=ALU.bypass):
                link(v.tensor_scalar(c_(o), a, s1, s2, op0, op1) if s2 is not None else
                     v.tensor_scalar(c_(o), a, s1, None, op0))

            def stt(o, a, s_, b_, op0, op1):
                link(v.scalar_tensor_tensor(out=c_(o), in0=a, scalar=s_, in1=b_, op0=op0, op1=op1))

            ts(TH, im, c_(DT), None, ALU.mult)
            ts(KN, c_(TH), 0.15915494309189535, None, ALU.mult)
            ts(KN, c_(KN), ROUND, None, ALU.add)
            ts(KN, c_(KN), -ROUND, None, ALU.add)
            for q in (TWO_PI_A, TWO_PI_B, TWO_PI_C):
                stt(TH, c_(KN), -q, c_(TH), ALU.mult, ALU.add)
            ts(TH, c_(TH), 0.125, None, ALU.mult)
            ts(VV, c_(TH), c_(TH), None, ALU.mult)
            ts(SN, c_(VV), 1.0 / 362880, -1.0 / 5040, ALU.mult, ALU.add)
            for q in (1.0 / 120, -1.0 / 6, 1.0):
                ts(SN, c_(SN), c_(VV), q, ALU.mult, ALU.add)
            ts(SN, c_(SN), c_(TH), None, ALU.mult)
            ts(CM, c_(VV), 1.0 / 40320, -1.0 / 720, ALU.mult, ALU.add)
            for q in (1.0 / 24, -0.5):
                ts(CM, c_(CM), c_(VV), q, ALU.mult, ALU.add)
            ts(CM, c_(CM), c_(VV), None, ALU.mult)
            for _ in range(3):
                ts(TMP, c_(CM), 1.0, 2.0, ALU.add, ALU.mult)
                ts(T2, c_(SN), c_(TMP), None, ALU.mult)
                ts(CM, c_(SN), c_(SN), -2.0, ALU.mult, ALU.mult)
                ts(SN, c_(T2), 1.0, None, ALU.mult)
            ts(CO, c_(CM), 1.0, None, ALU.add)
            stt(NR, c_(EA), c_(CO), c_(CM), ALU.mult, ALU.add)
            ts(NI, c_(RAD), c_(SN), None, ALU.mult)
            ts(DEN, re, re, None, ALU.mult)
            stt(DEN, im, im, c_(DEN), ALU.mult, ALU.add)
            link(v.reciprocal(c_(DEN), c_(DEN)))
            ts(FR, c_(NI), im, None, ALU.mult)
            stt(FR, c_(NR), re, c_(FR), ALU.mult, ALU.add)
            ts(FR, c_(FR), c_(DEN), None, ALU.mult)
            ts(FI, c_(NR), im, None, ALU.mult)
            stt(FI, c_(NI), re, c_(FI), ALU.mult, ALU.subtract)
            ts(FI, c_(FI), c_(DEN), None, ALU.mult)
            ts(SFI, c_(FI), sg, None, ALU.mult)
            ts(NSFR, c_(FR), sg, -1.0, ALU.mult, ALU.mult)
            ts(M2SG, sg, -2.0, None, ALU.mult)

        def s5_tables(v, link):
            v.wait_ge(ld_bc, 16 * 12)
            link(v.memset(CC[:, 0:1], 1.0))
            link(v.memset(SS[:, 0:1], 0.0))
            link(v.memset(RR, 1.0))
            link(v.tensor_scalar(RR, RR, c_(RAD), None, ALU.mult))
            link(v.tensor_copy(c_(ANG_C), c_(CO)))
            link(v.tensor_copy(c_(ANG_S), c_(SN)))
            n = 1
            while n < T:
                link(v.tensor_scalar(s5t[:, 0:n], SS[:, 0:n], c_(ANG_S), -1.0, ALU.mult, ALU.mult))
                link(v.scalar_tensor_tensor(out=CC[:, n:2 * n], in0=CC[:, 0:n], scalar=c_(ANG_C), in1=s5t[:, 0:n],
                                            op0=ALU.mult, op1=ALU.add))
                link(v.tensor_scalar(s5t[:, 0:n], SS[:, 0:n], c_(ANG_C), None, ALU.mult))
                link(v.scalar_tensor_tensor(out=SS[:, n:2 * n], in0=CC[:, 0:n], scalar=c_(ANG_S), in1=s5t[:, 0:n],
                                            op0=ALU.mult, op1=ALU.add))
                link(v.tensor_scalar(c_(TMP), c_(ANG_S), c_(ANG_S), -1.0, ALU.mult, ALU.mult))
                link(v.tensor_scalar(c_(T2), c_(ANG_S), c_(ANG_C), 2.0, ALU.mult, ALU.mult))
                link(v.scalar_tensor_tensor(out=c_(ANG_C), in0=c_(ANG_C), scalar=c_(ANG_C), in1=c_(TMP),
                                            op0=ALU.mult, op1=ALU.add))
                link(v.tensor_copy(c_(ANG_S), c_(T2)))
                n *= 2
            for a, (p_, q_) in enumerate(((FR, SFI), (FI, NSFR))):
                link(v.tensor_scalar(s5t[:, 0:D], s5B[:, 1, :], c_(q_), None, ALU.mult))
                link(v.scalar_tensor_tensor(out=s5W[:, a, :], in0=s5B[:, 0, :], scalar=c_(p_), in1=s5t[:, 0:D],
                                            op0=ALU.mult, op1=ALU.add))
            for k in range(DH):
                ins = v.tensor_scalar(diagD[:, k, :], ident[:, :], column("Dd", k), None, ALU.mult)
            ins.then_inc(s5_pre, 1)

        def setup_pe(pe):
            pe.wait_ge(ld_cond, 16)
            pe.wait_ge(ld_const, 16)
            pe.transpose(PS[:, 5, 0:8], rows[0:8, :], ident[0:8, 0:8]).then_inc(row_tr, 1)
            mod_rows(pe, 0, Wm0, cs, 3, [(silu_ready, 1), (ld_wm0, 16)])
            pe.wait_ge(ld_rows, 16 * 12)
            pe.transpose(PS[:, 4, 0:NROWS], rows[:, :], ident[0:NROWS, 0:NROWS]).then_inc(row_tr, 1)
            mod_turn(pe, 0, 3)
            pe.wait_ge(mod_ready, 1)

        def setup_act(act):
            act.wait_ge(cols_ready, 1)
            nc.scalar.activation(csig[:, :], col[:, 0:8], ACT.Exp, scale=-1.0).then_inc(silu_e, 1)

        def setup_dve(v, link):
            v.memset(cs[:, :, :], 0.0)
            v.memset(cc[:, :, :], 0.0)
            v.memset(lnc[:, :, :], 0.0)
            v.memset(h3[:, :, :], 0.0)
            link(v.memset(czero[:, :], 0.0))
            v.memset(mhalf[:, :], -0.5).then_inc(consts_set, 1)
            v.wait_ge(row_tr, 1)
            v.tensor_copy(col[:, 0:8], PS[:, 5, 0:8]).then_inc(cols_ready, 1)
            v.wait_ge(silu_e, 1)
            link(v.tensor_scalar(csig[:, :], csig[:, :], 1.0, None, ALU.add))
            link(v.reciprocal(csig[:, :], csig[:, :]))
            cond = col[:, 0:8].rearrange("p (b k) -> p k b", k=2)
            v.tensor_tensor(cs[:, :, 0:B], cond, csig[:, :].rearrange("p (b k) -> p k b", k=2), ALU.mult)
            v.tensor_copy(cc[:, :, 0:B], cond).then_inc(silu_ready, 1)
            v.wait_ge(row_tr, 2)
            v.tensor_copy(col[:, 8:NROWS], PS[:, 4, 8:NROWS]).then_inc(cols_ready, 1)
            v.wait_ge(cols_ready, 2)
            link(v.tensor_scalar(bq16[:, :], col[:, ROWS["L0_bq"][0]:ROWS["L0_bq"][0] + 2], 1.0 / HD, None, ALU.mult))

        def mod_simple(v, link, i, m, s_shift, s_scale, g=None, b_=None):
            for half in range(2):
                sh, sc = mod[:, m, 0, half, :], mod[:, m, 1, half, :]
                link(v.tensor_scalar(sc, section(i, s_scale, half), 1.0, None, ALU.add))
                if g is None:
                    link(v.tensor_copy(sh, section(i, s_shift, half)))
                else:
                    link(v.scalar_tensor_tensor(out=sh, in0=sc, scalar=column(b_, half),
                                                in1=section(i, s_shift, half), op0=ALU.mult, op1=ALU.add))
                    link(v.tensor_scalar(sc, sc, column(g, half), None, ALU.mult))

        SETS = ((1, Wm1, cc, 3), (2, Wc1, cc, 1), (3, Wm2, cs, 3))

        def tail_pe(pe, att, mlp):
            pe.wait_ge(mlp.t_out, 4)
            for t in att.tail():
                att.pe_task(pe)(*t)

        def fill0_pe(pe, slot, b):
            i, W, C, nchunk = SETS[b]
            if slot == 0:
                if b == 0:
                    tail_pe(pe, att0, mlp0)
                pe.wait_ge(mlp0.t_out, 2 * b + 4)
                mod_rows(pe, i, W, C, nchunk, [(ld_mid, 16 * 4)])
            else:
                if b == 0:
                    pe.wait_ge(att0.m_free, PJ0)
                mod_turn(pe, i, nchunk)

        def fill0_dve(v, link, b):
            i, W, C, nchunk = SETS[b]
            mod_evac(v, i, nchunk, [(gate_saved, 32 * (1, 2, 2)[b])])
            v.wait_ge(mod_ready, i + 1)
            if i == 1:
                mod_simple(v, link, 1, 2, SHIFT, SCALE)
                for half in range(2):
                    link(v.tensor_scalar(modf[:, 0, half, :], section(1, SCALE2, half), 1.0, None, ALU.add))
                    link(v.tensor_copy(modf[:, 1, half, :], section(1, SHIFT2, half)))
            elif i == 2:
                for half in range(2):
                    sh, sc, sf = mod[:, 3, 0, half, :], mod[:, 3, 1, half, :], modf[:, 0, half, :]
                    link(v.tensor_scalar(sc, section(2, 0, half), 1.0, None, ALU.add))
                    link(v.tensor_tensor(sc, sc, sf, ALU.mult))
                    link(v.tensor_tensor(sh, section(2, 1, half), sf, ALU.mult))
                    link(v.tensor_tensor(sh, sh, modf[:, 1, half, :], ALU.add))
            else:
                mod_simple(v, link, 3, 4, SHIFT, SCALE, "n1g", "n1b")
                mod_simple(v, link, 3, 5, SHIFT2, SCALE2, "n2g", "n2b")

        def s5_matrices_pe(pe):
            pe.wait_ge(s5_pre, 1)
            pe.wait_ge(mlp0.h_free, FM * B)
            for a in range(2):
                for k in range(DH):
                    pe.transpose(PS[:, 4, (2 * a + k) * P:(2 * a + k + 1) * P], s5W[:, a, k * P:(k + 1) * P], ident[:, :])
                    ins = pe.transpose(PS[:, 5, (2 * a + k) * P:(2 * a + k + 1) * P], s5C[:, a, k, :], ident[:, :])
            ins.then_inc(s5_tr, 1)

        def s5_matrices_dve(v):
            v.wait_ge(s5_tr, 1)
            v.tensor_copy(BT, bank(4).rearrange("p (a k n) -> p a k n", a=2, k=2))
            v.tensor_scalar(CT[:, 0, :], PS[:, 5, 0:D], c_(M2SG), None, ALU.mult)
            v.tensor_scalar(CT[:, 1, :], PS[:, 5, D:2 * D], -2.0, None, ALU.mult).then_inc(s5_ready, 1)

        def adapter_rows(pe, r):
            pe.wait_ge(l3_hg, 2)
            pe.wait_ge(ld_ring[r], 16 * 4)
            if r:
                pe.wait_ge(l3_wr, 1)
            for c in range(2):
                for k in range(DH):
                    for j in range(4):
                        ins = pe.matmul(PS[32 * j:32 * j + 32, 6 + c, :], h3[:, k, :],
                                        ring[j][:, k, 512 * c:512 * (c + 1)], start=(k == 0), stop=(k == 1))
            ins.then_inc(l3_w, 1)

        def fill1_pe(pe, slot, b):
            pe.wait_ge(mlp1.t_out, 2 * b + 4)
            if (slot, b) == (0, 0):
                pe.wait_ge(l3_ready, 1)
                for k in range(DH):
                    ins = pe.transpose(PS[:, 6, k * 32:k * 32 + B], c4[:, k * P:(k + 1) * P], ident[0:B, 0:B])
                ins.then_inc(l3_tr, 1)
            elif (slot, b) == (1, 0):
                pe.wait_ge(l3_ready, 2)
                for m in range(2):
                    for k in range(DH):
                        ins = pe.matmul(PS[:, 7, m * 32:m * 32 + B], WL3[:, k, m * P:(m + 1) * P], lnc[:, k, 0:B],
                                        start=(k == 0), stop=(k == 1))
                ins.then_inc(l3_h, 1)
            elif (slot, b) == (1, 1):
                adapter_rows(pe, 0)
            elif (slot, b) == (0, 2):
                adapter_rows(pe, 1)

        def fill1_act(act, b):
            if b == 1:
                for m in range(2):
                    act.wait_ge(l3_h, 1)
                    nc.scalar.activation(h3[:, m, 0:B], PS[:, 7, m * 32:m * 32 + B], ACT.Gelu,
                                         bias=column("L3_b1", m)).then_inc(l3_hg, 1)

        def cond_norm(v, link):
            link(v.bn_stats(c4s[:, 0:6], c4[:, :]))
            link(v.bn_aggr(c4s[:, 6:8], c4s[:, 0:6]))
            v.tensor_scalar(c4s[:, 0:1], c4s[:, 7:8], EPS, None, ALU.add).then_inc(l3_bt, 1)
            v.wait_ge(l3_bt, 2)
            v.tensor_scalar(c4[:, :], c4[:, :], c4s[:, 6:7], c4s[:, 1:2], ALU.subtract, ALU.mult).then_inc(l3_ready, 1)

        def fill1_dve(v, link, b):
            if b == 0:
                v.wait_ge(l3_tr, 1)
                for k in range(DH):
                    ins = v.tensor_scalar(lnc[:, k, 0:B], PS[:, 6, k * 32:k * 32 + B], column("lng", k),
                                          column("lnb", k), ALU.mult, ALU.add)
                ins.then_inc(l3_ready, 1)
            else:
                r = b - 1
                v.wait_ge(l3_w, r + 1)
                v.wait_ge(ld_b2[r], 16 * 4)
                v.tensor_tensor(wrow[r], PS[:, 6:8, :].rearrange("p a b -> p (a b)"), b2row[r],
                                ALU.add).then_inc(l3_wr, 1)

        def cond_norm_pool(pool, link):
            pool.wait_ge(l3_bt, 1)
            link(pool.tensor_tensor(c4s[:, 1:2], c4s[:, 0:1], mhalf[0:B, 0:1], ALU.pow))
            link(pool.tensor_tensor(c4s[:, 2:3], c4s[:, 1:2], c4s[:, 1:2], ALU.mult))
            link(pool.tensor_tensor(c4s[:, 2:3], c4s[:, 2:3], c4s[:, 0:1], ALU.mult))
            link(pool.tensor_scalar(c4s[:, 2:3], c4s[:, 2:3], -0.5, 1.5, ALU.mult, ALU.add))
            pool.tensor_tensor(c4s[:, 1:2], c4s[:, 1:2], c4s[:, 2:3], ALU.mult).then_inc(l3_bt, 1)

        def nothing(*_):
            pass

        f_bt, f_btr, f_t, f_to = sem("f_bt"), sem("f_btr"), sem("f_t"), sem("f_to")
        f_z, f_zo, f_y, f_yo, f_z2, f_z2o, f_o, f_oo = (sem("f_" + n) for n in (
            "z", "zo", "y", "yo", "z2", "z2o", "o", "oo"))

        class Low:

            def __init__(self, before, xready):
                self.before, self.xready = before, xready

            def pe(self, pe):
                for s_, n in self.before:
                    pe.wait_ge(s_, n)
                pe.wait_ge(ld_low, 64)
                for w in range(2):
                    for b in range(B):
                        for h in range(DH):
                            q = (w * B + b) * DH + h
                            ins = pe.transpose(PS[0:RANK, q // 4, (q % 4) * P:(q % 4 + 1) * P],
                                               raw_a1[:, 1 + 2 * w, b, h, :], ident[:, :])
                ins.then_inc(f_bt, 1)
                for b in range(B):
                    pe.wait_ge(self.xready[0], self.xready[1] * (b + 1))
                    if b:
                        pe.wait_ge(f_to, 2 * b)
                    for half in range(2):
                        turn(pe, bank(6 + half), half,
                             lambda t: x[:, TT * b + t, half * P:(half + 1) * P]).then_inc(f_t, 1)
                for b in range(B):
                    pe.wait_ge(f_to, 2 * b + 2)
                    if b >= 2:
                        pe.wait_ge(f_zo, b - 1)
                    for k in range(DH):
                        ins = pe.matmul(PS[0:RANK, 4 + b % 2, :], raw_a1[:, 0, b, k, :], xT[b][:, k, :],
                                        start=(k == 0), stop=(k == 1))
                    ins.then_inc(f_z, 1)
                pe.wait_ge(f_btr, 4)
                for b in range(B):
                    pe.wait_ge(f_zo, b + 1)
                    for h in range(DH):
                        q = 2 * b + h
                        if q >= 4:
                            pe.wait_ge(f_yo, q - 3)
                        pe.matmul(bank(q % 4), btr[0:RANK, 0, b, h * P:(h + 1) * P], z1[b][0:RANK, :],
                                  start=True, stop=True).then_inc(f_y, 1)
                for b in range(B):
                    pe.wait_ge(f_yo, 2 * b + 2)
                    if b < 2:
                        pe.wait_ge(f_zo, 3 + b)
                    else:
                        pe.wait_ge(f_z2o, b - 1)
                    for k in range(DH):
                        ins = pe.matmul(PS[0:RANK, 4 + b % 2, :], raw_a1[:, 2, b, k, :], gT[b][:, k, :],
                                        start=(k == 0), stop=(k == 1))
                    ins.then_inc(f_z2, 1)
                for b in range(B):
                    pe.wait_ge(f_z2o, b + 1)
                    pe.wait_ge(f_yo, 2 * B)
                    if b:
                        pe.wait_ge(f_oo, b)
                    for t in range(TT):
                        ins = pe.matmul(bank(t, D), z2[b][0:RANK, t * P:(t + 1) * P], btr[0:RANK, 1, b, :],
                                        start=True, stop=True)
                    ins.then_inc(f_o, 1)

            def act(self, act):
                for b in range(B):
                    for h in range(DH):
                        q = 2 * b + h
                        act.wait_ge(f_y, q + 1)
                        nc.scalar.activation(gT[b][:, h, :], bank(q % 4), ACT.Gelu).then_inc(f_yo, 1)

            def dve(self, v, link):
                v.wait_ge(f_bt, 1)
                for w in range(2):
                    for c in range(2):
                        v.tensor_copy(btr[0:RANK, w, 2 * c:2 * c + 2, :], PS[0:RANK, 2 * w + c, :].rearrange(
                            "p (b d) -> p b d", b=2)).then_inc(f_btr, 1)
                for b in range(B):
                    for half in range(2):
                        v.wait_ge(f_t, 2 * b + half + 1)
                        v.tensor_copy(xT[b][:, half, :], bank(6 + half)).then_inc(f_to, 1)
                for b in range(B):
                    v.wait_ge(f_z, b + 1)
                    v.tensor_copy(z1[b][0:RANK, :], PS[0:RANK, 4 + b % 2, :]).then_inc(f_zo, 1)
                for b in range(B):
                    v.wait_ge(f_z2, b + 1)
                    v.tensor_copy(z2[b][0:RANK, :], PS[0:RANK, 4 + b % 2, :]).then_inc(f_z2o, 1)
                for b in range(B):
                    v.wait_ge(f_o, b + 1)
                    v.tensor_tensor(batch(b), batch(b), PS[:, 0:TT, 0:D], ALU.add).then_inc(f_oo, 1)

            def sync(self, sp):
                for b in range(B):
                    sp.wait_ge(f_oo, b + 1)
                    sp.dma_start(out[b].rearrange("(t p) d -> p t d", p=P), batch(b)).then_inc(out_done, 16)
                sp.wait_ge(out_done, 16 * B)

        PJ0, PJ1 = (len([k for k in misc if k[0] == a]) for a in range(2))
        att0 = Attention(0, [])
        mlp0 = MLP(0, [(att0.st_read, NSTEP)], (att0.xd, 2), 4, "L0_b1", ACT.Gelu, 2, att0, lambda b: [
            [(att0.sm_free, 8 * NG)], [(att0.o_free, NG), (att0.m_free, att0.idx("PJ", B - 1, 0))],
            [(att0.m_free, PJ0), (mod_ready, 2)], [(mod_ready, 3)]][b])
        s5 = S5([(s5_ready, 1), (mlp0.acc_free, B)], (mlp0.xd, 1), 8)
        mlp1 = MLP(1, [(s5.acc_free, B), (s5.bu_free, B)], (s5.xd, 1), 12, "L1_b1", ACT.Gelu_apprx_tanh, 3, s5,
                   lambda b: [[(s5.t_out, 2 * B)], [], [(l3_ready, 2), (l3_hg, 2)], [(l3_wr, 1)]][b])
        att1 = Attention(1, [(mlp1.acc_free, B), (mlp1.h_free, FM * B)])
        mlp2 = MLP(2, [(att1.st_read, NSTEP)], (att1.xd, 2), 20, None, ACT.Gelu, None, att1, lambda b: [
            [(att1.sm_free, 8 * NG)], [(att1.o_free, NG), (att1.m_free, att1.idx("PJ", B - 1, 0))],
            [(att1.m_free, PJ1)], []][b])
        low = Low([(mlp2.t_out, 2 * B), (mlp2.acc_free, B), (mlp2.h_free, FM * B)], (mlp2.xd, 1))
        att0.mlp, att1.mlp = mlp0, mlp2

        def calls(task, tasks):
            return [lambda t=t: task(*t) for t in tasks]

        block = ctx.enter_context(nc.Block())

        @block.tensor
        def _(pe):
            setup_pe(pe)
            for t in att0.lead():
                att0.pe_task(pe)(*t)
            att0.pe(pe)

            def s5_first():
                pe.wait_ge(mod_ready, 4)
                s5.pe_transposes(pe, 0)

            mlp0.pe(pe, lambda slot, b: fill0_pe(pe, slot, b), [s5_first, lambda: s5_matrices_pe(pe)])
            s5.pe(pe)

            def att1_first():
                pe.wait_ge(l3_wr, 2)
                pe.wait_ge(mlp1.t_out, 2 * B)

            mlp1.pe(pe, lambda slot, b: fill1_pe(pe, slot, b),
                    [att1_first] + calls(att1.pe_task(pe), [t for t in att1.lead() if t[0] in MISC_KINDS]))
            att1.pe(pe)
            mlp2.pe(pe, lambda slot, b: tail_pe(pe, att1, mlp2) if (slot, b) == (0, 0) else None, [])
            low.pe(pe)

        @block.scalar
        def _(act):
            act.dma_start(batch(0), A["x"][0].rearrange("(t p) d -> p t d", p=P)).then_inc(ld_x[0], 16)
            for k, name in enumerate(("L0_cond_Wq", "L0_cond_Wk", "L0_cond_Wv", "L0_cond_Wo")):
                act.dma_start(WA[:, k], view(A[name])).then_inc(ld_wa, 16)
            for k, name in enumerate(("L0_cond_bv", "L0_cond_bo", "L0_cond_b2", "L1_cond_b2")):
                act.dma_start(bias_bc[:, k, :], A[name].partition_broadcast(P)).then_inc(ld_bias, 16)
            setup_act(act)
            act.wait_ge(cols_ready, 2)
            act.wait_ge(mods_set, 1)
            for t in att0.lead():
                att0.act_task(act)(*t)
            att0.act(act)
            mlp0.act(act, nothing, [])
            mlp1.act(act, lambda b: fill1_act(act, b), calls(att1.act_task(act), att1.lead()))
            att1.act(act)
            mlp2.act(act, nothing, [])
            low.act(act)

        @block.vector
        def _(v):
            link = Chain(v, dve_c)
            setup_dve(v, link)
            lead = att0.lead()
            for t in lead[:2]:
                att0.dve_task(v, link)(*t)
            mod_evac(v, 0, 3, [])
            v.wait_ge(mod_ready, 1)
            mod_simple(v, link, 0, 0, SHIFT, SCALE)
            mod_simple(v, link, 0, 1, SHIFT2, SCALE2)
            v.tensor_copy(czero2[:, :], czero[:, :]).then_inc(mods_set, 1)
            for t in lead[2:]:
                att0.dve_task(v, link)(*t)
            att0.dve(v, link)

            def s5_side(b):
                (s5_decay, s5_angles, s5_tables)[b](v, link)

            mlp0.dve(v, link, s5_side, lambda b: fill0_dve(v, link, b),
                     [lambda: s5.dve_norm(v, link, 0), lambda: s5_matrices_dve(v)])
            s5.dve(v, link)

            def att1_first():
                v.wait_ge(low_saved, 128)

            mlp1.dve(v, link, lambda b: cond_norm(v, link) if b == 0 else None,
                     lambda b: fill1_dve(v, link, b), [att1_first] + calls(att1.dve_task(v, link), att1.lead()))
            att1.dve(v, link)
            mlp2.dve(v, link, nothing, nothing, [])
            low.dve(v, link)

        @block.gpsimd
        def _(pool):
            link = Chain(pool, pool_c)
            pool.wait_ge(consts_set, 1)
            for t in att0.lead():
                att0.pool_task(pool, link)(*t)
            att0.pool(pool, link)
            mlp0.pool(pool, link, nothing, [lambda: norm_rstd(pool, link, s5.norm0)])
            s5.pool(pool, link)
            mlp1.pool(pool, link, lambda b: cond_norm_pool(pool, link) if b == 0 else None,
                      calls(att1.pool_task(pool, link), att1.lead()))
            pool.wait_ge(l3_wr, 2)
            att1.pool(pool, link)
            mlp2.pool(pool, link, nothing, [])

        @block.sync
        def _(sp):
            sp.dma_start(rows[0:8, :], A["cond_1024"].rearrange("b (k p) -> (b k) p", p=P)).then_inc(ld_cond, 16)
            sp.dma_start(ident[:, :], A["const_ident"]).then_inc(ld_const, 16)
            sp.dma_start(Wm0, view(A["L0_cond_Wc"])).then_inc(ld_wm0, 16)
            load_mbias(sp, A["L0_cond_bc"], 3)
            for name, src in (("L0_bq", "L0_cond_bq"), ("L0_bk", "L0_cond_bk"),
                              ("L0_b1", "L0_cond_b1"), ("L1_b1", "L1_cond_b1"), ("n1g", "L2_cond_norm1_g"),
                              ("n1b", "L2_cond_norm1_b"), ("n2g", "L2_cond_norm2_g"), ("n2b", "L2_cond_norm2_b"),
                              ("lng", "L3_cond_ln_g"), ("lnb", "L3_cond_ln_b"), ("L3_b1", "L3_cond_b1"),
                              ("Dd", "L1_cond_D_diag")):
                r0, n = ROWS[name]
                sp.dma_start(rows[r0:r0 + n, :], A[src].rearrange("(r c) -> r c", c=P)).then_inc(ld_rows, 16)
            for b in range(1, B):
                sp.dma_start(batch(b), A["x"][b].rearrange("(t p) d -> p t d", p=P)).then_inc(ld_x[b], 16)
            save_gates(sp, 0)
            load_gates(sp, 0)
            lead = [t for t in att0.tasks(-100, 1000)]
            for t in lead[:len(att0.lead())]:
                att0.sync_task(sp)(*t)
            sp.dma_start(W1[:, :, :], view(A["L0_cond_W1"])).then_inc(ld_mlp[0], 16)
            sp.dma_start(W2[:, :, :], view(A["L0_cond_W2"])).then_inc(ld_mlp[0], 16)
            sp.dma_start(rot[:, :], A["const_rot"]).then_inc(ld_rope, 16)
            for k in range(2):
                sp.dma_start(rope[:, k, :], A["const_rope"][k]).then_inc(ld_rope, 16)
            sp.dma_start(c4[:, :], A["cond_1024"]).then_inc(ld_s5, 16)
            for k, name in enumerate(("Lam_re", "Lam_im", "log_step")):
                for h in range(2):
                    sp.dma_start(lam[SSM * h:SSM * (h + 1), k:k + 1],
                                 A["L1_cond_" + name].rearrange("(n o) -> n o", o=1)).then_inc(ld_s5, 16)
            sp.dma_start(lam[:, 3:4], A["const_sign"]).then_inc(ld_s5, 16)
            for t in lead[len(att0.lead()):]:
                att0.sync_task(sp)(*t)
            load_mbias(sp, A["L1_cond_bm"], 3)
            sp.wait_ge(att0.pv_done, 4 * NG)
            sp.dma_start(Wm1, view(A["L1_cond_Wm"])).then_inc(ld_mid, 16)
            sp.dma_start(Wc1, view(A["L1_cond_Wc"])).then_inc(ld_mid, 16)
            sp.dma_start(Wm2, view(A["L2_cond_ada_W"])).then_inc(ld_mid, 16)
            sp.dma_start(WL3, view(A["L3_cond_W1"])).then_inc(ld_mid, 16)
            sp.wait_ge(att0.m_free, PJ0)
            for h in range(2):
                for a in range(2):
                    sp.dma_start(s5B[SSM * h:SSM * (h + 1), a, :],
                                 A["L1_cond_B_im" if h != a else "L1_cond_B_re"]).then_inc(ld_bc, 16)
                    for k in range(DH):
                        sp.dma_start(s5C[:, a, k, SSM * h:SSM * (h + 1)],
                                     A["L1_cond_C_im" if h != a else "L1_cond_C_re"][k * P:(k + 1) * P, :]).then_inc(
                                         ld_bc, 16)
            for k, name in enumerate(("L2_cond_Wq", "L2_cond_Wk", "L2_cond_Wv", "L2_cond_Wo")):
                sp.dma_start(WA[:, k], view(A[name])).then_inc(ld_wa, 16)
            save_gates(sp, 1)
            load_mbias(sp, A["L1_cond_bc"], 1)
            load_gates(sp, 1)
            sp.wait_ge(mod_row, 3)
            load_mbias(sp, A["L2_cond_ada_b"], 3)
            save_gates(sp, 3)
            sp.wait_ge(mlp0.w2, B)
            sp.dma_start(W1[:, :, :], view(A["L1_cond_W1"])).then_inc(ld_mlp[1], 16)
            sp.dma_start(W2[:, :, :], view(A["L1_cond_W2"])).then_inc(ld_mlp[1], 16)
            sp.wait_ge(mlp0.xd, B)
            load_gates(sp, 2)
            w3, b3 = view(A["L3_cond_W2"]), A["L3_cond_b2"]

            def load_ring(r):
                for j in range(4):
                    c = slice(2048 * j + 1024 * r, 2048 * j + 1024 * (r + 1))
                    sp.dma_start(ring[j], w3[:, :, c]).then_inc(ld_ring[r], 16)
                    sp.dma_start(b2row[r][32 * j:32 * j + 32, :], b3[c].partition_broadcast(32)).then_inc(ld_b2[r], 16)

            sp.wait_ge(mlp1.t_full, 2)
            sp.wait_ge(s5.c_full, B)
            load_ring(0)
            sp.wait_ge(l3_w, 1)
            load_ring(1)
            for r in range(2):
                sp.wait_ge(l3_wr, r + 1)
                for j in range(4):
                    sp.dma_start(d_low[j][:, 1024 * r:1024 * (r + 1)],
                                 wrow[r][32 * j:32 * j + B, :]).then_inc(low_saved, 16)
            sp.wait_ge(low_saved, 128)
            for j in range(4):
                sp.dma_start(raw_a1[:, j], d_low[j].rearrange("b (h d r) -> d b h r", h=DH, r=RANK)).then_inc(ld_low, 16)
            lead = [t for t in att1.tasks(-100, 1000)]
            for t in lead[:len(att1.lead())]:
                att1.sync_task(sp)(*t)
            sp.wait_ge(mlp1.w2, B)
            sp.dma_start(W1[:, :, :], view(A["L2_cond_W1"])).then_inc(ld_mlp[2], 16)
            sp.dma_start(W2[:, :, :], view(A["L2_cond_W2"])).then_inc(ld_mlp[2], 16)
            for t in lead[len(att1.lead()):]:
                att1.sync_task(sp)(*t)
            low.sync(sp)


def constants():
    import numpy as np
    rot = np.zeros((P, P), np.float32)
    for h in range(P // HD):
        for j in range(HD // 2):
            rot[h * HD + 2 * j + 1, h * HD + j] = -1.0
            rot[h * HD + 2 * j, h * HD + HD // 2 + j] = 1.0
    inv = np.float32(1.0) / np.float32(10000.0) ** (np.arange(0, HD, 2, dtype=np.float32) / np.float32(HD))
    f = np.outer(np.arange(T, dtype=np.float32), inv).astype(np.float32)
    e = np.concatenate([f, f], -1).T
    rope = np.stack([np.tile(np.cos(e), (P // HD, 1)), np.tile(np.sin(e), (P // HD, 1))]).astype(np.float32)
    sign = np.concatenate([-np.ones((SSM, 1)), np.ones((SSM, 1))]).astype(np.float32)
    return {"const_ident": np.eye(P, dtype=np.float32), "const_rot": rot, "const_rope": rope, "const_sign": sign}


def kernel(**inputs):
    import numpy as _np
    import concourse.bacc as _bacc
    from concourse import mybir as _mybir
    from concourse.bass_utils import run_bass_kernel_spmd as _run

    nc = _bacc.Bacc("TRN2", target_bir_lowering=False, num_devices=1)
    arrays, args = {}, {}
    for name, value in list(inputs.items()) + list(constants().items()):
        a = _np.ascontiguousarray(value)
        arrays[f"in_{name}_dram"] = a
        args[name] = nc.dram_tensor(f"in_{name}_dram", a.shape, _mybir.dt.from_np(a.dtype), kind="ExternalInput").ap()
    out = nc.dram_tensor("out_0_dram", (B, T, D), F32, kind="ExternalOutput").ap()
    build(nc, args, out)
    r = _run(nc, [arrays], core_ids=[0])
    return r.results[0]["out_0_dram"]
```

```python
from contextlib import ExitStack

import concourse.bass as bass
from concourse import mybir

F32 = mybir.dt.float32
BF16 = mybir.dt.bfloat16
I32 = mybir.dt.int32
ACT = mybir.ActivationFunctionType
ALU = mybir.AluOpType
AX = mybir.AxisListType

P = 128
B, T, D = 4, 512, 256
TT = T // P
DH = D // P
NH, HD = 16, 16
F = 1024
FM = F // P
SSM = 64
RANK = 8
EPS = 1e-5
LOG2E = 1.4426950408889634
LN2_HI, LN2_LO = 0.693145751953125, 1.4286068203094172e-06
TWO_PI_A, TWO_PI_B, TWO_PI_C = 6.28125, 0.0019350051879882812, 3.019916050561733e-07
ROUND = 12582912.0

ROWS = {}
for _name, _n in (("cond", 8), ("L0_bq", 2), ("L0_bk", 2), ("L0_b1", 8), ("L1_b1", 8), ("n1g", 2), ("n1b", 2),
                  ("n2g", 2), ("n2b", 2), ("lng", 2), ("lnb", 2), ("L3_b1", 2), ("Dd", 2)):
    ROWS[_name] = (sum(n for _, n in ROWS.values()), _n)
NROWS = sum(n for _, n in ROWS.values())

SHIFT, SCALE, GATE, SHIFT2, SCALE2, GATE2 = range(6)

NG = 16
NSTEP = NG * 16
LOOK = 28
FILLS = 12 * 16
LEAD, TAIL = -30, NSTEP + 2
MISC_KINDS = ("V", "T", "Q", "K", "RQ", "RK", "M", "PJ")


def attention_schedule(rope):
    s = {}

    def put(n, *task):
        s.setdefault(n, []).append(task)

    for b in range(B):
        o = 64 * (b - 1)
        first = b == 0
        for i in range(2):
            put((-62, -52, o - 42, o - 42)[b] + (i if b < 2 else 4 * i), "LNS", b, i)
            put((-60, -47, o - 32, o - 32)[b] + (i if b < 2 else 4 * i), "LNN", b, i)
            put(-58 + i if first else o - 18 + 3 * i, "T", b, i)
        for half in range(2):
            q, k = (-56 + 6 * half, -54 + 6 * half) if first else ((o - 12, o - 5), (o + 8, o + 14))[half]
            for at, c in ((q, "Q"), (k, "K")):
                put(at, c, b, half)
                if rope:
                    put(at + (0 if first else 4 if at == o - 12 else 3), "R" + c, b, half)
                put(at + (1 if first else 5), "S" + c, b, half)
                put(at + (1 if first else 20), "W" + c, b, half)
        for g in range(4):
            put((-52, -52, -46, -8)[g] if first else o + (18, 35, 50, 66)[g], "FILL", b, g)
        put(64 * b + 1, "V", b, 0)
        put(64 * b + 4, "V", b, 1)
        put(64 * b + 91, "PJ", b, 0)
        put(64 * b + 94, "PJ", b, 1)
        put(226 + 6 * b, "W1S", b, 0)
    for G in range(NG):
        put(16 * G - 10, "M", G, 0)
        put(16 * G - 9, "MROW", G, 0)
        put(16 * G + 18, "O", G, 0)
        put(16 * G + 19, "OSAVE", G, 0)
        put(16 * G + 23, "OLOAD", G, 0)
        if G % 2:
            put(16 * G + 27, "RCP", G // 2, 0)
            put(16 * G + 28, "RSAVE", G // 2, 0)
            put(16 * G + 32, "RLOAD", G // 2, 0)
            put(16 * G + 38, "NORM", G // 2, 0)
    put(162, "S5N", 0, 0)
    put(190, "S5N", 1, 0)
    put(215, "MLS", 0, 0)
    put(225, "MLN", 0, 0)
    put(236, "MLT", 0, 0)
    return s




def build(nc, A, out):
    misc = {}
    scheds = [attention_schedule(False), attention_schedule(True)]
    for a, sched in enumerate(scheds):
        for n in sorted(sched):
            for task in sched[n]:
                if task[0] in MISC_KINDS:
                    misc[(a,) + task] = sum(1 for k in misc if k[0] == a)

    with ExitStack() as ctx:
        def sb(name, shape, dt=F32):
            return ctx.enter_context(nc.sbuf_tensor(name, shape, dt))

        def alias(name, shape):
            with nc.sbuf_tensor(name, shape, mybir.dt.float32r) as t:
                return t

        def sem(name):
            return ctx.enter_context(nc.semaphore(name))

        def scratch(name, shape, dt=F32):
            return nc.dram_tensor(name, shape, dt, kind="Internal").ap()

        PS = ctx.enter_context(nc.psum_tensor("PS", [P, 8, 512], F32))

        x = sb("x", [P, B * TT, D])
        WA = sb("WA", [P, 4, DH, D])
        W1R = alias("W1R", [P, DH, F])
        W1 = sb("W1", [P, DH, F])
        W2R = alias("W2R", [P, FM, D])
        W2 = sb("W2", [P, FM, D])
        gates = sb("gates", [P, 2, 2, B, D])
        gate_bias = sb("gate_bias", [P, D])
        bias_bc = sb("bias_bc", [P, 4, D])
        ident = sb("ident", [P, P])
        rot = sb("rot", [P, P])
        rope = sb("rope", [P, 2, T])
        rows = sb("rows", [NROWS, P])
        col = sb("col", [P, NROWS])
        bq16 = sb("bq16", [P, 2])
        cs = sb("cs", [P, 2, 32])
        cc = sb("cc", [P, 2, 32])
        csig = sb("csig", [P, 8])
        mrow_f = sb("mrow_f", [96, 512])
        mbias = sb("mbias", [96, 512])
        mcol = sb("mcol", [P, 2, 4, 96])
        mod = sb("mod", [P, 6, 2, 2, B])
        st6 = sb("st6", [P, TT, 6])
        mv = sb("mv", [P, TT, 2])
        ve = sb("ve", [P, TT])
        rs = sb("rs", [P, 3, TT])
        mhalf = sb("mhalf", [P, TT])
        xnorm = sb("xnorm", [P, TT, D])
        XNR = alias("XNR", [P, 2, DH, T])
        XN = sb("XN", [P, 2, DH, T])
        tsc = sb("tsc", [P, 4, D])
        PHR = alias("PHR", [P, 2, 4, T])
        PH = sb("PH", [P, 2, 4, T])
        H = PH[:, :, :, :].rearrange("p a b t -> p (a b) t")
        UW = 21504
        UR = alias("UR", [P, UW])
        U = sb("U", [P, UW])

        at = [0]

        def take(words, dt=F32):
            ap = U[:, at[0]:at[0] + words]
            at[0] += words
            assert at[0] <= UW, at[0]
            return ap if dt == F32 else ap.bitcast(dt)

        QP = [take(1024, BF16).rearrange("p (j t) -> p j t", j=4) for _ in range(4)]
        KP = [take(1024, BF16).rearrange("p (j t) -> p j t", j=4) for _ in range(4)]
        Vt = take(TT * NH * 32).rearrange("p (k h c) -> p k h c", k=TT, h=NH)
        parts = [take(768, BF16).rearrange("p (c t) -> p c t", c=3) for _ in range(4)]
        q32 = [take(T) for _ in range(4)]
        resid = take(T)
        Osb = [take(T) for _ in range(2)]
        Onum = [take(T) for _ in range(2)]
        Oden = [take(T) for _ in range(2)]
        Osum = [take(32) for _ in range(2)]
        yT = take(2 * T).rearrange("p (h t) -> p h t", h=2)
        mx = take(32).rearrange("p (a c) -> p a c", a=2)
        mneg = [take(128, BF16).rearrange("p (i c) -> p i c", i=2) for _ in range(2)]
        rt = [take(T) for _ in range(2)]

        at[0] = 0
        ring = [take(2048).rearrange("p (k n) -> p k n", k=2) for _ in range(4)]
        Wm1 = take(3072).rearrange("p (k n) -> p k n", k=2)
        Wm2 = take(3072).rearrange("p (k n) -> p k n", k=2)
        Wc1 = take(1024).rearrange("p (k n) -> p k n", k=2)
        WL3 = take(512).rearrange("p (k n) -> p k n", k=2)
        ROT = take(3 * T).rearrange("p (a t) -> p a t", a=3)
        CC, SS, RR = ROT[:, 1, :], ROT[:, 2, :], take(T)
        BT = take(512).rearrange("p (a k n) -> p a k n", a=2, k=2)
        CT = take(512).rearrange("p (a n) -> p a n", a=2)
        diagD = take(256).rearrange("p (k n) -> p k n", k=2)
        s5B = take(512).rearrange("p (a n) -> p a n", a=2)
        s5C = take(512).rearrange("p (a k n) -> p a k n", a=2, k=2)
        s5W = take(512).rearrange("p (a n) -> p a n", a=2)
        s5t = take(512).rearrange("p (a n) -> p a n", a=2)
        Wm0 = PH[:, :, :, :].rearrange("p a b t -> p (a b t)")[:, 0:3072].rearrange("p (k n) -> p k n", k=2)
        at[0] = 0
        bu = [take(T) for _ in range(2)]
        ysc = [[take(T) for _ in range(2)] for _ in range(2)]
        yst = [take(T) for _ in range(2)]
        XS2 = take(2 * T)
        at[0] = 6144
        XS = [t.rearrange("p (h t) -> p h t", h=2) for t in (take(2 * T), take(2 * T), XS2)]
        at[0] = 0
        xT = [take(2 * T).rearrange("p (h t) -> p h t", h=2) for _ in range(B)]
        gT = [take(2 * T).rearrange("p (h t) -> p h t", h=2) for _ in range(B)]
        z1 = [take(T) for _ in range(B)]
        z2 = [take(T) for _ in range(B)]
        btr = take(2 * B * D).rearrange("p (a b d) -> p a b d", a=2, b=B)

        W1h = UR[:, 0:2048].rearrange("p (k n) -> p k n", k=DH)
        W2h = UR[:, 2048:4096].rearrange("p (m n) -> p m n", m=FM)
        XH = UR[:, 4096:6144].rearrange("p (a k t) -> p a k t", a=2, k=DH)
        HH = PHR[:, 1]

        sv = sb("sv", [P, 64])
        lam = sb("lam", [P, 4])
        lam_i = sb("lam_i", [P, 1], I32)
        c4 = sb("c4", [B, D])
        c4s = sb("c4s", [B, 8])
        lnc = sb("lnc", [P, 2, 32])
        h3 = sb("h3", [P, 2, 32])
        b2row = [U[:, 8192 + 1024 * r:8192 + 1024 * (r + 1)] for r in range(2)]
        wrow = [U[:, 10240 + 1024 * r:10240 + 1024 * (r + 1)] for r in range(2)]
        modf = sb("modf", [P, 2, 2, B])
        czero, czero2 = sb("czero", [P, 1]), sb("czero2", [P, 1])
        mods_set = sem("mods_set")

        raw_a1 = sb("raw_a1", [P, 4, B, 2, RANK])

        d_gate = scratch("d_gate", (3, 2, B, D))
        d_parts = scratch("d_parts", (2, 16, P, 3, T), BF16)
        d_o = scratch("d_o", (2, NG, P, T))
        d_rec = scratch("d_rec", (2, NG // 2, 8, T))
        d_low = scratch("d_low", (4, B, 2 * D * RANK // 2))

        ld_cond, ld_bc = sem("ld_cond"), sem("ld_bc")
        ld_rows, ld_const, ld_rope, ld_s5 = sem("ld_rows"), sem("ld_const"), sem("ld_rope"), sem("ld_s5")
        ld_x = [sem(f"ld_x{b}") for b in range(B)]
        ld_wm0, ld_mb = sem("ld_wm0"), sem("ld_mb")
        ld_wa, ld_bias = sem("ld_wa"), sem("ld_bias")
        ld_mlp = [sem(f"ld_mlp{i}") for i in range(3)]
        ld_mid = sem("ld_mid")
        ld_ring = [sem("ld_ring0"), sem("ld_ring1")]
        ld_b2 = [sem("ld_b2_0"), sem("ld_b2_1")]
        ld_low = sem("ld_low")
        ld_gate = [sem(f"ld_gate{i}") for i in range(3)]
        gate_saved = sem("gate_saved")
        low_saved = sem("low_saved")
        out_done = sem("out_done")
        dve_c, pool_c = sem("dve_c"), sem("pool_c")
        cols_ready, silu_e, silu_ready = sem("cols_ready"), sem("silu_e"), sem("silu_ready")
        mod_ps, mod_row, mod_tr, mod_ready = sem("mod_ps"), sem("mod_row"), sem("mod_tr"), sem("mod_ready")
        row_tr = sem("row_tr")
        s5_tr, s5_ready, s5_pre, s5_num = (sem("s5_" + n) for n in ("tr", "ready", "pre", "num"))
        l3_tr, l3_h, l3_hg, l3_w, l3_wr, l3_bt, l3_ready = (sem(n) for n in (
            "l3_tr", "l3_h", "l3_hg", "l3_w", "l3_wr", "l3_bt", "l3_ready"))
        consts_set = sem("consts_set")
        ln_stats, ln_rstd, ln_done = sem("ln_stats"), sem("ln_rstd"), sem("ln_done")

        class Chain:

            def __init__(self, eng, s):
                self.eng, self.s, self.n = eng, s, 0

            def __call__(self, ins):
                self.n += 1
                ins.then_inc(self.s, 1)
                self.eng.wait_ge(self.s, self.n)

        def column(name, i):
            return col[:, ROWS[name][0] + i:ROWS[name][0] + i + 1]

        def batch(b):
            return x[:, TT * b:TT * (b + 1), :]

        def bank(i, n=512):
            return PS[:, i, 0:n]

        def tiles(part):
            return range(TT) if part is None else range(2 * part, 2 * part + 2)

        def norm_stats(v, link, k, b, waits, part=None):
            for s, n in waits:
                v.wait_ge(s, n)
            for t in tiles(part):
                ins = v.bn_stats(st6[:, t, :], x[:, TT * b + t, :])
            link(ins)
            if part == 0:
                return
            for t in range(TT):
                ins = v.bn_aggr(mv[:, t, :], st6[:, t, :])
            link(ins)
            v.tensor_scalar(ve[:, :], mv[:, :, 1], EPS, None, ALU.add).then_inc(ln_stats, 1)

        def norm_rstd(pool, link, k):
            pool.wait_ge(ln_stats, k + 1)
            link(pool.tensor_tensor(rs[:, 0, :], ve[:, :], mhalf[:, :], ALU.pow))
            link(pool.tensor_tensor(rs[:, 1, :], rs[:, 0, :], rs[:, 0, :], ALU.mult))
            link(pool.tensor_tensor(rs[:, 1, :], rs[:, 1, :], ve[:, :], ALU.mult))
            link(pool.tensor_scalar(rs[:, 1, :], rs[:, 1, :], -0.5, 1.5, ALU.mult, ALU.add))
            pool.tensor_tensor(rs[:, 2, :], rs[:, 0, :], rs[:, 1, :], ALU.mult).then_inc(ln_rstd, 1)

        def norm_apply(v, k, b, waits, part=None):
            v.wait_ge(ln_rstd, k + 1)
            for s, n in waits:
                v.wait_ge(s, n)
            for t in tiles(part):
                ins = v.tensor_scalar(xnorm[:, t, :], x[:, TT * b + t, :], mv[:, t, 0:1], rs[:, 2, t:t + 1],
                                      ALU.subtract, ALU.mult)
            if part != 0:
                ins.then_inc(ln_done, 1)

        def turn(pe, dst, half, src=None):
            for t in range(TT):
                s_ = xnorm[:, t, half * P:(half + 1) * P] if src is None else src(t)
                ins = pe.transpose(dst[:, t * P:(t + 1) * P], s_, ident[:, :])
            return ins

        def section(i, s_, half):
            return mcol[:, i % 2, 2 * (s_ % 2) + half, 32 * (s_ // 2):32 * (s_ // 2) + B]


        def mod_rows(pe, i, W, C, nchunk, waits):
            for s, n in waits:
                pe.wait_ge(s, n)
            for k in range(DH):
                for c in range(nchunk):
                    ins = pe.matmul(PS[32 * c:32 * c + 32, 6, :], C[:, k, :], W[:, k, 512 * c:512 * (c + 1)],
                                    start=(k == 0), stop=(k == 1))
            ins.then_inc(mod_ps, 1)

        def mod_turn(pe, i, nchunk):
            pe.wait_ge(mod_row, i + 1)
            for f in range(4):
                ins = pe.transpose(PS[:, 7, f * 96:f * 96 + 32 * nchunk], mrow_f[0:32 * nchunk, f * P:(f + 1) * P],
                                   ident[0:32 * nchunk, 0:32 * nchunk])
            ins.then_inc(mod_tr, 1)

        MOD_L = (0, 1, None, 2)
        MBIAS = (3, 6, 7, 10)

        def mod_evac(v, i, nchunk, save_waits):
            v.wait_ge(mod_ps, i + 1)
            v.wait_ge(ld_mb, 16 * MBIAS[i])
            for s, n in save_waits:
                v.wait_ge(s, n)
            v.tensor_tensor(mrow_f[0:32 * nchunk, :], PS[0:32 * nchunk, 6, :], mbias[0:32 * nchunk, :],
                            ALU.add).then_inc(mod_row, 1)
            v.wait_ge(mod_tr, i + 1)
            for f in range(4):
                ins = v.tensor_copy(mcol[:, i % 2, f, 0:32 * nchunk], PS[:, 7, f * 96:f * 96 + 32 * nchunk])
            ins.then_inc(mod_ready, 1)

        def load_mbias(sp, src, nchunk):
            for c in range(nchunk):
                sp.dma_start(mbias[32 * c:32 * c + 32, :],
                             src[512 * c:512 * (c + 1)].partition_broadcast(32)).then_inc(ld_mb, 16)

        def save_gates(sp, i):
            l = MOD_L[i]
            sp.wait_ge(mod_row, i + 1)
            sp.dma_start(d_gate[l, 0], mrow_f[32:32 + B, 0:D]).then_inc(gate_saved, 16)
            sp.dma_start(d_gate[l, 1], mrow_f[64:64 + B, D:2 * D]).then_inc(gate_saved, 16)

        def load_gates(sp, l):
            sp.wait_ge(gate_saved, 32 * (l + 1))
            src = d_gate[l].rearrange("a b d -> (a b d)")
            sp.dma_start(gates[:, l % 2].rearrange("p a b d -> p (a b d)"),
                         src.partition_broadcast(P)).then_inc(ld_gate[l], 16)

        def view(w):
            return w.rearrange("(k p) n -> p k n", p=P)

        moved = [[sem(f"{n}{i}") for i in range(m)] for n, m in (
            ("parts_saved", 2), ("filled", 4), ("max_set", 4), ("o_saved", 2), ("o_loaded", 2), ("sums_loaded", 2),
            ("recip_saved", 2), ("recip_loaded", 2))]

        class Attention:

            def __init__(self, a, before):
                self.a, self.before, self.sched = a, before, scheds[a]
                n = f"a{a}_"
                self.st_full, self.st_read = sem(n + "st_full"), sem(n + "st_read")
                self.sm_full, self.sm_free = sem(n + "sm_full"), sem(n + "sm_free")
                self.pv_done, self.o_free = sem(n + "pv_done"), sem(n + "o_free")
                self.m_full, self.m_free = sem(n + "misc_full"), sem(n + "misc_free")
                self.split = [sem(n + f"split{i}") for i in range(2)]
                (self.saved, self.filled, self.mset, self.osaved, self.oloaded, self.sloaded, self.rsaved,
                 self.rloaded) = moved
                self.b0 = B * a
                self.rec, self.y = sem(n + "rec"), sem(n + "y")
                self.mlp = None
                self.xd = sem(n + "x_done")
                self.init = sem(n + "init")
                self.norm0 = 0 if a == 0 else 16

            def idx(self, *task):
                return misc[(self.a,) + task]

            def steps(self, task):
                for n in range(LEAD, TAIL + 1):
                    for t in self.sched.get(n, []):
                        task(*t)
                    yield n

            def tasks(self, lo, hi):
                return [t for n in sorted(self.sched) if lo <= n < hi for t in self.sched[n]]

            def lead(self):
                return self.tasks(-100, LEAD)

            def tail(self):
                return self.tasks(TAIL + 1, 1000)

            def pe_task(self, pe):
                def misc_done(ins):
                    ins.then_inc(self.m_full, 1)

                def task(kind, b, i):
                    if kind == "MLT":
                        self.mlp.pe_transposes(pe, 0)
                    if kind not in MISC_KINDS:
                        return
                    k = self.idx(kind, b, i)
                    if k:
                        pe.wait_ge(self.m_free, k)
                    if kind == "T":
                        pe.wait_ge(ln_done, self.norm0 + b + 1)
                        misc_done(turn(pe, bank(7), i))
                    elif kind in ("Q", "K"):
                        pe.wait_ge(ld_wa, 64 * (self.a + 1))
                        pe.wait_ge(self.m_free, self.idx("T", b, 1) + 1)
                        w = WA[:, "QK".index(kind)]
                        for k_ in range(DH):
                            ins = pe.matmul(bank(7), w[:, k_, i * P:(i + 1) * P], XN[:, b % 2, k_, :],
                                            start=(k_ == 0), stop=(k_ == 1))
                        misc_done(ins)
                    elif kind in ("RQ", "RK"):
                        pe.wait_ge(self.m_free, self.idx(kind[1], b, i) + 1)
                        pe.wait_ge(ld_rope, 48)
                        misc_done(pe.matmul(bank(7), rot[:, :], q32[2 * i + (kind == "RK")], start=True, stop=True))
                    elif kind == "V":
                        for t in range(2):
                            for k_ in range(DH):
                                ins = pe.matmul(PS[:, 7, 256 * t:256 * (t + 1)],
                                                XN[:, b % 2, k_, (2 * i + t) * P:(2 * i + t + 1) * P], WA[:, 2, k_, :],
                                                start=(k_ == 0), stop=(k_ == 1))
                        misc_done(ins)
                    elif kind == "M":
                        pe.wait_ge(self.sm_free, 8 * (b + 1))
                        misc_done(pe.transpose(PS[0:16, 7, 0:P], mx[:, b % 2, :], ident[:, :]))
                    elif kind == "PJ":
                        pe.wait_ge(self.y, 2 * b + 2)
                        for t in range(2):
                            for k_ in range(DH):
                                ins = pe.matmul(PS[:, 7, 256 * t:256 * (t + 1)],
                                                yT[:, k_, (2 * i + t) * P:(2 * i + t + 1) * P], WA[:, 3, k_, :],
                                                start=(k_ == 0), stop=(k_ == 1))
                        misc_done(ins)

                return task

            def pe(self, pe):
                for s, n in self.before:
                    pe.wait_ge(s, n)
                for n in self.steps(self.pe_task(pe)):
                    if n == 0:
                        pe.wait_ge(self.init, 1)
                    if 0 <= n < NSTEP:
                        b, g, kt, j = n // 64, n // 16 % 4, n // 4 % 4, n % 4
                        if n % 16 == 0:
                            pe.wait_ge(self.mset[g], 32 * (self.b0 + b + 1))
                        if n >= 2:
                            pe.wait_ge(self.st_read, n - 1)
                        pe.matmul(bank(n % 2), KP[g][0:98, j, kt * P:(kt + 1) * P], QP[g][0:98, j, :],
                                  start=True, stop=True).then_inc(self.st_full, 1)
                    w = n + LOOK
                    if 0 <= w < NSTEP:
                        b, g, j, qt = w // 64, w // 16 % 4, w // 4 % 4, w % 4
                        if w % 16 == 0:
                            pe.wait_ge(self.filled[g], FILLS * (self.b0 + b + 1))
                        if w % 2 == 0 and w >= 4:
                            pe.wait_ge(self.sm_free, w // 2 - 1)
                        ins = pe.matmul(bank(2 + w % 4), QP[g][0:96, j, qt * P:(qt + 1) * P], KP[g][0:96, j, :],
                                        start=True, stop=True)
                        if w % 2:
                            ins.then_inc(self.sm_full, 1)
                    if n % 4 == 1 and 0 <= (n - 5) // 4 < NG * 4:
                        m = (n - 5) // 4
                        b, g, kt = m // 16, m // 4 % 4, m % 4
                        pe.wait_ge(self.st_read, 4 * m + 4)
                        if kt == 0:
                            pe.wait_ge(self.m_free, self.idx("V", b, 1) + 1)
                            if m:
                                pe.wait_ge(self.o_free, m // 4)
                        for j in range(4):
                            ins = pe.matmul(PS[32 * j:32 * j + 32, 6, :], Vt[:, kt, 4 * g + j, :], PH[:, m % 2, j, :],
                                            start=(kt == 0), stop=(kt == 3))
                        ins.then_inc(self.pv_done, 1)

            def act_task(self, act):
                def task(kind, b, i):
                    if kind == "T":
                        act.wait_ge(self.m_full, self.idx(kind, b, i) + 1)
                        if b >= 2:
                            act.wait_ge(self.m_full, self.idx("V", b - 2, 1) + 1)
                        elif self.a == 0:
                            act.wait_ge(mod_ready, 1)
                        m = 0 if self.a == 0 else 4
                        nc.scalar.activation(XN[:, b % 2, i, :], bank(7), ACT.Identity, bias=mod[:, m, 0, i, b:b + 1],
                                             scale=mod[:, m, 1, i, b:b + 1]).then_inc(self.m_free, 1)
                    elif kind in ("Q", "K"):
                        act.wait_ge(self.m_full, self.idx(kind, b, i) + 1)
                        if b:
                            act.wait_ge(self.split[i], 2 * b + (kind == "K") - 1)
                        o = q32[2 * i + (kind == "K")]
                        if self.a == 0:
                            bias = bq16[:, i:i + 1] if kind == "Q" else column("L0_bk", i)
                            ins = nc.scalar.activation(o, bank(7), ACT.Identity, bias=bias,
                                                       scale=1.0 / HD if kind == "Q" else 1.0)
                        else:
                            ins = nc.scalar.activation(o, bank(7), ACT.Copy, scale=HD ** -0.5 if kind == "Q" else 1.0)
                        ins.then_inc(self.m_free, 1)
                    elif kind == "V" and self.a == 1:
                        act.wait_ge(self.m_full, self.idx(kind, b, i) + 1)
                        if b:
                            act.wait_ge(self.pv_done, 16 * b)
                        nc.scalar.activation(Vt[:, 2 * i:2 * i + 2, :, 0:HD],
                                             bank(7).rearrange("p (t h c) -> p t h c", t=2, h=NH),
                                             ACT.Copy).then_inc(self.m_free, 1)
                    elif kind == "O":
                        act.wait_ge(self.pv_done, 4 * b + 4)
                        if b >= 2:
                            act.wait_ge(self.osaved[b % 2], 16 * (2 * self.b0 + b // 2))
                        nc.scalar.activation(Osb[b % 2], bank(6), ACT.Copy).then_inc(self.o_free, 1)

                return task

            def act(self, act):
                for n in self.steps(self.act_task(act)):
                    if 0 <= n < NSTEP:
                        m, j = n // 4, n % 4
                        act.wait_ge(self.st_full, n + 1)
                        if j == 0 and m >= 2:
                            act.wait_ge(self.pv_done, m - 1)
                        nc.scalar.activation(PH[:, m % 2, j, :], bank(n % 2), ACT.Exp).then_inc(self.st_read, 1)

            def split_part(self, eng, link, kind, b, i, rest):
                zero = czero[:, 0:1].to_broadcast([P, T])
                if b:
                    eng.wait_ge(self.saved[i], 32 * (self.b0 + b))
                k = kind == "SK"
                eng.wait_ge(self.m_free, self.idx(("R" if self.a else "") + kind[1], b, i) + 1)
                src, d = q32[2 * i + k], parts[2 * i + k]
                if self.a:
                    link(eng.tensor_tensor(src, src, rope[:, 0, :], ALU.mult))
                    eng.tensor_tensor(d[:, 0, :], src, rt[k], ALU.add)
                    link(eng.tensor_tensor(src, src, rt[k], ALU.add))
                else:
                    link(eng.tensor_tensor(d[:, 0, :], src, zero, ALU.add))
                link(eng.tensor_tensor(rest, src, d[:, 0, :], ALU.subtract))
                link(eng.tensor_tensor(d[:, 1, :], rest, zero, ALU.add))
                eng.tensor_tensor(d[:, 2, :], rest, d[:, 1, :], ALU.subtract).then_inc(self.split[i], 1)

            def dve_task(self, v, link):
                def task(kind, b, i):
                    if kind == "LNS":
                        norm_stats(v, link, self.norm0 + b, b, [(ld_x[b], 16) if self.a == 0 else (mlp1.xd, b + 1)], i)
                    elif kind in ("SQ", "SK") and (b, i) == (0, 0):
                        self.split_part(v, link, kind, b, i, resid)
                    elif kind == "MLT":
                        self.mlp.dve_modulate(v, 0)
                    elif kind == "MLS":
                        norm_stats(v, link, self.mlp.norm0, 0, [(self.xd, 2)])
                    elif kind == "MLN":
                        norm_apply(v, self.mlp.norm0, 0, [(self.m_full, self.idx("T", B - 1, 1) + 1)])
                    elif kind == "LNN":
                        norm_apply(v, self.norm0 + b, b, [(self.m_full, self.idx("T", b - 1, 1) + 1)] if b else
                                   [(mlp1.t_full, 2 * B)] if self.a else [], i)
                    elif kind == "V" and self.a == 0:
                        v.wait_ge(self.m_full, self.idx(kind, b, i) + 1)
                        if b:
                            v.wait_ge(self.pv_done, 16 * b)
                        else:
                            v.wait_ge(ld_bias, 64)
                        for t in range(2):
                            ins = v.tensor_tensor(Vt[:, 2 * i + t, :, 0:HD],
                                                  PS[:, 7, 256 * t:256 * (t + 1)].rearrange("p (h c) -> p h c", h=NH),
                                                  bias_bc[:, 0, :].rearrange("p (h c) -> p h c", h=NH), ALU.add)
                        ins.then_inc(self.m_free, 1)
                    elif kind in ("RQ", "RK"):
                        v.wait_ge(self.m_full, self.idx(kind, b, i) + 1)
                        k = kind == "RK"
                        if b or i:
                            v.wait_ge(self.split[1 - i], 2 * (b - 1 + i) + k + 1)
                        v.tensor_tensor(rt[k], bank(7), rope[:, 1, :], ALU.mult).then_inc(self.m_free, 1)
                    elif kind == "M":
                        v.wait_ge(self.m_full, self.idx(kind, b, i) + 1)
                        if b >= 2:
                            v.wait_ge(self.mset[(b - 2) % 4], 32 * (self.b0 + (b - 2) // 4 + 1))
                        d = mneg[b % 2]
                        link(v.tensor_scalar(d[0:16, 0, :], PS[0:16, 7, 0:P], -1.0, None, ALU.mult))
                        ins = v.scalar_tensor_tensor(out=d[0:16, 1, :], in0=PS[0:16, 7, 0:P], scalar=-1.0,
                                                     in1=d[0:16, 0, :], op0=ALU.mult, op1=ALU.subtract)
                        ins.then_inc(self.m_free, 1)
                    elif kind == "NORM":
                        v.wait_ge(self.oloaded[b % 2], 32 * (self.b0 + b // 2 + 1))
                        v.wait_ge(self.rloaded[b % 2], 16 * (self.b0 + b // 2 + 1))
                        if b >= 2:
                            v.wait_ge(self.m_full, self.idx("PJ", b // 2 - 1, 1) + 1)
                        v.tensor_tensor(yT[:, b % 2, :], Onum[b % 2], Oden[b % 2], ALU.mult).then_inc(self.y, 1)
                    elif kind == "RCP":
                        v.wait_ge(self.sloaded[b % 2], 32 * (self.b0 + b // 2 + 1))
                        v.reciprocal(Osum[b % 2], Osum[b % 2]).then_inc(self.rec, 1)
                    elif kind == "PJ":
                        v.wait_ge(self.m_full, self.idx(kind, b, i) + 1)
                        if b == 0 and i == 0:
                            v.wait_ge(ld_gate[2 * self.a], 16)
                        if b:
                            v.wait_ge(self.xd, 2 * b + i - 1)
                        if b == B - 1:
                            v.wait_ge(self.mlp.xd, 1)
                        v.tensor_tensor(tsc[:, 2 * i:2 * i + 2, :],
                                        bank(7).rearrange("p (t c) -> p t c", t=2),
                                        gates[:, 0, 0, b:b + 1, :].to_broadcast([P, 2, D]),
                                        ALU.mult).then_inc(self.m_free, 1)

                return task

            def set_ones(self, eng, link):
                for g in range(4):
                    link(eng.memset(KP[g][96:98, :, :], 1.0))
                eng.memset(Vt[:, :, :, HD:2 * HD], 1.0).then_inc(self.init, 1)

            def dve(self, v, link):
                for n in self.steps(self.dve_task(v, link)):
                    w = n + LOOK
                    if 0 <= w < NSTEP and w % 2:
                        u = w // 2
                        G, c = w // 16, (w - 1) % 16
                        v.wait_ge(self.sm_full, u + 1)
                        if u % 8 == 0 and G >= 2:
                            v.wait_ge(self.m_full, self.idx("M", G - 2, 0) + 1)
                        v.tensor_reduce(mx[:, G % 2, c:c + 2], PS[:, 2 + (w - 1) % 4:4 + (w - 1) % 4, :],
                                        AX.X, ALU.max).then_inc(self.sm_free, 1)

            def pool_task(self, pool, link):
                def task(kind, b, i):
                    if kind == "LNS":
                        if i:
                            norm_rstd(pool, link, self.norm0 + b)
                    elif kind == "MLS":
                        norm_rstd(pool, link, self.mlp.norm0)
                    elif kind == "S5N" and self.a == 0:
                        (s5_decay, s5_angles)[b](pool, link)
                    elif kind == "W1S":
                        if b == 0:
                            pool.wait_ge(ld_mlp[self.mlp.l], 32)
                            pool.wait_ge(self.st_full, NSTEP - 32)
                        c = slice(512 * (b % 2), 512 * (b % 2 + 1))
                        link(pool.tensor_tensor(W1h[:, b // 2, c], W1[:, b // 2, c],
                                                czero[:, 0:1].to_broadcast([P, 512]), ALU.add))
                        pool.tensor_tensor(W1R[:, b // 2, c], W1[:, b // 2, c], W1h[:, b // 2, c].bitcast(F32),
                                           ALU.subtract).then_inc(self.mlp.w_low, 1)
                    elif kind in ("SQ", "SK") and (b, i) != (0, 0):
                        self.split_part(pool, link, kind, b, i, Onum[1] if b == 0 else resid)
                    elif kind == "PJ":
                        if self.a == 0 and i == 0:
                            pool.wait_ge(ld_gate[0], 16)
                            pool.wait_ge(ln_done, self.norm0 + b + 1)
                            link(pool.tensor_tensor(gate_bias[:, :], gates[:, 0, 0, b, :], bias_bc[:, 1, :], ALU.mult))
                            for t in range(TT):
                                ins = pool.tensor_tensor(x[:, TT * b + t, :], x[:, TT * b + t, :], gate_bias[:, :], ALU.add)
                            link(ins)
                        pool.wait_ge(self.m_free, self.idx(kind, b, i) + 1)
                        xs = x[:, TT * b + 2 * i:TT * b + 2 * i + 2, :]
                        pool.tensor_tensor(xs, xs, tsc[:, 2 * i:2 * i + 2, :], ALU.add).then_inc(self.xd, 1)

                return task

            def pool(self, pool, link):
                for n in self.steps(self.pool_task(pool, link)):
                    pass

            def sync_task(self, sp):
                def task(kind, b, i):
                    if kind in ("WQ", "WK"):
                        k = kind == "WK"
                        sp.wait_ge(self.split[i], 2 * b + k + 1)
                        sp.dma_start(d_parts[self.a, 4 * b + 2 * i + k], parts[2 * i + k]).then_inc(self.saved[i], 16)
                    elif kind == "FILL":
                        g = i
                        sp.wait_ge(self.saved[g // 2], 32 * (self.b0 + b + 1))
                        if b:
                            sp.wait_ge(self.st_full, 64 * (b - 1) + 16 * (g + 1))
                        q = d_parts[self.a, 4 * b + 2 * (g // 2)]
                        k = d_parts[self.a, 4 * b + 2 * (g // 2) + 1]
                        for dst, src, plan in ((QP[g], q, ("000", "11", "2")), (KP[g], k, ("012", "01", "0"))):
                            slot = 0
                            for pieces in plan:
                                for c in pieces:
                                    s_ = src[64 * (g % 2):64 * (g % 2) + 64, int(c), :].rearrange(
                                        "(j d) t -> d j t", j=4)
                                    sp.dma_start(dst[16 * slot:16 * slot + 16, :, :], s_).then_inc(self.filled[g], 16)
                                    slot += 1
                    elif kind == "MROW":
                        g = b % 4
                        sp.wait_ge(self.m_free, self.idx("M", b, 0) + 1)
                        for r in range(2):
                            sp.dma_start(QP[g][96 + r:97 + r, :, :].rearrange("p j (q c) -> p (j q) c", c=P),
                                         mneg[b % 2][0:16, r, :]).then_inc(self.mset[g], 16)
                    elif kind == "OSAVE":
                        sp.wait_ge(self.o_free, b + 1)
                        sp.dma_start(d_o[self.a, b], Osb[b % 2]).then_inc(self.osaved[b % 2], 16)
                    elif kind == "OLOAD":
                        sp.wait_ge(self.osaved[b % 2], 16 * (2 * self.b0 + b // 2 + 1))
                        hp = b // 2
                        if hp >= 2:
                            sp.wait_ge(self.y, hp - 1)
                        src = d_o[self.a, b].rearrange("(j r) t -> j r t", j=4)
                        r0 = 64 * (b % 2)
                        sp.dma_start(Onum[hp % 2][r0:r0 + 64, :], src[:, 0:HD, :]).then_inc(self.oloaded[hp % 2], 16)
                        sp.dma_start(Osum[hp % 2][r0:r0 + 64, :], src[:, HD, :].rearrange(
                            "j (a c) -> j a c", c=32)).then_inc(self.sloaded[hp % 2], 16)
                    elif kind == "RSAVE":
                        sp.wait_ge(self.rec, b + 1)
                        sp.dma_start(d_rec[self.a, b].rearrange("j (a c) -> (j a) c", c=32),
                                     Osum[b % 2]).then_inc(self.rsaved[b % 2], 16)
                    elif kind == "RLOAD":
                        sp.wait_ge(self.rsaved[b % 2], 16 * (self.b0 + b // 2 + 1))
                        sp.dma_start(Oden[b % 2], d_rec[self.a, b].unsqueeze(1).to_broadcast([8, HD, T])).then_inc(
                            self.rloaded[b % 2], 16)

                return task


        def share(lead, slot):
            return lead[len(lead) * slot // (2 * FM):len(lead) * (slot + 1) // (2 * FM)]

        class MLP:

            def __init__(self, l, before, xready, norm0, b1, func, bias_row, after, t_free):
                self.l, self.before, self.xready, self.norm0 = l, before, xready, norm0
                self.b1, self.func, self.bias_row, self.after, self.t_free = b1, func, bias_row, after, t_free
                n = f"m{l}_"
                self.t_full, self.t_out = sem(n + "t_full"), sem(n + "t_out")
                self.h_full, self.h_free = sem(n + "h_full"), sem(n + "h_free")
                self.w2, self.acc_free, self.xd = sem(n + "w2"), sem(n + "acc_free"), sem(n + "x_done")
                self.batch_w2 = 1

            def t_bank(self, b, half):
                return bank((6 if b or self.l == 1 else 2) + half)

            def pe_transposes(self, pe, b):
                pe.wait_ge(ln_done, self.norm0 + b + 1)
                for s_, n in self.t_free(b):
                    pe.wait_ge(s_, n)
                if b:
                    pe.wait_ge(self.t_out, 2 * b)
                for half in range(2):
                    turn(pe, self.t_bank(b, half), half).then_inc(self.t_full, 1)

            def pe(self, pe, fill, lead):
                for s_, n in self.before:
                    pe.wait_ge(s_, n)
                if self.l != 1:
                    self.pe_transposes(pe, 0)
                pe.wait_ge(ld_mlp[self.l], 32)
                for b in range(B):
                    pe.wait_ge(self.t_out, 2 * b + 2)
                    for m in range(FM):
                        q = FM * b + m
                        if q >= 2:
                            pe.wait_ge(self.h_free, q - 1)
                        for k in range(DH):
                            ins = pe.matmul(bank(4 + q % 2), W1[:, k, m * P:(m + 1) * P], XN[:, b % 2, k, :],
                                            start=(k == 0), stop=(k == 1))
                        ins.then_inc(self.h_full, 1)
                        if b and m in (2, 5):
                            fill(1 if m == 2 else 2, b - 1)
                        if b == B - 1:
                            for task in share(lead, m):
                                task()
                    if b + 1 < B:
                        self.pe_transposes(pe, b + 1)
                    if b:
                        pe.wait_ge(self.acc_free, b)
                    else:
                        pe.wait_ge(self.t_out, 2)
                    for m in range(FM):
                        if b == B - 1:
                            for task in share(lead, FM + m):
                                task()
                        pe.wait_ge(self.h_free, FM * b + m + 1)
                        for t in range(TT):
                            ins = pe.matmul(bank(t, D), H[:, m, t * P:(t + 1) * P], W2[:, m, :],
                                            start=(m == 0), stop=(m == FM - 1))
                    ins.then_inc(self.w2, 1)
                    if b + 1 < B:
                        fill(0, b)

            def act(self, act, fill, lead):
                for b in range(B):
                    for m in range(FM):
                        act.wait_ge(self.h_full, FM * b + m + 1)
                        if m == 0 and b:
                            act.wait_ge(self.w2, b)
                        bias = column(self.b1, m) if self.b1 else 0.0
                        nc.scalar.activation(H[:, m, :], bank(4 + (FM * b + m) % 2), self.func,
                                             bias=bias).then_inc(self.h_free, 1)
                        if b == B - 1:
                            for task in share(lead, m):
                                task()
                    fill(b)
                for m in range(FM):
                    for task in share(lead, FM + m):
                        task()

            def dve_norm(self, v, link, b):
                s_, n = self.xready
                norm_stats(v, link, self.norm0 + b, b, [(s_, n * (b + 1))])
                norm_apply(v, self.norm0 + b, b, [(self.t_full, 2 * b)] if b else
                           [(s5.t_full, 2 * B)] if self.l == 1 else [])

            def dve_modulate(self, v, b):
                if b >= 2:
                    v.wait_ge(self.h_full, FM * (b - 1))
                m = 2 * self.l + 1
                for half in range(2):
                    v.wait_ge(self.t_full, 2 * b + half + 1)
                    v.tensor_scalar(XN[:, b % 2, half, :], self.t_bank(b, half), mod[:, m, 1, half, b:b + 1],
                                    mod[:, m, 0, half, b:b + 1], ALU.mult, ALU.add).then_inc(self.t_out, 1)

            def dve(self, v, link, side, fill, lead):
                for b in range(B):
                    if b + 1 < B:
                        self.dve_norm(v, link, b + 1)
                    if b:
                        fill(b - 1)
                    if b + 1 < B:
                        if b == 0 and self.l != 1:
                            for t in self.after.tail():
                                if t[0] == "RCP":
                                    self.after.dve_task(v, link)(*t)
                        self.dve_modulate(v, b + 1)
                        if b == 0 and self.l != 1:
                            for t in self.after.tail():
                                if t[0] == "NORM":
                                    self.after.dve_task(v, link)(*t)
                        side(b)
                    else:
                        for task in lead:
                            task()
                    v.wait_ge(self.w2, self.batch_w2 * (b + 1))
                    if b:
                        v.wait_ge(self.xd, b)
                    if b == 0:
                        v.wait_ge(self.after.xd, B if self.l == 1 else 2 * (B - 1))
                    if b == 1 and self.l != 1:
                        v.wait_ge(self.after.xd, 2 * B)
                    v.tensor_tensor(tsc[:, :, :], PS[:, 0:TT, 0:D],
                                    gates[:, self.l % 2, 1, b:b + 1, :].to_broadcast([P, TT, D]),
                                    ALU.mult).then_inc(self.acc_free, 1)
                    if b == 0 and self.l != 1:
                        for t in self.after.tail():
                            if t[0] == "PJ":
                                self.after.dve_task(v, link)(*t)

            def pool(self, pool, link, fill, lead):
                for b in range(B):
                    if b + 1 < B:
                        norm_rstd(pool, link, self.norm0 + b + 1)
                        fill(b)
                    else:
                        for task in lead:
                            task()
                    if self.bias_row is not None:
                        link(pool.tensor_tensor(gate_bias[:, :], gates[:, self.l % 2, 1, b, :],
                                                bias_bc[:, self.bias_row, :], ALU.mult))
                        pool.wait_ge(ln_done, self.norm0 + b + 1)
                        for t in range(TT):
                            ins = pool.tensor_tensor(x[:, TT * b + t, :], x[:, TT * b + t, :], gate_bias[:, :], ALU.add)
                        link(ins)
                    pool.wait_ge(self.acc_free, b + 1)
                    pool.tensor_tensor(batch(b), batch(b), tsc[:, :, :], ALU.add).then_inc(self.xd, 1)
                    if b == 0 and self.l != 1:
                        for t in self.after.tail():
                            if t[0] == "PJ":
                                self.after.pool_task(pool, link)(*t)

        class SplitMLP(MLP):

            def __init__(self, *args):
                super().__init__(*args)
                n = f"m{self.l}_"
                self.w_high, self.w_low = sem(n + "w_high"), sem(n + "w_low")
                self.x_low, self.h_low = sem(n + "x_low"), sem(n + "h_low")
                self.batch_w2 = FM

            def pe(self, pe, fill, lead):
                for s_, n in self.before:
                    pe.wait_ge(s_, n)
                pe.wait_ge(self.w_low, 4)

                def product1(q):
                    b, m = q // FM, q % FM
                    if m == 0:
                        pe.wait_ge(self.x_low, b + 1)
                    if q >= 2:
                        pe.wait_ge(self.h_free, q - 1)
                    c = slice(m * P, (m + 1) * P)
                    for k in range(DH):
                        for i, (w, a) in enumerate(((W1h, XH), (W1h, XNR), (W1R, XH))):
                            ins = pe.matmul(bank(4 + q % 2), w[:, k, c], a[:, b % 2, k, :],
                                            start=(k == 0 and i == 0), stop=(k == 1 and i == 2))
                    ins.then_inc(self.h_full, 1)

                def product2(q):
                    b, m = q // FM, q % FM
                    if m == 0 and b:
                        pe.wait_ge(self.acc_free, b)
                    if b == 0:
                        pe.wait_ge(self.t_out, 2)
                        pe.wait_ge(self.w_low, 5 + m // 2)
                    pe.wait_ge(self.h_low, q + 1)
                    for t in range(TT):
                        c = slice(t * P, (t + 1) * P)
                        for i, (a, w) in enumerate(((HH, W2h), (HH, W2R), (PHR[:, 0], W2h))):
                            ins = pe.matmul(bank(t, D), a[:, q % 4, c], w[:, m, :],
                                            start=(m == 0 and i == 0), stop=(m == FM - 1 and i == 2))
                    ins.then_inc(self.w2, 1)

                product1(0)
                product1(1)
                for q in range(FM * B):
                    b, m = q // FM, q % FM
                    if b and m in (1, 2):
                        fill(m, b - 1)
                    if m == 4 and b + 1 < B:
                        self.pe_transposes(pe, b + 1)
                    if q + 2 < FM * B:
                        product1(q + 2)
                    product2(q)
                    if b == B - 1:
                        for task in share(lead, 2 * m) + share(lead, 2 * m + 1):
                            task()
                    elif m == FM - 1:
                        fill(0, b)

            def act(self, act, fill, lead):
                for c in range(4):
                    if c == 0:
                        act.wait_ge(ld_mlp[self.l], 32)
                        act.wait_ge(self.after.st_full, NSTEP)
                    nc.scalar.activation(W2h[:, 2 * c:2 * c + 2, :], W2[:, 2 * c:2 * c + 2, :],
                                         ACT.Copy).then_inc(self.w_high, 1)
                for q in range(FM * B):
                    act.wait_ge(self.h_full, q + 1)
                    if q >= 4:
                        act.wait_ge(self.w2, q - 3)
                    bias = column(self.b1, q % FM) if self.b1 else 0.0
                    nc.scalar.activation(PH[:, 0, q % 4, :], bank(4 + q % 2), self.func, bias=bias)
                    nc.scalar.activation(HH[:, q % 4, :], bank(4 + q % 2), self.func, bias=bias).then_inc(self.h_free, 1)

            def dve_modulate(self, v, b):
                if b >= 2:
                    v.wait_ge(self.h_full, FM * (b - 1))
                m = 2 * self.l + 1
                for half in range(2):
                    v.wait_ge(self.t_full, 2 * b + half + 1)
                    scale, shift = mod[:, m, 1, half, b:b + 1], mod[:, m, 0, half, b:b + 1]
                    v.tensor_scalar(XN[:, b % 2, half, :], self.t_bank(b, half), scale, shift, ALU.mult, ALU.add)
                    v.tensor_scalar(XH[:, b % 2, half, :], self.t_bank(b, half), scale, shift, ALU.mult,
                                    ALU.add).then_inc(self.t_out, 1)
                v.wait_ge(self.t_out, 2 * b + 2)
                v.tensor_tensor(XNR[:, b % 2], XN[:, b % 2], XH[:, b % 2].bitcast(F32), ALU.subtract).then_inc(self.x_low, 1)

            def pool(self, pool, link, fill, lead):
                def w2_low(c):
                    pool.wait_ge(self.w_high, c + 1)
                    pool.tensor_tensor(W2R[:, 2 * c:2 * c + 2, :], W2[:, 2 * c:2 * c + 2, :],
                                       W2h[:, 2 * c:2 * c + 2, :].bitcast(F32), ALU.subtract).then_inc(self.w_low, 1)

                def tail(i):
                    for t in self.after.tail():
                        if t[0] == "PJ" and t[2] == i:
                            self.after.pool_task(pool, link)(*t)

                def add(b):
                    pool.wait_ge(self.acc_free, b + 1)
                    pool.tensor_tensor(batch(b), batch(b), tsc[:, :, :], ALU.add).then_inc(self.xd, 1)

                w2_low(0)
                for q in range(FM * B):
                    b, m = q // FM, q % FM
                    pool.wait_ge(self.h_free, q + 1)
                    pool.tensor_tensor(PHR[:, 0, q % 4, :], PH[:, 0, q % 4, :], HH[:, q % 4, :].bitcast(F32),
                                       ALU.subtract).then_inc(self.h_low, 1)
                    if q < 3:
                        w2_low(q + 1)
                    if m == 2:
                        if b + 1 < B:
                            norm_rstd(pool, link, self.norm0 + b + 1)
                            fill(b)
                        else:
                            lead[0]() if lead else None
                    elif m == 1 and b:
                        add(b - 1)
                    elif m in (3, 5) and b == 1:
                        tail(m // 4)
                    elif m == 4 and b == B - 1:
                        lead[1]() if lead else None
                    if m == 6 and self.bias_row is not None:
                        link(pool.tensor_tensor(gate_bias[:, :], gates[:, self.l % 2, 1, b, :],
                                                bias_bc[:, self.bias_row, :], ALU.mult))
                        pool.wait_ge(ln_done, self.norm0 + b + 1)
                        for t in range(TT):
                            ins = pool.tensor_tensor(x[:, TT * b + t, :], x[:, TT * b + t, :], gate_bias[:, :], ALU.add)
                        link(ins)
                add(B - 1)

        class S5:
            def __init__(self, before, xready, norm0):
                self.before, self.xready, self.norm0 = before, xready, norm0
                self.t_full, self.t_out = sem("s_t_full"), sem("s_t_out")
                self.bu_full, self.bu_free = sem("s_bu_full"), sem("s_bu_free")
                self.scan, self.yprod = sem("s_scan"), sem("s_yprod")
                self.c_full, self.acc_free, self.xd = sem("s_c_full"), sem("s_acc_free"), sem("s_x_done")

            def pe(self, pe):
                for s_, n in self.before:
                    pe.wait_ge(s_, n)

                def inputs(b):
                    pe.wait_ge(self.t_out, 2 * b + 2)
                    if b:
                        pe.wait_ge(self.bu_free, b)
                    for a in range(2):
                        for k in range(DH):
                            ins = pe.matmul(bank(4 + a), BT[:, a, k, :], XS[b % 3][:, k, :],
                                            start=(k == 0), stop=(k == 1))
                    ins.then_inc(self.bu_full, 1)

                def outputs(b):
                    pe.wait_ge(self.yprod, b + 1)
                    if b:
                        pe.wait_ge(self.acc_free, b)
                    for t in range(TT):
                        c = slice(t * P, (t + 1) * P)
                        for k in range(DH):
                            pe.matmul(PS[:, t, k * P:(k + 1) * P], XS[b % 3][:, k, c], diagD[:, k, :],
                                      start=(k == 0), stop=False, skip_group_check=True)
                        for a in range(2):
                            ins = pe.matmul(bank(t, D), ysc[b % 2][a][:, c], CT[:, a, :],
                                            start=False, stop=(a == 1), skip_group_check=True)
                    ins.then_inc(self.c_full, 1)

                for b in range(B):
                    inputs(b)
                    if b:
                        outputs(b - 1)
                    if b + 2 < B:
                        self.pe_transposes(pe, b + 2)
                    elif b + 2 == B:
                        mlp1.pe_transposes(pe, 0)
                outputs(B - 1)

            def pe_transposes(self, pe, b):
                pe.wait_ge(ln_done, self.norm0 + b + 1)
                if b:
                    pe.wait_ge(self.t_out, 2 * b)
                for half in range(2):
                    turn(pe, bank(6 + half), half).then_inc(self.t_full, 1)

            def dve_norm(self, v, link, b):
                    s_, n = self.xready
                    norm_stats(v, link, self.norm0 + b, b, [(s_, n * (b + 1))])
                    norm_apply(v, self.norm0 + b, b, [(self.t_full, 2 * b)] if b else [(mlp0.t_full, 2 * B)])
                    self.dve_modulate(v, b)

            def dve_modulate(self, v, b):
                    if b >= 3:
                        v.wait_ge(self.c_full, b - 2)
                    for half in range(2):
                        v.wait_ge(self.t_full, 2 * b + half + 1)
                        v.tensor_scalar(XS[b % 3][:, half, :], bank(6 + half), mod[:, 2, 1, half, b:b + 1],
                                        mod[:, 2, 0, half, b:b + 1], ALU.mult, ALU.add).then_inc(self.t_out, 1)

            def dve(self, v, link):
                def result(b):
                    v.wait_ge(self.c_full, b + 1)
                    if b == 0:
                        v.wait_ge(ld_gate[1], 16)
                        v.wait_ge(mlp0.xd, B)
                    else:
                        v.wait_ge(self.xd, b)
                    v.tensor_tensor(tsc[:, :, :], PS[:, 0:TT, 0:D],
                                    gates[:, 1, 0, b:b + 1, :].to_broadcast([P, TT, D]),
                                    ALU.mult).then_inc(self.acc_free, 1)

                for b in range(B):
                    if b + 2 < B:
                        norm_stats(v, link, self.norm0 + b + 2, b + 2, [(mlp0.xd, b + 3)])
                    elif b + 2 == B:
                        norm_stats(v, link, mlp1.norm0, 0, [(self.xd, 1)])
                    v.wait_ge(self.bu_full, b + 1)
                    if b:
                        v.wait_ge(self.scan, b)
                    v.tensor_tensor(bu[0], bank(4), CC, ALU.mult)
                    v.tensor_tensor(bu[1], bank(5), SS, ALU.mult).then_inc(self.bu_free, 1)
                    v.wait_ge(self.bu_free, b + 1)
                    link(v.tensor_tensor(bu[0], bu[0], bu[1], ALU.add))
                    if b >= 2:
                        v.wait_ge(self.yprod, b - 1)
                    v.tensor_tensor_scan(yst[b % 2], RR, bu[0], 0.0, ALU.mult, ALU.add).then_inc(self.scan, 1)
                    if b + 2 < B:
                        norm_apply(v, self.norm0 + b + 2, b + 2, [(self.t_full, 2 * (b + 2))])
                    elif b + 2 == B:
                        norm_apply(v, mlp1.norm0, 0, [(self.t_full, 2 * B)])
                    if b:
                        result(b - 1)
                    if b + 2 < B:
                        self.dve_modulate(v, b + 2)
                    elif b + 2 == B:
                        mlp1.dve_modulate(v, 0)
                result(B - 1)

            def pool(self, pool, link):
                def add(b):
                    pool.wait_ge(self.acc_free, b + 1)
                    pool.tensor_tensor(batch(b), batch(b), tsc[:, :, :], ALU.add).then_inc(self.xd, 1)

                for b in range(B):
                    if b + 2 < B:
                        norm_rstd(pool, link, self.norm0 + b + 2)
                    elif b + 2 == B:
                        norm_rstd(pool, link, mlp1.norm0)
                    pool.wait_ge(self.scan, b + 1)
                    if b >= 2:
                        pool.wait_ge(self.c_full, b - 1)
                    pool.tensor_tensor(ysc[b % 2][0], yst[b % 2], CC, ALU.mult)
                    pool.tensor_tensor(ysc[b % 2][1], yst[b % 2], SS, ALU.mult).then_inc(self.yprod, 1)
                    if b:
                        add(b - 1)
                add(B - 1)

        def c_(i):
            return sv[:, i:i + 1]

        (DT, KN, RD, EA, TH, VV, SN, CM, TMP, RAD, CO, NR, NI, FR, FI, SFI, NSFR, DEN, ANG_C, ANG_S, T2, M2SG,
         TWO_N, PART) = range(24)

        def s5_decay(pool, link):
            pool.wait_ge(ld_s5, 16 * 8)
            re, im, ls, sg = (lam[:, i:i + 1] for i in range(4))

            def ts(o, a, s1, s2, op0, op1=ALU.bypass):
                link(pool.tensor_scalar(c_(o), a, s1, s2, op0, op1) if s2 is not None else
                     pool.tensor_scalar(c_(o), a, s1, None, op0))

            def stt(o, a, s_, b_, op0, op1):
                link(pool.tensor_scalar(c_(PART), a, s_, None, op0))
                link(pool.tensor_tensor(c_(o), c_(PART), b_, op1))

            ts(KN, ls, LOG2E, None, ALU.mult)
            ts(KN, c_(KN), ROUND, None, ALU.add)
            ts(KN, c_(KN), -ROUND, None, ALU.add)
            stt(RD, c_(KN), -LN2_HI, ls, ALU.mult, ALU.add)
            stt(RD, c_(KN), -LN2_LO, c_(RD), ALU.mult, ALU.add)
            ts(DT, c_(RD), 1.0 / 5040, 1.0 / 720, ALU.mult, ALU.add)
            for q in (1.0 / 120, 1.0 / 24, 1.0 / 6, 0.5, 1.0, 1.0):
                ts(DT, c_(DT), c_(RD), q, ALU.mult, ALU.add)
            link(pool.tensor_scalar(lam_i[:, :], c_(KN), 127.0, 8388608.0, ALU.add, ALU.mult))
            stt(DT, c_(DT), 1.0, lam_i[:, :].bitcast(F32), ALU.mult, ALU.mult)
            ts(TMP, re, c_(DT), 1.0 / 64, ALU.mult, ALU.mult)
            ts(EA, c_(TMP), 1.0 / 40320, 1.0 / 5040, ALU.mult, ALU.add)
            for q in (1.0 / 720, 1.0 / 120, 1.0 / 24, 1.0 / 6, 0.5, 1.0):
                ts(EA, c_(EA), c_(TMP), q, ALU.mult, ALU.add)
            ts(EA, c_(EA), c_(TMP), None, ALU.mult)
            for _ in range(6):
                stt(EA, c_(EA), 2.0, c_(EA), ALU.add, ALU.mult)
            ts(RAD, c_(EA), 1.0, None, ALU.add)

        def s5_angles(pool, link):
            re, im, ls, sg = (lam[:, i:i + 1] for i in range(4))

            def ts(o, a, s1, s2, op0, op1=ALU.bypass):
                link(pool.tensor_scalar(c_(o), a, s1, s2, op0, op1) if s2 is not None else
                     pool.tensor_scalar(c_(o), a, s1, None, op0))

            def stt(o, a, s_, b_, op0, op1):
                link(pool.tensor_scalar(c_(PART), a, s_, None, op0))
                link(pool.tensor_tensor(c_(o), c_(PART), b_, op1))

            ts(TH, im, c_(DT), None, ALU.mult)
            ts(KN, c_(TH), 0.15915494309189535, None, ALU.mult)
            ts(KN, c_(KN), ROUND, None, ALU.add)
            ts(KN, c_(KN), -ROUND, None, ALU.add)
            for q in (TWO_PI_A, TWO_PI_B, TWO_PI_C):
                stt(TH, c_(KN), -q, c_(TH), ALU.mult, ALU.add)
            ts(TH, c_(TH), 0.125, None, ALU.mult)
            ts(VV, c_(TH), c_(TH), None, ALU.mult)
            ts(SN, c_(VV), 1.0 / 362880, -1.0 / 5040, ALU.mult, ALU.add)
            for q in (1.0 / 120, -1.0 / 6, 1.0):
                ts(SN, c_(SN), c_(VV), q, ALU.mult, ALU.add)
            ts(SN, c_(SN), c_(TH), None, ALU.mult)
            ts(CM, c_(VV), 1.0 / 40320, -1.0 / 720, ALU.mult, ALU.add)
            for q in (1.0 / 24, -0.5):
                ts(CM, c_(CM), c_(VV), q, ALU.mult, ALU.add)
            ts(CM, c_(CM), c_(VV), None, ALU.mult)
            for _ in range(3):
                ts(TMP, c_(CM), 1.0, 2.0, ALU.add, ALU.mult)
                ts(T2, c_(SN), c_(TMP), None, ALU.mult)
                ts(CM, c_(SN), c_(SN), -2.0, ALU.mult, ALU.mult)
                ts(SN, c_(T2), 1.0, None, ALU.mult)
            ts(CO, c_(CM), 1.0, None, ALU.add)
            stt(NR, c_(EA), c_(CO), c_(CM), ALU.mult, ALU.add)
            pool.tensor_scalar(c_(NI), c_(RAD), c_(SN), None, ALU.mult).then_inc(s5_num, 1)

        def s5_factors(v, link):
            re, im, ls, sg = (lam[:, i:i + 1] for i in range(4))

            def ts(o, a, s1, s2, op0, op1=ALU.bypass):
                link(v.tensor_scalar(c_(o), a, s1, s2, op0, op1) if s2 is not None else
                     v.tensor_scalar(c_(o), a, s1, None, op0))

            def stt(o, a, s_, b_, op0, op1):
                link(v.scalar_tensor_tensor(out=c_(o), in0=a, scalar=s_, in1=b_, op0=op0, op1=op1))

            v.wait_ge(s5_num, 1)
            ts(DEN, re, re, None, ALU.mult)
            stt(DEN, im, im, c_(DEN), ALU.mult, ALU.add)
            link(v.reciprocal(c_(DEN), c_(DEN)))
            ts(FR, c_(NI), im, None, ALU.mult)
            stt(FR, c_(NR), re, c_(FR), ALU.mult, ALU.add)
            ts(FR, c_(FR), c_(DEN), None, ALU.mult)
            ts(FI, c_(NR), im, None, ALU.mult)
            stt(FI, c_(NI), re, c_(FI), ALU.mult, ALU.subtract)
            ts(FI, c_(FI), c_(DEN), None, ALU.mult)
            ts(SFI, c_(FI), sg, None, ALU.mult)
            ts(NSFR, c_(FR), sg, -1.0, ALU.mult, ALU.mult)
            ts(M2SG, sg, -2.0, None, ALU.mult)

        def s5_tables(v, link):
            v.wait_ge(ld_bc, 16 * 12)
            v.memset(ROT[:, 0, 0:1], 0.0)
            v.memset(ROT[:, 1, 0:1], 1.0)
            v.memset(ROT[:, 2, 0:1], 0.0)
            v.memset(RR, 1.0)
            v.tensor_copy(ROT[:, 1, 1:2], c_(CO))
            v.tensor_copy(ROT[:, 2, 1:2], c_(SN))
            link(v.tensor_scalar(ROT[:, 0, 1:2], c_(SN), -1.0, None, ALU.mult))
            v.tensor_scalar(RR, RR, c_(RAD), None, ALU.mult)
            m = 1
            while m < T - 1:
                n = min(m, T - 1 - m)
                link(v.tensor_scalar(s5t[:, :, 0:n], ROT[:, 1:3, 1:n + 1], ROT[:, 1, m:m + 1], None, ALU.mult))
                link(v.scalar_tensor_tensor(out=ROT[:, 1:3, m + 1:m + n + 1], in0=ROT[:, 0:2, 1:n + 1],
                                            scalar=ROT[:, 2, m:m + 1], in1=s5t[:, :, 0:n], op0=ALU.mult, op1=ALU.add))
                link(v.tensor_scalar(ROT[:, 0, m + 1:m + n + 1], ROT[:, 2, m + 1:m + n + 1], -1.0, None, ALU.mult))
                m += n
            for a, (p_, q_) in enumerate(((FR, SFI), (FI, NSFR))):
                link(v.tensor_scalar(s5t[:, a, 0:D], s5B[:, 1, :], c_(q_), None, ALU.mult))
                v.scalar_tensor_tensor(out=s5W[:, a, :], in0=s5B[:, 0, :], scalar=c_(p_), in1=s5t[:, a, 0:D],
                                       op0=ALU.mult, op1=ALU.add)
            for k in range(DH):
                ins = v.tensor_scalar(diagD[:, k, :], ident[:, :], column("Dd", k), None, ALU.mult)
            ins.then_inc(s5_pre, 1)

        def setup_pe(pe):
            pe.wait_ge(ld_cond, 16)
            pe.wait_ge(ld_const, 16)
            pe.transpose(PS[:, 5, 0:8], rows[0:8, :], ident[0:8, 0:8]).then_inc(row_tr, 1)
            mod_rows(pe, 0, Wm0, cs, 3, [(silu_ready, 1), (ld_wm0, 16)])
            mod_turn(pe, 0, 3)
            pe.wait_ge(ld_rows, 16 * 12)
            pe.transpose(PS[:, 4, 0:NROWS], rows[:, :], ident[0:NROWS, 0:NROWS]).then_inc(row_tr, 1)
            pe.wait_ge(mod_ready, 1)

        def setup_act(act):
            act.wait_ge(cols_ready, 1)
            nc.scalar.activation(csig[:, :], col[:, 0:8], ACT.Exp, scale=-1.0).then_inc(silu_e, 1)

        def setup_dve(v, link):
            v.memset(cs[:, :, :], 0.0)
            v.memset(cc[:, :, :], 0.0)
            v.memset(lnc[:, :, :], 0.0)
            v.memset(h3[:, :, :], 0.0)
            link(v.memset(czero[:, :], 0.0))
            v.memset(mhalf[:, :], -0.5).then_inc(consts_set, 1)
            v.wait_ge(row_tr, 1)
            v.tensor_copy(col[:, 0:8], PS[:, 5, 0:8]).then_inc(cols_ready, 1)
            v.wait_ge(silu_e, 1)
            link(v.tensor_scalar(csig[:, :], csig[:, :], 1.0, None, ALU.add))
            link(v.reciprocal(csig[:, :], csig[:, :]))
            cond = col[:, 0:8].rearrange("p (b k) -> p k b", k=2)
            v.tensor_tensor(cs[:, :, 0:B], cond, csig[:, :].rearrange("p (b k) -> p k b", k=2), ALU.mult)
            v.tensor_copy(cc[:, :, 0:B], cond).then_inc(silu_ready, 1)

        def setup_columns(v, link):
            v.wait_ge(row_tr, 2)
            v.tensor_copy(col[:, 8:NROWS], PS[:, 4, 8:NROWS]).then_inc(cols_ready, 1)
            v.wait_ge(cols_ready, 2)
            v.tensor_scalar(bq16[:, :], col[:, ROWS["L0_bq"][0]:ROWS["L0_bq"][0] + 2], 1.0 / HD, None,
                            ALU.mult).then_inc(cols_ready, 1)

        def mod_simple(v, link, i, m, s_shift, s_scale, g=None, b_=None):
            for half in range(2):
                sh, sc = mod[:, m, 0, half, :], mod[:, m, 1, half, :]
                link(v.tensor_scalar(sc, section(i, s_scale, half), 1.0, None, ALU.add))
                if g is None:
                    link(v.tensor_copy(sh, section(i, s_shift, half)))
                else:
                    link(v.scalar_tensor_tensor(out=sh, in0=sc, scalar=column(b_, half),
                                                in1=section(i, s_shift, half), op0=ALU.mult, op1=ALU.add))
                    link(v.tensor_scalar(sc, sc, column(g, half), None, ALU.mult))

        SETS = ((1, Wm1, cc, 3), (2, Wc1, cc, 1), (3, Wm2, cs, 3))

        def tail_pe(pe, att, mlp, slot):
            pe.wait_ge(mlp.t_out, 4)
            for t in att.tail():
                if t[0] == "PJ" and t[2] == slot:
                    att.pe_task(pe)(*t)

        def fill0_pe(pe, slot, b):
            i, W, C, nchunk = SETS[b]
            if slot < 2 and b == 0:
                tail_pe(pe, att0, mlp0, slot)
            if slot == 0:
                pe.wait_ge(mlp0.t_out, 2 * b + 4)
                mod_rows(pe, i, W, C, nchunk, [(ld_mid, 16 * 4)])
            elif slot == 2:
                if b == 0:
                    pe.wait_ge(att0.m_free, PJ0)
                mod_turn(pe, i, nchunk)

        def fill0_dve(v, link, b):
            i, W, C, nchunk = SETS[b]
            mod_evac(v, i, nchunk, [(gate_saved, 32 * (1, 2, 2)[b])])
            v.wait_ge(mod_ready, i + 1)
            if i == 1:
                mod_simple(v, link, 1, 2, SHIFT, SCALE)
                for half in range(2):
                    link(v.tensor_scalar(modf[:, 0, half, :], section(1, SCALE2, half), 1.0, None, ALU.add))
                    link(v.tensor_copy(modf[:, 1, half, :], section(1, SHIFT2, half)))
            elif i == 2:
                for half in range(2):
                    sh, sc, sf = mod[:, 3, 0, half, :], mod[:, 3, 1, half, :], modf[:, 0, half, :]
                    link(v.tensor_scalar(sc, section(2, 0, half), 1.0, None, ALU.add))
                    link(v.tensor_tensor(sc, sc, sf, ALU.mult))
                    link(v.tensor_tensor(sh, section(2, 1, half), sf, ALU.mult))
                    link(v.tensor_tensor(sh, sh, modf[:, 1, half, :], ALU.add))
            else:
                mod_simple(v, link, 3, 4, SHIFT, SCALE, "n1g", "n1b")
                mod_simple(v, link, 3, 5, SHIFT2, SCALE2, "n2g", "n2b")

        def s5_matrices_pe(pe):
            pe.wait_ge(s5_pre, 1)
            pe.wait_ge(mlp0.h_free, FM * B)
            for a in range(2):
                for k in range(DH):
                    pe.transpose(PS[:, 4, (2 * a + k) * P:(2 * a + k + 1) * P], s5W[:, a, k * P:(k + 1) * P], ident[:, :])
                    ins = pe.transpose(PS[:, 5, (2 * a + k) * P:(2 * a + k + 1) * P], s5C[:, a, k, :], ident[:, :])
            ins.then_inc(s5_tr, 1)

        def s5_matrices_dve(v):
            v.wait_ge(s5_tr, 1)
            v.tensor_copy(BT, bank(4).rearrange("p (a k n) -> p a k n", a=2, k=2))
            v.tensor_scalar(CT[:, 0, :], PS[:, 5, 0:D], c_(M2SG), None, ALU.mult)
            v.tensor_scalar(CT[:, 1, :], PS[:, 5, D:2 * D], -2.0, None, ALU.mult).then_inc(s5_ready, 1)

        def adapter_rows(pe, r):
            pe.wait_ge(l3_hg, 2)
            pe.wait_ge(ld_ring[r], 16 * 4)
            if r:
                pe.wait_ge(l3_wr, 1)
            for c in range(2):
                for k in range(DH):
                    for j in range(4):
                        ins = pe.matmul(PS[32 * j:32 * j + 32, 6 + c, :], h3[:, k, :],
                                        ring[j][:, k, 512 * c:512 * (c + 1)], start=(k == 0), stop=(k == 1))
            ins.then_inc(l3_w, 1)

        def fill1_pe(pe, slot, b):
            pe.wait_ge(mlp1.t_out, 2 * b + 4)
            if (slot, b) == (0, 0):
                pe.wait_ge(l3_ready, 1)
                for k in range(DH):
                    ins = pe.transpose(PS[:, 6, k * 32:k * 32 + B], c4[:, k * P:(k + 1) * P], ident[0:B, 0:B])
                ins.then_inc(l3_tr, 1)
            elif (slot, b) == (2, 0):
                pe.wait_ge(l3_ready, 2)
                for m in range(2):
                    for k in range(DH):
                        ins = pe.matmul(PS[:, 7, m * 32:m * 32 + B], WL3[:, k, m * P:(m + 1) * P], lnc[:, k, 0:B],
                                        start=(k == 0), stop=(k == 1))
                ins.then_inc(l3_h, 1)
            elif (slot, b) == (2, 1):
                adapter_rows(pe, 0)
            elif (slot, b) == (0, 2):
                adapter_rows(pe, 1)

        def fill1_act(act, b):
            if b == 1:
                for m in range(2):
                    act.wait_ge(l3_h, 1)
                    nc.scalar.activation(h3[:, m, 0:B], PS[:, 7, m * 32:m * 32 + B], ACT.Gelu,
                                         bias=column("L3_b1", m)).then_inc(l3_hg, 1)

        def cond_norm(v, link):
            link(v.bn_stats(c4s[:, 0:6], c4[:, :]))
            link(v.bn_aggr(c4s[:, 6:8], c4s[:, 0:6]))
            v.tensor_scalar(c4s[:, 0:1], c4s[:, 7:8], EPS, None, ALU.add).then_inc(l3_bt, 1)
            v.wait_ge(l3_bt, 2)
            v.tensor_scalar(c4[:, :], c4[:, :], c4s[:, 6:7], c4s[:, 1:2], ALU.subtract, ALU.mult).then_inc(l3_ready, 1)

        def fill1_dve(v, link, b):
            if b == 0:
                v.wait_ge(l3_tr, 1)
                for k in range(DH):
                    ins = v.tensor_scalar(lnc[:, k, 0:B], PS[:, 6, k * 32:k * 32 + B], column("lng", k),
                                          column("lnb", k), ALU.mult, ALU.add)
                ins.then_inc(l3_ready, 1)
            else:
                r = b - 1
                v.wait_ge(l3_w, r + 1)
                v.wait_ge(ld_b2[r], 16 * 4)
                v.tensor_tensor(wrow[r], PS[:, 6:8, :].rearrange("p a b -> p (a b)"), b2row[r],
                                ALU.add).then_inc(l3_wr, 1)

        def cond_norm_pool(pool, link):
            pool.wait_ge(l3_bt, 1)
            link(pool.tensor_tensor(c4s[:, 1:2], c4s[:, 0:1], mhalf[0:B, 0:1], ALU.pow))
            link(pool.tensor_tensor(c4s[:, 2:3], c4s[:, 1:2], c4s[:, 1:2], ALU.mult))
            link(pool.tensor_tensor(c4s[:, 2:3], c4s[:, 2:3], c4s[:, 0:1], ALU.mult))
            link(pool.tensor_scalar(c4s[:, 2:3], c4s[:, 2:3], -0.5, 1.5, ALU.mult, ALU.add))
            pool.tensor_tensor(c4s[:, 1:2], c4s[:, 1:2], c4s[:, 2:3], ALU.mult).then_inc(l3_bt, 1)

        def nothing(*_):
            pass

        f_bt, f_btr, f_t, f_to = sem("f_bt"), sem("f_btr"), sem("f_t"), sem("f_to")
        f_z, f_zo, f_y, f_yo, f_z2, f_z2o, f_o, f_oo = (sem("f_" + n) for n in (
            "z", "zo", "y", "yo", "z2", "z2o", "o", "oo"))

        class Low:

            def __init__(self, before, xready):
                self.before, self.xready = before, xready

            def pe(self, pe):
                for s_, n in self.before:
                    pe.wait_ge(s_, n)
                pe.wait_ge(ld_low, 64)
                for w in range(2):
                    for b in range(B):
                        for h in range(DH):
                            q = (w * B + b) * DH + h
                            ins = pe.transpose(PS[0:RANK, q // 4, (q % 4) * P:(q % 4 + 1) * P],
                                               raw_a1[:, 1 + 2 * w, b, h, :], ident[:, :])
                ins.then_inc(f_bt, 1)
                for b in range(B):
                    pe.wait_ge(self.xready[0], self.xready[1] * (b + 1))
                    if b:
                        pe.wait_ge(f_to, 2 * b)
                    for half in range(2):
                        turn(pe, bank(6 + half), half,
                             lambda t: x[:, TT * b + t, half * P:(half + 1) * P]).then_inc(f_t, 1)
                for b in range(B):
                    pe.wait_ge(f_to, 2 * b + 2)
                    if b >= 2:
                        pe.wait_ge(f_zo, b - 1)
                    for k in range(DH):
                        ins = pe.matmul(PS[0:RANK, 4 + b % 2, :], raw_a1[:, 0, b, k, :], xT[b][:, k, :],
                                        start=(k == 0), stop=(k == 1))
                    ins.then_inc(f_z, 1)
                pe.wait_ge(f_btr, 4)
                for b in range(B):
                    pe.wait_ge(f_zo, b + 1)
                    for h in range(DH):
                        q = 2 * b + h
                        if q >= 4:
                            pe.wait_ge(f_yo, q - 3)
                        pe.matmul(bank(q % 4), btr[0:RANK, 0, b, h * P:(h + 1) * P], z1[b][0:RANK, :],
                                  start=True, stop=True).then_inc(f_y, 1)
                for b in range(B):
                    pe.wait_ge(f_yo, 2 * b + 2)
                    if b < 2:
                        pe.wait_ge(f_zo, 3 + b)
                    else:
                        pe.wait_ge(f_z2o, b - 1)
                    for k in range(DH):
                        ins = pe.matmul(PS[0:RANK, 4 + b % 2, :], raw_a1[:, 2, b, k, :], gT[b][:, k, :],
                                        start=(k == 0), stop=(k == 1))
                    ins.then_inc(f_z2, 1)
                for b in range(B):
                    pe.wait_ge(f_z2o, b + 1)
                    pe.wait_ge(f_yo, 2 * B)
                    if b:
                        pe.wait_ge(f_oo, b)
                    for t in range(TT):
                        ins = pe.matmul(bank(t, D), z2[b][0:RANK, t * P:(t + 1) * P], btr[0:RANK, 1, b, :],
                                        start=True, stop=True)
                    ins.then_inc(f_o, 1)

            def act(self, act):
                for b in range(B):
                    for h in range(DH):
                        q = 2 * b + h
                        act.wait_ge(f_y, q + 1)
                        nc.scalar.activation(gT[b][:, h, :], bank(q % 4), ACT.Gelu).then_inc(f_yo, 1)

            def dve(self, v, link):
                v.wait_ge(f_bt, 1)
                for w in range(2):
                    for c in range(2):
                        v.tensor_copy(btr[0:RANK, w, 2 * c:2 * c + 2, :], PS[0:RANK, 2 * w + c, :].rearrange(
                            "p (b d) -> p b d", b=2)).then_inc(f_btr, 1)
                for b in range(B):
                    for half in range(2):
                        v.wait_ge(f_t, 2 * b + half + 1)
                        v.tensor_copy(xT[b][:, half, :], bank(6 + half)).then_inc(f_to, 1)
                for b in range(B):
                    v.wait_ge(f_z, b + 1)
                    v.tensor_copy(z1[b][0:RANK, :], PS[0:RANK, 4 + b % 2, :]).then_inc(f_zo, 1)
                for b in range(B):
                    v.wait_ge(f_z2, b + 1)
                    v.tensor_copy(z2[b][0:RANK, :], PS[0:RANK, 4 + b % 2, :]).then_inc(f_z2o, 1)
                for b in range(B):
                    v.wait_ge(f_o, b + 1)
                    v.tensor_tensor(batch(b), batch(b), PS[:, 0:TT, 0:D], ALU.add).then_inc(f_oo, 1)

            def sync(self, sp):
                for b in range(B):
                    sp.wait_ge(f_oo, b + 1)
                    sp.dma_start(out[b].rearrange("(t p) d -> p t d", p=P), batch(b)).then_inc(out_done, 16)
                sp.wait_ge(out_done, 16 * B)

        PJ0, PJ1 = (len([k for k in misc if k[0] == a]) for a in range(2))
        att0 = Attention(0, [])
        mlp0 = SplitMLP(0, [(att0.st_read, NSTEP)], (att0.xd, 2), 4, "L0_b1", ACT.Gelu, 2, att0, lambda b: [
            [(att0.sm_free, 8 * NG)], [(att0.o_free, NG), (att0.m_free, att0.idx("PJ", B - 1, 0))],
            [(att0.m_free, PJ0), (mod_ready, 2)], [(mod_ready, 3)]][b])
        s5 = S5([(s5_ready, 1), (mlp0.acc_free, B)], (mlp0.xd, 1), 8)
        mlp1 = MLP(1, [(s5.acc_free, B), (s5.bu_free, B)], (s5.xd, 1), 12, "L1_b1", ACT.Gelu_apprx_tanh, 3, s5,
                   lambda b: [[(s5.t_out, 2 * B)], [], [(l3_ready, 2), (l3_hg, 2)], [(l3_wr, 1)]][b])
        att1 = Attention(1, [(mlp1.acc_free, B), (mlp1.h_free, FM * B)])
        mlp2 = SplitMLP(2, [(att1.st_read, NSTEP)], (att1.xd, 2), 20, None, ACT.Gelu, None, att1, lambda b: [
            [(att1.sm_free, 8 * NG)], [(att1.o_free, NG), (att1.m_free, att1.idx("PJ", B - 1, 0))],
            [(att1.m_free, PJ1)], []][b])
        low = Low([(mlp2.t_out, 2 * B), (mlp2.acc_free, B), (mlp2.h_free, FM * B)], (mlp2.xd, 1))
        att0.mlp, att1.mlp = mlp0, mlp2

        def calls(task, tasks):
            return [lambda t=t: task(*t) for t in tasks]

        block = ctx.enter_context(nc.Block())

        @block.tensor
        def _(pe):
            setup_pe(pe)
            for t in att0.lead():
                att0.pe_task(pe)(*t)
            att0.pe(pe)

            def s5_first():
                pe.wait_ge(mod_ready, 4)
                s5.pe_transposes(pe, 0)

            def s5_second():
                s5.pe_transposes(pe, 1)

            mlp0.pe(pe, lambda slot, b: fill0_pe(pe, slot, b), [nothing, nothing, nothing, s5_first, nothing,
                                                                  s5_second, lambda: s5_matrices_pe(pe), nothing])
            s5.pe(pe)

            def att1_first():
                pe.wait_ge(l3_wr, 2)
                pe.wait_ge(mlp1.t_out, 2 * B)

            mlp1.pe(pe, lambda slot, b: fill1_pe(pe, slot, b),
                    [att1_first] + calls(att1.pe_task(pe), att1.lead()))
            att1.pe(pe)
            mlp2.pe(pe, lambda slot, b: tail_pe(pe, att1, mlp2, slot) if slot < 2 and b == 0 else None, [])
            low.pe(pe)

        @block.scalar
        def _(act):
            act.dma_start(ident[:, :], A["const_ident"]).then_inc(ld_const, 16)
            act.dma_start(batch(0), A["x"][0].rearrange("(t p) d -> p t d", p=P)).then_inc(ld_x[0], 16)
            setup_act(act)
            for k, name in enumerate(("L0_cond_Wq", "L0_cond_Wk", "L0_cond_Wv", "L0_cond_Wo")):
                act.dma_start(WA[:, k], view(A[name])).then_inc(ld_wa, 16)
            for k, name in enumerate(("L0_cond_bv", "L0_cond_bo", "L0_cond_b2", "L1_cond_b2")):
                act.dma_start(bias_bc[:, k, :], A[name].partition_broadcast(P)).then_inc(ld_bias, 16)
            act.wait_ge(mods_set, 1)
            for t in att0.lead():
                if t == ("Q", 0, 0):
                    act.wait_ge(cols_ready, 3)
                att0.act_task(act)(*t)
            att0.act(act)
            mlp0.act(act, nothing, [])
            mlp1.act(act, lambda b: fill1_act(act, b),
                     [nothing] + calls(att1.act_task(act), att1.lead()))
            att1.act(act)
            mlp2.act(act, nothing, [])
            low.act(act)

        @block.vector
        def _(v):
            link = Chain(v, dve_c)
            setup_dve(v, link)
            lead = att0.lead()
            for t in lead[:4]:
                att0.dve_task(v, link)(*t)
            mod_evac(v, 0, 3, [])
            v.wait_ge(mod_ready, 1)
            mod_simple(v, link, 0, 0, SHIFT, SCALE)
            mod_simple(v, link, 0, 1, SHIFT2, SCALE2)
            v.tensor_copy(czero2[:, :], czero[:, :]).then_inc(mods_set, 1)
            setup_columns(v, link)
            for t in lead[4:]:
                att0.dve_task(v, link)(*t)
            att0.dve(v, link)

            def s5_side(b):
                if b < 2:
                    (s5_factors, s5_tables)[b](v, link)

            mlp0.dve(v, link, s5_side, lambda b: fill0_dve(v, link, b),
                     [lambda: s5.dve_norm(v, link, 0), lambda: s5.dve_norm(v, link, 1),
                      lambda: s5_matrices_dve(v)])
            s5.dve(v, link)

            def att1_ones():
                v.wait_ge(low_saved, 128)
                att1.set_ones(v, link)

            mlp1.dve(v, link, lambda b: cond_norm(v, link) if b == 0 else None,
                     lambda b: fill1_dve(v, link, b), calls(att1.dve_task(v, link), att1.lead()[:4]) +
                     [att1_ones] + calls(att1.dve_task(v, link), att1.lead()[4:]))
            att1.dve(v, link)
            mlp2.dve(v, link, nothing, nothing, [])
            low.dve(v, link)

        @block.gpsimd
        def _(pool):
            link = Chain(pool, pool_c)
            att0.set_ones(pool, link)
            pool.wait_ge(att0.init, 1)
            pool.wait_ge(consts_set, 1)
            for t in att0.lead():
                att0.pool_task(pool, link)(*t)
            att0.pool(pool, link)
            mlp0.pool(pool, link, nothing, [lambda: norm_rstd(pool, link, s5.norm0),
                                              lambda: norm_rstd(pool, link, s5.norm0 + 1)])
            s5.pool(pool, link)
            mlp1.pool(pool, link, lambda b: cond_norm_pool(pool, link) if b == 0 else None,
                      calls(att1.pool_task(pool, link), att1.lead()))
            att1.pool(pool, link)
            mlp2.pool(pool, link, nothing, [])

        @block.sync
        def _(sp):
            sp.dma_start(rows[0:8, :], A["cond_1024"].rearrange("b (k p) -> (b k) p", p=P)).then_inc(ld_cond, 16)
            sp.dma_start(Wm0, view(A["L0_cond_Wc"])).then_inc(ld_wm0, 16)
            load_mbias(sp, A["L0_cond_bc"], 3)
            for name, src in (("L0_bq", "L0_cond_bq"), ("L0_bk", "L0_cond_bk"),
                              ("L0_b1", "L0_cond_b1"), ("L1_b1", "L1_cond_b1"), ("n1g", "L2_cond_norm1_g"),
                              ("n1b", "L2_cond_norm1_b"), ("n2g", "L2_cond_norm2_g"), ("n2b", "L2_cond_norm2_b"),
                              ("lng", "L3_cond_ln_g"), ("lnb", "L3_cond_ln_b"), ("L3_b1", "L3_cond_b1"),
                              ("Dd", "L1_cond_D_diag")):
                r0, n = ROWS[name]
                sp.dma_start(rows[r0:r0 + n, :], A[src].rearrange("(r c) -> r c", c=P)).then_inc(ld_rows, 16)
            for b in range(1, B):
                sp.dma_start(batch(b), A["x"][b].rearrange("(t p) d -> p t d", p=P)).then_inc(ld_x[b], 16)
            save_gates(sp, 0)
            load_gates(sp, 0)
            lead = [t for t in att0.tasks(-100, 1000)]
            for t in lead[:len(att0.lead())]:
                att0.sync_task(sp)(*t)
            sp.dma_start(W1[:, :, :], view(A["L0_cond_W1"])).then_inc(ld_mlp[0], 16)
            sp.dma_start(W2[:, :, :], view(A["L0_cond_W2"])).then_inc(ld_mlp[0], 16)
            sp.dma_start(rot[:, :], A["const_rot"]).then_inc(ld_rope, 16)
            for k in range(2):
                sp.dma_start(rope[:, k, :], A["const_rope"][k]).then_inc(ld_rope, 16)
            sp.dma_start(c4[:, :], A["cond_1024"]).then_inc(ld_s5, 16)
            for k, name in enumerate(("Lam_re", "Lam_im", "log_step")):
                for h in range(2):
                    sp.dma_start(lam[SSM * h:SSM * (h + 1), k:k + 1],
                                 A["L1_cond_" + name].rearrange("(n o) -> n o", o=1)).then_inc(ld_s5, 16)
            sp.dma_start(lam[:, 3:4], A["const_sign"]).then_inc(ld_s5, 16)
            for t in lead[len(att0.lead()):]:
                att0.sync_task(sp)(*t)
            load_mbias(sp, A["L1_cond_bm"], 3)
            sp.wait_ge(att0.pv_done, 4 * NG)
            sp.dma_start(Wm1, view(A["L1_cond_Wm"])).then_inc(ld_mid, 16)
            sp.dma_start(Wc1, view(A["L1_cond_Wc"])).then_inc(ld_mid, 16)
            sp.dma_start(Wm2, view(A["L2_cond_ada_W"])).then_inc(ld_mid, 16)
            sp.dma_start(WL3, view(A["L3_cond_W1"])).then_inc(ld_mid, 16)
            sp.wait_ge(att0.m_free, PJ0)
            for h in range(2):
                for a in range(2):
                    sp.dma_start(s5B[SSM * h:SSM * (h + 1), a, :],
                                 A["L1_cond_B_im" if h != a else "L1_cond_B_re"]).then_inc(ld_bc, 16)
                    for k in range(DH):
                        sp.dma_start(s5C[:, a, k, SSM * h:SSM * (h + 1)],
                                     A["L1_cond_C_im" if h != a else "L1_cond_C_re"][k * P:(k + 1) * P, :]).then_inc(
                                         ld_bc, 16)
            for k, name in enumerate(("L2_cond_Wq", "L2_cond_Wk", "L2_cond_Wv", "L2_cond_Wo")):
                sp.dma_start(WA[:, k], view(A[name])).then_inc(ld_wa, 16)
            save_gates(sp, 1)
            load_mbias(sp, A["L1_cond_bc"], 1)
            load_gates(sp, 1)
            sp.wait_ge(mod_row, 3)
            load_mbias(sp, A["L2_cond_ada_b"], 3)
            save_gates(sp, 3)
            sp.wait_ge(mlp0.w2, FM * B)
            sp.dma_start(W1[:, :, :], view(A["L1_cond_W1"])).then_inc(ld_mlp[1], 16)
            sp.dma_start(W2[:, :, :], view(A["L1_cond_W2"])).then_inc(ld_mlp[1], 16)
            sp.wait_ge(mlp0.xd, B)
            load_gates(sp, 2)
            w3, b3 = view(A["L3_cond_W2"]), A["L3_cond_b2"]

            def load_ring(r):
                for j in range(4):
                    c = slice(2048 * j + 1024 * r, 2048 * j + 1024 * (r + 1))
                    sp.dma_start(ring[j], w3[:, :, c]).then_inc(ld_ring[r], 16)
                    sp.dma_start(b2row[r][32 * j:32 * j + 32, :], b3[c].partition_broadcast(32)).then_inc(ld_b2[r], 16)

            sp.wait_ge(mlp1.t_full, 2)
            sp.wait_ge(s5.c_full, B)
            load_ring(0)
            sp.wait_ge(l3_w, 1)
            load_ring(1)
            for r in range(2):
                sp.wait_ge(l3_wr, r + 1)
                for j in range(4):
                    sp.dma_start(d_low[j][:, 1024 * r:1024 * (r + 1)],
                                 wrow[r][32 * j:32 * j + B, :]).then_inc(low_saved, 16)
            sp.wait_ge(low_saved, 128)
            for j in range(4):
                sp.dma_start(raw_a1[:, j], d_low[j].rearrange("b (h d r) -> d b h r", h=DH, r=RANK)).then_inc(ld_low, 16)
            lead = [t for t in att1.tasks(-100, 1000)]
            for t in lead[:len(att1.lead())]:
                att1.sync_task(sp)(*t)
            sp.wait_ge(mlp1.w2, B)
            sp.dma_start(W1[:, :, :], view(A["L2_cond_W1"])).then_inc(ld_mlp[2], 16)
            sp.dma_start(W2[:, :, :], view(A["L2_cond_W2"])).then_inc(ld_mlp[2], 16)
            for t in lead[len(att1.lead()):]:
                att1.sync_task(sp)(*t)
            low.sync(sp)


def constants():
    import numpy as np
    rot = np.zeros((P, P), np.float32)
    for h in range(P // HD):
        for j in range(HD // 2):
            rot[h * HD + 2 * j + 1, h * HD + j] = -1.0
            rot[h * HD + 2 * j, h * HD + HD // 2 + j] = 1.0
    inv = np.float32(1.0) / np.float32(10000.0) ** (np.arange(0, HD, 2, dtype=np.float32) / np.float32(HD))
    f = np.outer(np.arange(T, dtype=np.float32), inv).astype(np.float32)
    e = np.concatenate([f, f], -1).T
    rope = np.stack([np.tile(np.cos(e), (P // HD, 1)), np.tile(np.sin(e), (P // HD, 1))]).astype(np.float32)
    sign = np.concatenate([-np.ones((SSM, 1)), np.ones((SSM, 1))]).astype(np.float32)
    return {"const_ident": np.eye(P, dtype=np.float32), "const_rot": rot, "const_rope": rope, "const_sign": sign}


def kernel(**inputs):
    import numpy as _np
    import concourse.bacc as _bacc
    from concourse import mybir as _mybir
    from concourse.bass_utils import run_bass_kernel_spmd as _run

    nc = _bacc.Bacc("TRN2", target_bir_lowering=False, num_devices=1)
    arrays, args = {}, {}
    for name, value in list(inputs.items()) + list(constants().items()):
        a = _np.ascontiguousarray(value)
        arrays[f"in_{name}_dram"] = a
        args[name] = nc.dram_tensor(f"in_{name}_dram", a.shape, _mybir.dt.from_np(a.dtype), kind="ExternalInput").ap()
    out = nc.dram_tensor("out_0_dram", (B, T, D), F32, kind="ExternalOutput").ap()
    build(nc, args, out)
    r = _run(nc, [arrays], core_ids=[0])
    return r.results[0]["out_0_dram"]
```
